# Optimizing a Trainium2 kernel written in Bass

```python
import numpy as np
import jax
import jax.numpy as jnp

def _softmax(x, axis=-1):
    return jax.nn.softmax(x, axis=axis)

def _gelu(x):
    return jax.nn.gelu(x, approximate=True)

def _silu(x):
    return jax.nn.silu(x)

def _sigmoid(x):
    return jax.nn.sigmoid(x)

def _layernorm(x, axis=-1, eps=1e-05):
    m = jnp.mean(x, axis=axis, keepdims=True)
    v = jnp.var(x, axis=axis, keepdims=True)
    return (x - m) / jnp.sqrt(v + eps)

def _scatter_add(tgt, idx, src, axis=0):
    return tgt.at[idx].add(src)

def _segment_sum(src, seg, n):
    return jax.ops.segment_sum(src, seg, n)
kernel_name = 'mk_cond_seq_d2_seqx_r8_a4cafb'

def setup_inputs(seed: int=0):
    np.random.seed(seed)
    _w = jnp.asarray

    def _rec_inputs():
        import jax
        import jax.numpy as jnp
        _rk = jax.random.key(seed)
        x = 7.22e-05 + 1 * jax.random.normal(jax.random.fold_in(_rk, 1), (16, 128, 128), jnp.float32)
        _lenS = 128 - jax.random.randint(jax.random.fold_in(_rk, 7), (16,), 0, max(1, 128 // 4) + 1, jnp.int32)
        _lenS2 = 128 - jax.random.randint(jax.random.fold_in(_rk, 8), (16,), 0, max(1, 128 // 4) + 1, jnp.int32)
        cond_1024 = 0.0061147 + 1.02565 * jax.random.normal(jax.random.fold_in(_rk, 11), (16, 128), jnp.float32)
        return (x, cond_1024)
    x, cond_1024 = _rec_inputs()

    def _L0_cond_setup():
        import jax, jax.numpy as jnp
        import numpy as np
        D_MODEL = 128
        NHEAD = 16
        HEAD_DIM = D_MODEL // NHEAD
        D_FF = 512
        EPS = 1e-05

        def _layernorm(x):
            mu = jnp.mean(x, axis=-1, keepdims=True)
            var = jnp.var(x, axis=-1, keepdims=True)
            return (x - mu) * jax.lax.rsqrt(var + EPS)
        key = jax.random.key(seed)
        ks = jax.random.split(key, 16)
        B, N = (4, 256)
        s = 0.02
        inp = {'x': jax.random.normal(ks[0], (B, N, D_MODEL), jnp.float32), 'c': jax.random.normal(ks[1], (B, D_MODEL), jnp.float32), 'W_ada': jax.random.normal(ks[2], (D_MODEL, 6 * D_MODEL), jnp.float32) * s, 'b_ada': jnp.zeros((6 * D_MODEL,), jnp.float32), 'Wq': jax.random.normal(ks[3], (D_MODEL, D_MODEL), jnp.float32) * s, 'bq': jnp.zeros((D_MODEL,), jnp.float32), 'Wk': jax.random.normal(ks[4], (D_MODEL, D_MODEL), jnp.float32) * s, 'bk': jnp.zeros((D_MODEL,), jnp.float32), 'Wv': jax.random.normal(ks[5], (D_MODEL, D_MODEL), jnp.float32) * s, 'bv': jnp.zeros((D_MODEL,), jnp.float32), 'Wo': jax.random.normal(ks[6], (D_MODEL, D_MODEL), jnp.float32) * s, 'bo': jnp.zeros((D_MODEL,), jnp.float32), 'W1': jax.random.normal(ks[7], (D_MODEL, D_FF), jnp.float32) * s, 'b1': jnp.zeros((D_FF,), jnp.float32), 'W2': jax.random.normal(ks[8], (D_FF, D_MODEL), jnp.float32) * s, 'b2': jnp.zeros((D_MODEL,), jnp.float32)}
        return inp
    _L0_cond_all = _L0_cond_setup()
    _L0_cond_in = {k: v for k, v in _L0_cond_all.items() if k in ('W_ada', 'b_ada', 'Wq', 'bq', 'Wk', 'bk', 'Wv', 'bv', 'Wo', 'bo', 'W1', 'b1', 'W2', 'b2')}
    del _L0_cond_all

    def _L1_cond_setup():
        import jax, jax.numpy as jnp
        import numpy as np
        B, N, D = (2, 256, 128)
        H, HD = (16, 64)
        E, DD = (8, 512)
        EPS = 1e-05

        def _ln(x, g, b):
            m = jnp.mean(x, axis=-1, keepdims=True)
            v = jnp.var(x, axis=-1, keepdims=True)
            return (x - m) * jax.lax.rsqrt(v + EPS) * g + b
        key = jax.random.key(seed)
        ks = jax.random.split(key, 16)
        s = 0.02
        return {'x': jax.random.normal(ks[0], (B, N, D), jnp.float32), 't': jax.random.normal(ks[1], (B, 1, D), jnp.float32), 'W_ada': jax.random.normal(ks[2], (D, D), jnp.float32) * s, 'b_ada': jnp.zeros((D,), jnp.float32), 'ln1_g': jnp.ones((D,), jnp.float32), 'ln1_b': jnp.zeros((D,), jnp.float32), 'Wqkv': jax.random.normal(ks[3], (3 * H * HD, D), jnp.float32) * s, 'qn_g': jnp.ones((HD,), jnp.float32), 'qn_b': jnp.zeros((HD,), jnp.float32), 'kn_g': jnp.ones((HD,), jnp.float32), 'kn_b': jnp.zeros((HD,), jnp.float32), 'Wout': jax.random.normal(ks[4], (D, H * HD), jnp.float32) * s, 'mlp_g': jnp.ones((D,), jnp.float32), 'mlp_b': jnp.zeros((D,), jnp.float32), 'Wgate': jax.random.normal(ks[5], (E, D), jnp.float32) * s, 'fc1s': jax.random.normal(ks[6], (E, DD, D), jnp.float32) * s, 'b1s': jnp.zeros((E, DD), jnp.float32), 'fc2s': jax.random.normal(ks[7], (E, D, DD), jnp.float32) * s, 'b2s': jnp.zeros((E, D), jnp.float32)}
    _L1_cond_all = _L1_cond_setup()
    _L1_cond_in = {k: v for k, v in _L1_cond_all.items() if k in ('W_ada', 'b_ada', 'ln1_g', 'ln1_b', 'Wqkv', 'qn_g', 'qn_b', 'kn_g', 'kn_b', 'Wout', 'mlp_g', 'mlp_b', 'Wgate', 'fc1s', 'b1s', 'fc2s', 'b2s')}
    del _L1_cond_all
    return {'x': x, 'cond_1024': cond_1024, 'L0_cond_W_ada': _L0_cond_in['W_ada'], 'L0_cond_b_ada': _L0_cond_in['b_ada'], 'L0_cond_Wq': _L0_cond_in['Wq'], 'L0_cond_bq': _L0_cond_in['bq'], 'L0_cond_Wk': _L0_cond_in['Wk'], 'L0_cond_bk': _L0_cond_in['bk'], 'L0_cond_Wv': _L0_cond_in['Wv'], 'L0_cond_bv': _L0_cond_in['bv'], 'L0_cond_Wo': _L0_cond_in['Wo'], 'L0_cond_bo': _L0_cond_in['bo'], 'L0_cond_W1': _L0_cond_in['W1'], 'L0_cond_b1': _L0_cond_in['b1'], 'L0_cond_W2': _L0_cond_in['W2'], 'L0_cond_b2': _L0_cond_in['b2'], 'L1_cond_W_ada': _L1_cond_in['W_ada'], 'L1_cond_b_ada': _L1_cond_in['b_ada'], 'L1_cond_ln1_g': _L1_cond_in['ln1_g'], 'L1_cond_ln1_b': _L1_cond_in['ln1_b'], 'L1_cond_Wqkv': _L1_cond_in['Wqkv'], 'L1_cond_qn_g': _L1_cond_in['qn_g'], 'L1_cond_qn_b': _L1_cond_in['qn_b'], 'L1_cond_kn_g': _L1_cond_in['kn_g'], 'L1_cond_kn_b': _L1_cond_in['kn_b'], 'L1_cond_Wout': _L1_cond_in['Wout'], 'L1_cond_mlp_g': _L1_cond_in['mlp_g'], 'L1_cond_mlp_b': _L1_cond_in['mlp_b'], 'L1_cond_Wgate': _L1_cond_in['Wgate'], 'L1_cond_fc1s': _L1_cond_in['fc1s'], 'L1_cond_b1s': _L1_cond_in['b1s'], 'L1_cond_fc2s': _L1_cond_in['fc2s'], 'L1_cond_b2s': _L1_cond_in['b2s']}

def reference(x, cond_1024, L0_cond_W_ada, L0_cond_b_ada, L0_cond_Wq, L0_cond_bq, L0_cond_Wk, L0_cond_bk, L0_cond_Wv, L0_cond_bv, L0_cond_Wo, L0_cond_bo, L0_cond_W1, L0_cond_b1, L0_cond_W2, L0_cond_b2, L1_cond_W_ada, L1_cond_b_ada, L1_cond_ln1_g, L1_cond_ln1_b, L1_cond_Wqkv, L1_cond_qn_g, L1_cond_qn_b, L1_cond_kn_g, L1_cond_kn_b, L1_cond_Wout, L1_cond_mlp_g, L1_cond_mlp_b, L1_cond_Wgate, L1_cond_fc1s, L1_cond_b1s, L1_cond_fc2s, L1_cond_b2s):
    import jax
    import jax.numpy as jnp

    def _L0_cond_ref(x, c, W_ada, b_ada, Wq, bq, Wk, bk, Wv, bv, Wo, bo, W1, b1, W2, b2):
        import jax, jax.numpy as jnp
        import numpy as np
        D_MODEL = 128
        NHEAD = 16
        HEAD_DIM = D_MODEL // NHEAD
        D_FF = 512
        EPS = 1e-05

        def _layernorm(x):
            mu = jnp.mean(x, axis=-1, keepdims=True)
            var = jnp.var(x, axis=-1, keepdims=True)
            return (x - mu) * jax.lax.rsqrt(var + EPS)
        B, N, _ = x.shape
        ada = (c @ W_ada + b_ada)[:, None, :]
        shift1, scale1, gate1, shift2, scale2, gate2 = jnp.split(ada, 6, axis=-1)
        h = _layernorm(x) * (1.0 + scale1) + shift1
        Q = (h @ Wq + bq).reshape(B, N, NHEAD, HEAD_DIM)
        K = (h @ Wk + bk).reshape(B, N, NHEAD, HEAD_DIM)
        V = (h @ Wv + bv).reshape(B, N, NHEAD, HEAD_DIM)
        scores = jnp.einsum('bqhd,bkhd->bhqk', Q, K) / np.sqrt(HEAD_DIM).astype(np.float32)
        attn = jax.nn.softmax(scores, axis=-1)
        attn_out = jnp.einsum('bhqk,bkhd->bqhd', attn, V).reshape(B, N, D_MODEL)
        attn_out = attn_out @ Wo + bo
        x = x + gate1 * attn_out
        h = _layernorm(x) * (1.0 + scale2) + shift2
        ff = jax.nn.gelu(h @ W1 + b1, approximate=False) @ W2 + b2
        return x + gate2 * ff

    def _L1_cond_ref(x, t, W_ada, b_ada, ln1_g, ln1_b, Wqkv, qn_g, qn_b, kn_g, kn_b, Wout, mlp_g, mlp_b, Wgate, fc1s, b1s, fc2s, b2s):
        import jax, jax.numpy as jnp
        import numpy as np
        B, N, D = (2, 256, 128)
        H, HD = (16, 64)
        E, DD = (8, 512)
        EPS = 1e-05

        def _ln(x, g, b):
            m = jnp.mean(x, axis=-1, keepdims=True)
            v = jnp.var(x, axis=-1, keepdims=True)
            return (x - m) * jax.lax.rsqrt(v + EPS) * g + b
        b, n, d = x.shape
        shift = jax.nn.silu(t) @ W_ada.T + b_ada
        h = _ln(x, ln1_g, ln1_b) + shift
        qkv = (h @ Wqkv.T).reshape(b, n, 3, H, HD)
        q = _ln(qkv[:, :, 0].transpose(0, 2, 1, 3), qn_g, qn_b)
        k = _ln(qkv[:, :, 1].transpose(0, 2, 1, 3), kn_g, kn_b)
        v = qkv[:, :, 2].transpose(0, 2, 1, 3)
        scores = jnp.einsum('bhnd,bhmd->bhnm', q, k) / jnp.sqrt(jnp.float32(HD))
        attn = jax.nn.softmax(scores, axis=-1)
        o = jnp.einsum('bhnm,bhmd->bhnd', attn, v)
        o = o.transpose(0, 2, 1, 3).reshape(b, n, H * HD)
        x = x + o @ Wout.T
        tok = x.reshape(-1, d)
        bs = tok.shape[0]
        gate = jax.nn.softmax(tok @ Wgate.T, axis=-1)
        k_cap = bs // E
        vals, idx = jax.lax.top_k(gate.T, k_cap)
        idx_flat = idx.T.reshape(-1)
        w = vals.T
        g = _ln(tok[idx_flat], mlp_g, mlp_b).reshape(k_cap, E, d)
        y = jnp.einsum('ked,ehd->keh', g, fc1s) + b1s
        y = jax.nn.gelu(y, approximate=True)
        y = jnp.einsum('keh,edh->ked', y, fc2s) + b2s
        y = y * w[..., None]
        tok = tok.at[idx_flat].add(y.reshape(-1, d))
        return tok.reshape(x.shape)
    x = _L0_cond_ref(x, cond_1024, L0_cond_W_ada, L0_cond_b_ada, L0_cond_Wq, L0_cond_bq, L0_cond_Wk, L0_cond_bk, L0_cond_Wv, L0_cond_bv, L0_cond_Wo, L0_cond_bo, L0_cond_W1, L0_cond_b1, L0_cond_W2, L0_cond_b2)
    x = _L1_cond_ref(x, cond_1024[:, None, :], L1_cond_W_ada, L1_cond_b_ada, L1_cond_ln1_g, L1_cond_ln1_b, L1_cond_Wqkv, L1_cond_qn_g, L1_cond_qn_b, L1_cond_kn_g, L1_cond_kn_b, L1_cond_Wout, L1_cond_mlp_g, L1_cond_mlp_b, L1_cond_Wgate, L1_cond_fc1s, L1_cond_b1s, L1_cond_fc2s, L1_cond_b2s)
    return x

_drawn_inputs = setup_inputs


def setup_inputs(seed=0):
    import zlib

    import numpy as np

    out = dict(_drawn_inputs(seed))
    spreads = {'L0_cond_b_ada': (0.0, 0.564),
     'L0_cond_bq': (0.0, 0.8),
     'L0_cond_bk': (0.0, 0.8),
     'L0_cond_bv': (0.0, 0.8),
     'L0_cond_bo': (0.0, 0.336),
     'L0_cond_b1': (0.0, 0.8),
     'L0_cond_b2': (0.0, 0.319),
     'L1_cond_b_ada': (0.0, 0.546),
     'L1_cond_ln1_g': (1.0, 0.6),
     'L1_cond_ln1_b': (0.0, 0.528),
     'L1_cond_qn_g': (1.0, 0.6),
     'L1_cond_qn_b': (0.0, 0.8),
     'L1_cond_kn_g': (1.0, 0.6),
     'L1_cond_kn_b': (0.0, 0.8),
     'L1_cond_mlp_g': (1.0, 0.6),
     'L1_cond_mlp_b': (0.0, 0.8),
     'L1_cond_b1s': (0.0, 0.8),
     'L1_cond_b2s': (0.0, 0.467)}
    factors = {'L0_cond_Wq': 8.0,
     'L0_cond_Wk': 8.0,
     'L0_cond_Wv': 8.0,
     'L0_cond_Wo': 8.0,
     'L0_cond_W1': 4.095,
     'L0_cond_W2': 3.686,
     'L1_cond_W_ada': 2.762,
     'L1_cond_Wgate': 2.978,
     'L1_cond_fc1s': 5.719,
     'L1_cond_fc2s': 5.176}
    for name, (base, spread) in spreads.items():
        noise = np.random.default_rng([zlib.crc32(name.encode()), seed]).standard_normal(out[name].shape)
        drawn = base * np.exp(spread * noise) if base else spread * noise
        out[name] = jnp.asarray(drawn.astype(out[name].dtype))
    for name, factor in factors.items():
        out[name] = (out[name] * factor).astype(out[name].dtype)
    return out
```

```python
from contextlib import ExitStack

import numpy as np

import concourse.bass as bass
from concourse import mybir

B, N, D = 16, 128, 128
H0, HD0 = 16, 8
F0, FC0 = 512, 4
H1, HD1 = 16, 64
HP = H1 // 2
E, DD, DC = 8, 512, 4
CAP = B * N // E
HALVES = CAP // 128
GH = 4
NG = H0 // GH
ROW = D + E
EPS = 1e-5
TOPBIT = 29

_WIDTHS = [("ident", 128), ("headmask", H0), ("same", 128), ("before", 128), ("emask", E),
           ("slots", CAP), ("base", 1), ("slotid", HALVES), ("pow2", TOPBIT + 1)]
COLS, _at = {}, 0
for _n, _w in _WIDTHS:
    COLS[_n] = (_at, _at + _w)
    _at += _w
CONST_W = _at

_PW = [("b_ada", 6), ("bq", 1), ("bk", 1), ("bv", 1), ("bo", 1), ("b1", FC0), ("b2", 1), ("b_ada1", 1),
       ("ln1_g", 1), ("ln1_b", 1), ("qn_g", 1), ("qn_b", 1), ("kn_g", 1), ("kn_b", 1), ("mlp_g", 1),
       ("mlp_b", 1), ("b1s", E * DC), ("cT", B), ("wgate", E)]
PCOLS, _at = {}, 0
for _n, _w in _PW:
    PCOLS[_n] = (_at, _at + _w)
    _at += _w
PARAM_W = _at


def cond_seq_kernel(nc, x, const, bits, sel, param, w_ada, wqkv0, wo, w1, w2, w_ada1, wqkv1, wout,
                    fc1, fc2, b2s, out, rows):
    f32, bf16, i32 = mybir.dt.float32, mybir.dt.bfloat16, mybir.dt.int32
    ALU, ACT, AX = mybir.AluOpType, mybir.ActivationFunctionType, mybir.AxisListType

    ctx = ExitStack()
    with ctx:
        def sb(name, shape, dt=f32):
            return ctx.enter_context(nc.sbuf_tensor(name, shape, dt))

        def sem(name):
            return ctx.enter_context(nc.semaphore(name))

        K = sb("K", [128, CONST_W])
        P = sb("P", [128, PARAM_W])
        BITS = sb("BITS", [128, TOPBIT + 1], i32)
        selF = sb("selF", [H0, H0 * 128])
        selB = sb("selB", [H0, H0, 128], bf16)
        Wada = sb("Wada", [128, 6 * D])
        Wqkv0 = sb("Wqkv0", [128, 3 * D])
        Wo = sb("Wo", [128, D])
        W1 = sb("W1", [128, F0])
        W2 = sb("W2", [128, FC0, D])
        Wada1 = sb("Wada1", [128, D])
        Wqkv1 = sb("Wqkv1", [128, 3 * H1 * HD1])
        Wout = sb("Wout", [128, HP, D])
        FC1 = sb("FC1", [128, E, DD])
        FC2 = sb("FC2", [128, E, DC, D])
        B2S = sb("B2S", [1, E * D])
        ones = sb("ones", [1, 128])
        mhalf = sb("mhalf", [128, 16])
        epsT = sb("epsT", [128, 16])
        tick = sb("tick", [1, 1])
        zero = sb("zero", [128, 128])

        def k(name):
            return K[:, COLS[name][0]:COLS[name][1]]

        def p(name, j=None):
            a, z = PCOLS[name]
            return P[:, a:z] if j is None else P[:, a + j:a + j + 1]

        ident = k("ident")

        def hi(ap):
            return ap.bitcast(bf16).rearrange("p (n two) -> p n two", two=2)[:, :, 1]

        X = sb("X", [128, B, D])
        adaT = sb("adaT", [128, 6, B])
        sT = sb("sT", [128, B])
        sT2 = sb("sT2", [128, B])
        shT = sb("shT", [128, B])
        st = sb("st", [128, 4, 6])
        mv = sb("mv", [128, 4, 2])
        veps = sb("veps", [128, 4])
        rstd = sb("rstd", [128, 4])
        xn = sb("xn", [128, D])
        hT = sb("hT", [128, 128])
        mneg = sb("mneg", [128, H0])
        mTb = sb("mTb", [H0, 128], bf16)
        EX = sb("EX", [128, H0, 128])

        qT = sb("qT", [128, 128])
        kT = sb("kT", [128, 128])
        Qm = sb("Qm", [128, H0, 128])
        Vp = sb("Vp", [128, H0, 32])
        oTs = sb("oTs", [128, 4 * 128])
        rec0 = sb("rec0", [128, H0])
        o0 = sb("o0", [128, H0, HD0])
        o0T = sb("o0T", [128, 128])
        aT = sb("aT", [128, 128])

        xnB = sb("xnB", [128, 4, D])
        hB = sb("hB", [128, 512])
        gB = sb("gB", [128, FC0, 512])
        fB = sb("fB", [128, 512])

        sq = sb("sq", [128, 2, 512])
        ss = sb("ss", [128, 4, 8])
        sse = sb("sse", [128, 4, 8])
        rq = sb("rq", [128, 4, 8])
        qn = sb("qn", [128, 4, 512])
        QT = sb("QT", [128, HP, 128])
        KT = sb("KT", [128, HP, 128])
        Va = sb("Va", [128, H1, HD1 + 1])
        rec1 = sb("rec1", [128, H1])
        o1 = sb("o1", [128, H1, HD1])
        o1T = sb("o1T", [128, HP, 128])
        x3 = sb("x3", [128, D])
        x3T = sb("x3T", [128, 128])
        G = sb("G", [128, B, E])
        R = sb("R", [128, B, ROW])
        st3 = sb("st3", [128, 6])
        mv3 = sb("mv3", [128, 2])
        ve3 = sb("ve3", [128, 1])
        rs3 = sb("rs3", [128, 1])
        wmean = sb("wmean", [128, 2 * H1])

        gm = sb("gm", [128, B])
        gs = sb("gs", [128, B])
        gr = sb("gr", [128, B])
        GP = sb("GP", [128, B, E])
        GT = sb("GT", [128, 128])
        ge = sb("ge", [128, 128])
        cnt = sb("cnt", [128, 1])
        cand = sb("cand", [128, 1], i32)
        flip = sb("flip", [128, 1], i32)
        gtm = sb("gtm", [128, 128])
        ngt = sb("ngt", [128, 1])
        eqm = sb("eqm", [128, 128])
        neq = sb("neq", [128, 1])
        eqs = sb("eqs", [128, 128])
        lim = sb("lim", [128, 2])
        eqt = sb("eqt", [128, 128])
        CC = sb("CC", [128, 130])
        hiS = sb("hiS", [128, 1])
        inA = sb("inA", [128, CAP])
        inC = sb("inC", [128, CAP], bf16)
        CE = sb("CE", [128, E, 130], bf16)
        rr = sb("rr", [128, HALVES, E])
        le = sb("le", [128, E, 128])
        nle = sb("nle", [128, HALVES, E])
        idx = sb("idx", [128, HALVES, E], i32)
        GX = sb("GX", [128, E, HALVES, ROW])
        gT = sb("gT", [128, 2, CAP])
        yh = sb("yh", [128, 2, DC, CAP])
        Y = sb("Y", [128, E, HALVES, D])

        PS = ctx.enter_context(nc.psum_tensor("PS", [128, 8, 512], f32))

        def bank(i):
            return PS[:, i, :]

        ld_c, ld_x, ld_w0, ld_w1, ld_wB, ld_w2 = (sem(f"ld_{n}") for n in ("const", "x", "w0", "w1", "wB", "w2"))
        names = """pre_const pre_sel pre_ada pre_adab pre_e pre_e1 pre_r pre_s pre_sh pre_shb pre_wm pre_wc pre_wcs
        pre_vpad
        a_st a_mv a_ve a_rs a_xn a_xT a_hT a_qk a_vp a_qT a_kT a_v a_qm a_s a_m a_mT a_mTb a_sT a_e a_pv a_oT
        a_ot a_rec a_o a_oo a_o2 a_wo a_aT a_xo a_x1
        b_st b_mv b_ve b_rs b_xn b_xT b_hT b_f1 b_g b_f2 b_f b_fT b_x2
        c_st c_mv c_ve c_rs c_xn c_xT c_hT c_qk c_sq c_ss c_sse c_rq c_qn c_T c_qkT c_vp c_v c_s c_m c_mT c_mTb
        c_sT c_e c_pv c_rec c_o c_oT c_oTs c_wo c_x3 c_xs c_st3 c_mv3 c_ve3 c_rs3 c_xg c_x3T c_x3Ts c_g c_gs
        d_gm d_gsub d_ge d_gs d_gr d_gp d_gpr d_T d_GT d_cand d_cnt d_sum d_flip d_masks d_sums d_scan d_lim d_eqt
        d_C d_off d_offs d_hi d_inA d_inC d_CE d_row d_rr d_le d_nle d_idx d_xout d_rows
        e_gx e_T e_gT e_f1 e_g e_f2 e_y e_out""".split()
        S = {n: sem(n) for n in names if n != "e_gx"}
        S["e_gx"] = [sem(f"e_gx{e}") for e in range(E)]
        (pre_const, pre_sel, pre_ada, pre_adab, pre_e, pre_e1, pre_r, pre_s, pre_sh, pre_shb, pre_wm, pre_wc,
         pre_wcs, pre_vpad) = (S[n] for n in names[:14])

        block = ctx.enter_context(nc.Block())

        @block.sync
        def _(sp):
            sp.dma_start(P[:, :], param).then_inc(ld_c, 16)
            sp.dma_start(K[:, :], const).then_inc(ld_c, 16)
            sp.dma_start(Wada[:, :], w_ada).then_inc(ld_c, 16)
            sp.dma_start(Wada1[:, :], w_ada1).then_inc(ld_c, 16)
            sp.dma_start(selF[:, :], sel).then_inc(ld_c, 16)
            sp.dma_start(BITS[:, :], bits).then_inc(ld_c, 16)
            sp.dma_start(X[:, :, :], x.rearrange("b p d -> p b d")).then_inc(ld_x, 16)
            sp.dma_start(Wqkv0[:, :], wqkv0).then_inc(ld_w0, 16)
            sp.dma_start(Wo[:, :], wo).then_inc(ld_w0, 16)
            sp.dma_start(Wqkv1[:, :], wqkv1).then_inc(ld_w1, 16)
            sp.dma_start(W1[:, :], w1).then_inc(ld_wB, 16)
            sp.dma_start(W2[:, :, :], w2).then_inc(ld_wB, 16)
            sp.dma_start(Wout[:, :, :], wout).then_inc(ld_w2, 16)
            sp.dma_start(B2S[:, :], b2s).then_inc(ld_w2, 16)
            sp.dma_start(FC1[:, :, :], fc1).then_inc(ld_w2, 16)
            sp.dma_start(FC2[:, :, :, :], fc2).then_inc(ld_w2, 16)
            sp.wait_ge(S["c_xs"], B)
            sp.dma_start(out.rearrange("b p d -> p b d"), X[:, :, :]).then_inc(S["d_xout"], 16)
            sp.wait_ge(S["d_gpr"], 1)
            sp.dma_start(rows.rearrange("(b p) w -> p b w", p=128), R[:, :, :]).then_inc(S["d_rows"], 16)
            sp.wait_ge(S["d_xout"], 16)
            sp.wait_ge(S["d_rows"], 16)

        @block.tensor
        def _(pe):
            pe.wait_ge(ld_c, 96)
            for j in range(6):
                mm = nc.tensor.matmul(PS[:, 0, j * B:(j + 1) * B], Wada[:, j * D:(j + 1) * D], p("cT"),
                                      start=True, stop=True)
            mm.then_inc(pre_ada, 1)
            pe.wait_ge(pre_s, 1)
            nc.tensor.matmul(PS[:, 1, 0:B], Wada1[:, :], sT[:, :], start=True, stop=True).then_inc(pre_sh, 1)
            pe.wait_ge(ld_w0, 32)
            pe.wait_ge(pre_sel, 1)
            pe.wait_ge(pre_adab, 2)
            pe.wait_ge(pre_shb, 2)

            def transposed(o, i):
                return nc.tensor.transpose(o, i, ident)

            def scoresT0(b, g, first):
                if g == 0:
                    pe.wait_ge(S["a_mTb"], b * 1 + 1)
                if g < 2:
                    if not first:
                        pe.wait_ge(S["a_e"], b * NG + g - 1)
                else:
                    pe.wait_ge(S["a_e"], b * NG + g - 1)
                for h in range(GH):
                    nc.tensor.matmul(PS[:, g % 2, 128 * h:128 * h + 128], selB[:, GH * g + h, :], mTb[:, :],
                                     start=(h == 0), stop=False, skip_group_check=True)
                mm = nc.tensor.matmul(bank(g % 2), kT[:, :], Qm[:, GH * g:GH * g + GH, :], start=False, stop=True,
                                      skip_group_check=True)
                mm.then_inc(S["a_sT"], 1)

            def values0(b, g, first):
                pe.wait_ge(S["a_e"], b * NG + g + 1)
                if g == 0:
                    pe.wait_ge(S["a_v"], b * 1 + 1)
                    if not first:
                        pe.wait_ge(S["a_oT"], b * 1)
                for h in range(GH):
                    mm = nc.tensor.matmul(PS[32 * h:32 * h + 32, 4, 128 * g:128 * g + 128],
                                          Vp[:, GH * g + h, :], EX[:, GH * g + h, :], start=True, stop=True,
                                          tile_position=(0, 32 * h))
                mm.then_inc(S["a_pv"], 1)

            def scores0(n, g, first):
                if g == 0:
                    pe.wait_ge(S["a_kT"], n * 1 + 1)
                pe.wait_ge(S["a_qm"], n * NG + g + 1)
                if not (first and g < 2):
                    pe.wait_ge(S["a_m"], n * NG + g - 1)
                for h in range(GH):
                    mm = nc.tensor.matmul(PS[:, 2 + g % 2, 128 * h:128 * h + 128], hi(Qm[:, GH * g + h, :]),
                                          hi(kT[:, :]), start=True, stop=True)
                mm.then_inc(S["a_s"], 1)

            def step0(b, front, attn, tail, first):
                n, t = b + 1, b - 1
                if front:
                    pe.wait_ge(S["a_xn"], n * 1 + 1)
                    if not first:
                        pe.wait_ge(S["a_mTb"], n * 1)
                    transposed(PS[:, 6, 0:128], xn[:, :]).then_inc(S["a_xT"], 1)
                if attn:
                    scoresT0(b, 0, not tail)
                if front:
                    pe.wait_ge(S["a_hT"], n * 1 + 1)
                    if not first:
                        pe.wait_ge(S["a_kT"], n * 1)
                    nc.tensor.matmul(PS[:, 5, 0:128], Wqkv0[:, 0:128], hT[:, :], start=True, stop=True)
                    nc.tensor.matmul(PS[:, 5, 128:256], Wqkv0[:, 128:256], hT[:, :], start=True, stop=True)\
                        .then_inc(S["a_qk"], 1)
                    nc.tensor.matmul(PS[:, 6, 128:256], hT[:, :], Wqkv0[:, 256:384], start=True, stop=True)\
                        .then_inc(S["a_vp"], 1)
                if tail:
                    pe.wait_ge(S["a_oT"], t * 1 + 1)
                    if not isinstance(t, int) or t > 0:
                        pe.wait_ge(S["a_x1"], t * 1)
                    for g in range(NG):
                        mm = transposed(PS[:, 7, 128 * g:128 * g + 128], oTs[:, 128 * g:128 * g + 128])
                    mm.then_inc(S["a_ot"], 1)
                if attn:
                    scoresT0(b, 1, not tail)
                    values0(b, 0, not tail)
                if tail:
                    pe.wait_ge(S["a_o"], t * 1 + 1)
                    transposed(PS[:, 7, 0:128], o0[:, :, :].rearrange("p h d -> p (h d)")).then_inc(S["a_oo"], 1)
                if attn:
                    scoresT0(b, 2, not tail)
                    values0(b, 1, not tail)
                if tail:
                    pe.wait_ge(S["a_o2"], t * 1 + 1)
                    nc.tensor.matmul(PS[:, 7, 128:256], Wo[:, :], o0T[:, :], start=True, stop=True)\
                        .then_inc(S["a_wo"], 1)
                if attn:
                    scoresT0(b, 3, not tail)
                    values0(b, 2, not tail)
                if tail:
                    pe.wait_ge(S["a_aT"], t * 1 + 1)
                    transposed(PS[:, 7, 0:128], aT[:, :]).then_inc(S["a_xo"], 1)
                if front:
                    scores0(n, 0, first)
                if attn:
                    values0(b, 3, not tail)
                if front:
                    for g in range(1, NG):
                        scores0(n, g, first)
                    pe.wait_ge(S["a_m"], n * NG + NG)
                    pe.wait_ge(S["a_v"], n * 1 + 1)
                    transposed(PS[0:H0, 6, 256:384], mneg[:, :]).then_inc(S["a_mT"], 1)

            pe.wait_ge(ld_x, 16)
            step0(-1, True, False, False, True)
            step0(0, True, True, False, False)
            with pe.Fori(1, B - 1) as b:
                step0(b, True, True, True, False)
            step0(B - 1, False, True, True, False)
            step0(B, False, False, True, False)

            pe.wait_ge(S["a_x1"], B)
            pe.wait_ge(S["a_e"], B * NG)
            pe.wait_ge(ld_wB, 32)
            NB = B // 4

            def front_ff(n):
                pe.wait_ge(S["b_xn"], n + 1)
                if n:
                    pe.wait_ge(S["b_hT"], n)
                for j in range(4):
                    mm = transposed(PS[:, 0, 128 * j:128 * j + 128], xnB[:, j, :])
                mm.then_inc(S["b_xT"], 1)

            def tail_ff(n):
                pe.wait_ge(S["b_f"], n + 1)
                if n:
                    pe.wait_ge(S["b_x2"], n)
                for j in range(4):
                    mm = transposed(PS[:, 6, 128 * j:128 * j + 128], fB[:, 128 * j:128 * j + 128])
                mm.then_inc(S["b_fT"], 1)

            front_ff(0)
            for n in range(NB):
                pe.wait_ge(S["b_hT"], n + 1)
                for c in range(FC0):
                    if n:
                        pe.wait_ge(S["b_g"], FC0 * (n - 1) + c + 1)
                    nc.tensor.matmul(bank(1 + c), W1[:, 128 * c:128 * c + 128], hB[:, :], start=True, stop=True)\
                        .then_inc(S["b_f1"], 1)
                if n + 1 < NB:
                    front_ff(n + 1)
                if n:
                    tail_ff(n - 1)
                for c in range(FC0):
                    pe.wait_ge(S["b_g"], FC0 * n + c + 1)
                    mm = nc.tensor.matmul(bank(5), W2[:, c, :], gB[:, c, :], start=(c == 0), stop=(c == FC0 - 1))
                mm.then_inc(S["b_f2"], 1)
            tail_ff(NB - 1)

            pe.wait_ge(S["b_x2"], NB)
            pe.wait_ge(S["b_hT"], NB)
            pe.wait_ge(S["b_g"], FC0 * NB)
            pe.wait_ge(pre_wcs, 2)
            pe.wait_ge(ld_w2, 64)

            def head1(g, i):
                return 8 * (g // 2) + 2 * i + g % 2

            def rows64(h):
                return slice(64 * (h % 2), 64 * (h % 2) + 64)

            def scoresT1(b, g, first):
                if g == 0:
                    pe.wait_ge(S["c_mTb"], b * 1 + 1)
                    pe.wait_ge(S["c_qkT"], b * 4 + 4)
                if not (first and g < 2):
                    pe.wait_ge(S["c_e"], b * NG + g - 1)
                for i in range(GH):
                    h = head1(g, i)
                    o = PS[:, g % 2, 128 * i:128 * i + 128]
                    nc.tensor.matmul(o, KT[rows64(h), h // 2, :], QT[rows64(h), h // 2, :], start=True, stop=False)
                    mm = nc.tensor.matmul(o, selB[:, GH * g + i, :], mTb[:, :], start=False, stop=True)
                mm.then_inc(S["c_sT"], 1)

            def values1(b, g, first):
                pe.wait_ge(S["c_e"], b * NG + g + 1)
                if g == 0:
                    pe.wait_ge(S["c_v"], b * 2 + 2)
                if not (first and g < 2):
                    pe.wait_ge(S["c_o"], b * NG + g - 1)
                w = HD1 + 1
                for i in range(GH):
                    h = head1(g, i)
                    mm = nc.tensor.matmul(PS[:, 5 + g % 2, w * i:w * i + w], EX[:, GH * g + i, :], Va[:, h, :],
                                          start=True, stop=True)
                mm.then_inc(S["c_pv"], 1)

            def project1(n, j):
                if j < 2:
                    if j == 1:
                        pe.wait_ge(S["c_hT"], n * 1 + 1)
                    elif not isinstance(n, int) or n > 0:
                        pe.wait_ge(S["c_mTb"], n * 1)
                else:
                    pe.wait_ge(S["c_qn"], n * 4 + j - 1)
                pe.wait_ge(S["c_hT"], n * 1 + 1)
                nc.tensor.matmul(bank(4 - j % 2), hT[:, :], Wqkv1[:, 512 * j:512 * j + 512], start=True, stop=True)\
                    .then_inc(S["c_qk"], 1)

            def turn1(n, j):
                pe.wait_ge(S["c_qn"], n * 4 + j + 1)
                if j < 2:
                    pe.wait_ge(S["c_qn"], n * 4 + 3 + j)
                else:
                    pe.wait_ge(S["c_v"], n * 2 + j - 1)
                for i in range(4):
                    mm = transposed(PS[:, 4 - j % 2, 128 * i:128 * i + 128], qn[:, j, 128 * i:128 * i + 128])
                mm.then_inc(S["c_T"], 1)

            def value_proj1(n, j):
                pe.wait_ge(S["c_qkT"], n * 4 + j + 1)
                nc.tensor.matmul(bank(4 - j), hT[:, :], Wqkv1[:, 2048 + 512 * j:2560 + 512 * j], start=True,
                                 stop=True).then_inc(S["c_vp"], 1)

            def scores1(n, g, first):
                if not (first and g == 0):
                    pe.wait_ge(S["c_m"], n * NG + g)
                pe.wait_ge(S["c_qkT"], n * 4 + 3 + g // 2)
                for i in range(GH):
                    h = head1(g, i)
                    mm = nc.tensor.matmul(PS[:, 2, 128 * i:128 * i + 128], hi(QT[rows64(h), h // 2, :]),
                                          hi(KT[rows64(h), h // 2, :]), start=True, stop=True)
                mm.then_inc(S["c_s"], 1)

            def step1(b, front, attn, tail, first):
                n, t = b + 1, b - 1
                if front:
                    pe.wait_ge(S["c_xn"], n * 1 + 1)
                    if not first:
                        pe.wait_ge(S["c_qkT"], n * 4)
                    transposed(PS[:, 3, 0:128], xn[:, :]).then_inc(S["c_xT"], 1)
                if attn:
                    scoresT1(b, 0, not tail)
                if front:
                    project1(n, 0)
                if tail:
                    pe.wait_ge(S["c_o"], t * NG + NG)
                    if not isinstance(t, int) or t > 0:
                        pe.wait_ge(S["c_gs"], t * 1)
                    for i in range(4):
                        mm = transposed(PS[:, 7, 128 * i:128 * i + 128],
                                        o1[:, 2 * i:2 * i + 2, :].rearrange("p h d -> p (h d)"))
                    mm.then_inc(S["c_oT"], 1)
                if attn:
                    scoresT1(b, 1, not tail)
                if front:
                    project1(n, 1)
                if tail:
                    pe.wait_ge(S["c_oTs"], t * 2 + 1)
                    for i in range(4):
                        mm = transposed(PS[:, 7, 128 * i:128 * i + 128],
                                        o1[:, 8 + 2 * i:10 + 2 * i, :].rearrange("p h d -> p (h d)"))
                    mm.then_inc(S["c_oT"], 1)
                if attn:
                    values1(b, 0, not tail)
                    scoresT1(b, 2, not tail)
                if front:
                    project1(n, 2)
                if attn:
                    values1(b, 1, not tail)
                if tail:
                    pe.wait_ge(S["c_oTs"], t * 2 + 2)
                    for i in range(HP):
                        mm = nc.tensor.matmul(PS[:, 7, 0:128], o1T[:, i, :], Wout[:, i, :], start=(i == 0),
                                              stop=(i == HP - 1))
                    mm.then_inc(S["c_wo"], 1)
                if attn:
                    scoresT1(b, 3, not tail)
                if front:
                    project1(n, 3)
                if attn:
                    values1(b, 2, not tail)
                if tail:
                    pe.wait_ge(S["c_x3"], t * 1 + 1)
                    transposed(PS[:, 7, 128:256], x3[:, :]).then_inc(S["c_x3T"], 1)
                if front:
                    turn1(n, 0)
                if attn:
                    values1(b, 3, not tail)
                if tail:
                    pe.wait_ge(S["c_x3Ts"], t * 1 + 1)
                    nc.tensor.matmul(PS[:, 7, 256:256 + E], x3T[:, :], p("wgate"), start=True, stop=True)\
                        .then_inc(S["c_g"], 1)
                if front:
                    turn1(n, 1)
                    value_proj1(n, 0)
                    value_proj1(n, 1)
                    turn1(n, 2)
                    turn1(n, 3)
                    for g in range(NG):
                        scores1(n, g, first)
                    pe.wait_ge(S["c_m"], n * NG + NG)
                    transposed(PS[0:H1, 4, 0:128], mneg[:, :]).then_inc(S["c_mT"], 1)

            step1(-1, True, False, False, True)
            step1(0, True, True, False, False)
            with pe.Fori(1, B - 1) as b:
                step1(b, True, True, True, False)
            step1(B - 1, False, True, True, False)
            step1(B, False, False, True, False)

            pe.wait_ge(S["d_gp"], 1)
            transposed(PS[:, 0, 0:128], GP[:, :, :].rearrange("p b e -> p (b e)")).then_inc(S["d_T"], 1)
            pe.wait_ge(S["d_cnt"], 1)
            nc.tensor.matmul(PS[:, 1, 0:1], k("same"), cnt[:, :], start=True, stop=True).then_inc(S["d_sum"], 1)
            with pe.Fori(1, TOPBIT + 1) as i:
                pe.wait_ge(S["d_cnt"], i + 1)
                nc.tensor.matmul(PS[:, 1, 0:1], k("same"), cnt[:, :], start=True, stop=True)\
                    .then_inc(S["d_sum"], 1)
            pe.wait_ge(S["d_masks"], 2)
            nc.tensor.matmul(PS[:, 0, 0:1], k("same"), ngt[:, :], start=True, stop=True)
            nc.tensor.matmul(PS[:, 0, 1:2], k("before"), neq[:, :], start=True, stop=True).then_inc(S["d_sums"], 1)
            pe.wait_ge(S["d_C"], 1)
            nc.tensor.matmul(PS[:, 2, 0:1], k("before"), CC[:, 127:128], start=True, stop=True)\
                .then_inc(S["d_off"], 1)
            pe.wait_ge(S["d_CE"], 1)
            pe.wait_ge(S["d_inC"], 1)
            for h in range(HALVES):
                for j, (a, z) in enumerate(((0, 3), (3, 6), (6, 8))):
                    mm = nc.tensor.matmul(PS[:, 2 + 3 * h + j, 0:130 * (z - a)], inC[:, 128 * h:128 * h + 128],
                                          CE[:, a:z, :].rearrange("p e w -> p (e w)"), start=True, stop=True)
                mm.then_inc(S["d_row"], 1)

            pe.wait_ge(S["d_le"], HALVES)

            def turn_e(e):
                pe.wait_ge(S["e_gx"][e], 32)
                if e:
                    pe.wait_ge(S["e_gT"], e)
                for h in range(HALVES):
                    mm = transposed(PS[:, 0, 128 * h:128 * h + 128], GX[:, e, h, 0:D])
                mm.then_inc(S["e_T"], 1)

            def hidden_e(e):
                pe.wait_ge(S["e_gT"], e + 1)
                if e >= 2:
                    pe.wait_ge(S["e_g"], DC * (e - 1))
                for c in range(DC):
                    mm = nc.tensor.matmul(PS[:, 1 + 2 * (e % 2) + c // 2, CAP * (c % 2):CAP * (c % 2) + CAP],
                                          FC1[:, e, 128 * c:128 * c + 128], gT[:, e % 2, :], start=True, stop=True)
                    if c % 2:
                        mm.then_inc(S["e_f1"], 1)

            def out_e(e):
                pe.wait_ge(S["e_g"], DC * (e + 1))
                if e >= 2:
                    pe.wait_ge(S["e_y"], HALVES * (e - 1))
                for h in range(HALVES):
                    o = PS[:, 5 + e % 2, 128 * h:128 * h + 128]
                    nc.tensor.matmul(o, ones[:, :], B2S[:, D * e:D * e + D], start=True, stop=False)
                    for c in range(DC):
                        mm = nc.tensor.matmul(o, yh[:, e % 2, c, 128 * h:128 * h + 128], FC2[:, e, c, :],
                                              start=False, stop=(c == DC - 1))
                mm.then_inc(S["e_f2"], 1)

            turn_e(0)
            for e in range(E):
                hidden_e(e)
                if e + 1 < E:
                    turn_e(e + 1)
                if e:
                    out_e(e - 1)
            out_e(E - 1)

        @block.scalar
        def _(act):
            act.wait_ge(ld_c, 96)
            nc.scalar.activation(selB[:, :, :].rearrange("p h n -> p (h n)"), selF[:, :], ACT.Copy)\
                .then_inc(pre_sel, 1)
            nc.scalar.activation(sT[:, :], p("cT"), ACT.Exp, scale=-1.0).then_inc(pre_e, 1)

            def step0(b, front, attn, tail, first):
                n = b + 1
                if attn:
                    for g in range(NG):
                        act.wait_ge(S["a_sT"], b * NG + g + 1)
                        if g == 1 and front:
                            pass
                        if tail:
                            act.wait_ge(S["a_pv"], b * NG + g - NG + 1)
                        nc.scalar.activation(EX[:, GH * g:GH * g + GH, :].rearrange("p h n -> p (h n)"),
                                             bank(g % 2), ACT.Exp, scale=float(1.0 / np.sqrt(np.float32(HD0))))\
                            .then_inc(S["a_e"], 1)
                    act.wait_ge(S["a_pv"], b * NG + NG)
                    if tail:
                        act.wait_ge(S["a_ot"], b * 1)
                    nc.scalar.activation(oTs[:, :], bank(4), ACT.Copy).then_inc(S["a_oT"], 1)
                if front:
                    act.wait_ge(S["a_vp"], n * 1 + 1)
                    if first:
                        act.wait_ge(pre_vpad, 1)
                    nc.scalar.activation(Vp[:, :, 0:HD0], PS[:, 6, 128:256].rearrange("p (h d) -> p h d", d=HD0),
                                         ACT.Copy).then_inc(S["a_v"], 1)
                    act.wait_ge(S["a_mT"], n * 1 + 1)
                    nc.scalar.activation(mTb[:, :], PS[0:H0, 6, 256:384], ACT.Copy).then_inc(S["a_mTb"], 1)

            step0(-1, True, False, False, True)
            step0(0, True, True, False, False)
            with act.Fori(1, B - 1) as b:
                step0(b, True, True, True, False)
            step0(B - 1, False, True, True, False)

            for n in range(B // 4):
                for c in range(FC0):
                    act.wait_ge(S["b_f1"], FC0 * n + c + 1)
                    if n:
                        act.wait_ge(S["b_f2"], n)
                    nc.scalar.activation(gB[:, c, :], bank(1 + c), ACT.Gelu, bias=p("b1", c)).then_inc(S["b_g"], 1)

            def step1(b, front, attn, tail, first):
                n, t = b + 1, b - 1

                def exps(g):
                    act.wait_ge(S["c_sT"], b * NG + g + 1)
                    if tail:
                        act.wait_ge(S["c_pv"], b * NG + g - NG + 1)
                    nc.scalar.activation(EX[:, GH * g:GH * g + GH, :].rearrange("p h n -> p (h n)"),
                                         bank(g % 2), ACT.Exp, scale=float(1.0 / np.sqrt(np.float32(HD1))))\
                        .then_inc(S["c_e"], 1)

                def squares(j):
                    act.wait_ge(S["c_qk"], n * 4 + j + 1)
                    if j >= 2:
                        act.wait_ge(S["c_ss"], n * 4 + j - 1)
                    elif not first:
                        act.wait_ge(S["c_ss"], n * 4 - 2 + j + 1)
                    nc.scalar.activation(sq[:, j % 2, :], bank(4 - j % 2), ACT.Square,
                                         scale=1.0 / float(np.sqrt(np.float32(HD1)))).then_inc(S["c_sq"], 1)

                def copy_oT(j):
                    act.wait_ge(S["c_oT"], t * 2 + j + 1)
                    if (not isinstance(t, int) or t > 0) and j == 0:
                        act.wait_ge(S["c_wo"], t * 1)
                    nc.scalar.activation(o1T[:, 4 * j:4 * j + 4, :].rearrange("p i n -> p (i n)"), bank(7), ACT.Copy)\
                        .then_inc(S["c_oTs"], 1)

                def turned(j):
                    act.wait_ge(S["c_T"], n * 4 + j + 1)
                    if not first:
                        act.wait_ge(S["c_sT"], n * NG)
                    dst = (QT, KT)[j // 2]
                    gn = ("qn", "kn")[j // 2]
                    nc.scalar.activation(dst[:, 4 * (j % 2):4 * (j % 2) + 4, :].rearrange("p i n -> p (i n)"),
                                         bank(4 - j % 2), ACT.Identity, scale=p(gn + "_g"), bias=p(gn + "_b"))\
                        .then_inc(S["c_qkT"], 1)

                def copy_v(j):
                    act.wait_ge(S["c_vp"], n * 2 + j + 1)
                    if not first:
                        act.wait_ge(S["c_pv"], n * NG)
                    nc.scalar.activation(Va[:, 8 * j:8 * j + 8, 0:HD1],
                                         bank(4 - j).rearrange("p (h d) -> p h d", d=HD1), ACT.Copy)\
                        .then_inc(S["c_v"], 1)

                if attn:
                    exps(0)
                if front:
                    squares(0)
                if tail:
                    copy_oT(0)
                if attn:
                    exps(1)
                if front:
                    squares(1)
                if tail:
                    copy_oT(1)
                if attn:
                    exps(2)
                if front:
                    squares(2)
                if attn:
                    exps(3)
                if front:
                    squares(3)
                if tail:
                    act.wait_ge(S["c_x3T"], t * 1 + 1)
                    nc.scalar.activation(x3T[:, :], PS[:, 7, 128:256], ACT.Copy).then_inc(S["c_x3Ts"], 1)
                if front:
                    turned(0)
                    turned(1)
                    copy_v(0)
                    copy_v(1)
                    turned(2)
                    turned(3)
                    act.wait_ge(S["c_mT"], n * 1 + 1)
                    nc.scalar.activation(mTb[:, :], PS[0:H1, 4, 0:128], ACT.Copy).then_inc(S["c_mTb"], 1)

            act.wait_ge(S["c_xn"], 1)
            step1(-1, True, False, False, True)
            step1(0, True, True, False, False)
            with act.Fori(1, B - 1) as b:
                step1(b, True, True, True, False)
            step1(B - 1, False, True, True, False)
            step1(B, False, False, True, False)

            act.wait_ge(S["d_gsub"], 1)
            nc.scalar.activation(GP[:, :, :], G[:, :, :], ACT.Exp).then_inc(S["d_ge"], 1)
            for e in range(E):
                for c in range(DC):
                    act.wait_ge(S["e_f1"], DC // 2 * e + c // 2 + 1)
                    if e >= 2:
                        act.wait_ge(S["e_f2"], e - 1)
                    nc.scalar.activation(yh[:, e % 2, c, :],
                                         PS[:, 1 + 2 * (e % 2) + c // 2, CAP * (c % 2):CAP * (c % 2) + CAP],
                                         ACT.Gelu_apprx_tanh, bias=p("b1s", DC * e + c)).then_inc(S["e_g"], 1)

        @block.vector
        def _(dve):
            V = nc.vector
            V.memset(Vp[:, :, :], 0.0).then_inc(pre_const, 1)
            V.memset(Va[:, :, HD1:HD1 + 1], 1.0)
            V.memset(mhalf[:, :], -0.5)
            V.memset(epsT[:, :], EPS)
            V.memset(zero[:, :], 0.0)
            V.memset(ones[:, :], 1.0).then_inc(pre_const, 1)
            dve.wait_ge(pre_const, 1)
            V.memset(Vp[:, :, HD0:HD0 + 1], 1.0).then_inc(pre_vpad, 1)
            dve.wait_ge(pre_ada, 1)
            V.tensor_tensor(adaT[:, :, :], PS[:, 0, 0:6 * B].rearrange("p (j b) -> p j b", b=B),
                            p("b_ada").unsqueeze(2).to_broadcast([128, 6, B]), ALU.add).then_inc(pre_adab, 1)
            dve.wait_ge(pre_adab, 1)
            sc = adaT[:, :, :].rearrange("p (t j) b -> p t j b", t=2)[:, :, 1, :]
            V.tensor_scalar_add(sc, sc, 1.0).then_inc(pre_adab, 1)
            dve.wait_ge(pre_e, 1)
            V.tensor_scalar_add(sT2[:, :], sT[:, :], 1.0).then_inc(pre_e1, 1)
            dve.wait_ge(pre_e1, 1)
            V.reciprocal(sT2[:, :], sT2[:, :]).then_inc(pre_r, 1)
            dve.wait_ge(pre_r, 1)
            V.tensor_tensor(sT[:, :], p("cT"), sT2[:, :], ALU.mult).then_inc(pre_s, 1)
            dve.wait_ge(pre_sh, 1)
            V.tensor_scalar(shT[:, :], PS[:, 1, 0:B], p("b_ada1"), p("ln1_b"), ALU.add, ALU.add)\
                .then_inc(pre_shb, 1)
            dve.wait_ge(pre_shb, 1)
            dve.wait_ge(pre_adab, 2)
            V.memset(mneg[:, :], 0.0).then_inc(pre_shb, 1)

            def step0(b, front, attn, tail, first):
                n, t = b + 1, b - 1
                if front:
                    xb = X[:, n, :]
                    V.bn_stats(st[:, 0, :], xb).then_inc(S["a_st"], 1)
                    dve.wait_ge(S["a_st"], n * 1 + 1)
                    if not first:
                        dve.wait_ge(S["a_ve"], n * 1)
                    V.memset(tick[:, :], 0.0)
                    V.bn_aggr(mv[:, 0, :], st[:, 0, :]).then_inc(S["a_mv"], 1)
                    dve.wait_ge(S["a_rs"], n * 1 + 1)
                    dve.wait_ge(S["a_mv"], n * 1 + 1)
                    if not first:
                        dve.wait_ge(S["a_xT"], n * 1)
                    V.tensor_scalar(xn[:, :], xb, mv[:, 0, 0:1], rstd[:, 0:1], ALU.subtract, ALU.mult)\
                        .then_inc(S["a_xn"], 1)
                    dve.wait_ge(S["a_xT"], n * 1 + 1)
                    if not first:
                        dve.wait_ge(S["a_vp"], n * 1)
                    V.tensor_scalar(hT[:, :], PS[:, 6, 0:128], adaT[:, 1, bass.ds(n, 1)],
                                    adaT[:, 0, bass.ds(n, 1)], ALU.mult, ALU.add).then_inc(S["a_hT"], 1)
                if tail:
                    dve.wait_ge(S["a_ot"], t * 1 + 1)
                    ot = bank(7).rearrange("p (h w) -> p h w", w=32)
                    V.reciprocal(rec0[:, :], ot[:, :, HD0]).then_inc(S["a_rec"], 1)
                    dve.wait_ge(S["a_rec"], t * 1 + 1)
                    V.tensor_tensor(o0[:, :, :], ot[:, :, 0:HD0],
                                    rec0[:, :].unsqueeze(2).to_broadcast([128, H0, HD0]), ALU.mult)\
                        .then_inc(S["a_o"], 1)
                if front:
                    dve.wait_ge(S["a_qk"], n * 1 + 1)
                    if not first:
                        dve.wait_ge(S["a_qm"], n * NG)
                    V.tensor_scalar_add(qT[:, :], PS[:, 5, 0:128], p("bq")).then_inc(S["a_qT"], 1)
                if tail:
                    dve.wait_ge(S["a_oo"], t * 1 + 1)
                    V.tensor_scalar_add(o0T[:, :], PS[:, 7, 0:128], p("bv")).then_inc(S["a_o2"], 1)
                    dve.wait_ge(S["a_wo"], t * 1 + 1)
                    V.tensor_scalar(aT[:, :], PS[:, 7, 128:256], p("bo"), adaT[:, 2, bass.ds(t, 1)],
                                    ALU.add, ALU.mult).then_inc(S["a_aT"], 1)
                if front:
                    if not first:
                        dve.wait_ge(S["a_sT"], n * NG)
                    V.tensor_scalar_add(kT[:, :], PS[:, 5, 128:256], p("bk")).then_inc(S["a_kT"], 1)
                if tail:
                    dve.wait_ge(S["a_xo"], t * 1 + 1)
                    xt = X[:, t, :]
                    V.tensor_tensor(xt, PS[:, 7, 0:128], xt, ALU.add).then_inc(S["a_x1"], 1)
                if front:
                    for g in range(NG):
                        dve.wait_ge(S["a_s"], n * NG + g + 1)
                        if g == 0 and not first:
                            dve.wait_ge(S["a_mT"], n * 1)
                        V.tensor_reduce(mneg[:, GH * g:GH * g + GH],
                                        bank(2 + g % 2).rearrange("p (h k) -> p h k", h=GH), AX.X, ALU.max,
                                        negate=True).then_inc(S["a_m"], 1)

            dve.wait_ge(ld_x, 16)
            step0(-1, True, False, False, True)
            step0(0, True, True, False, False)
            with dve.Fori(1, B - 1) as b:
                step0(b, True, True, True, False)
            step0(B - 1, False, True, True, False)
            step0(B, False, False, True, False)

            NB = B // 4
            dve.wait_ge(ld_w1, 16)
            wqk = Wqkv1[:, 0:2 * H1 * HD1].rearrange("p (h d) -> p h d", d=HD1)
            V.tensor_reduce(wmean[:, :], wqk, AX.X, ALU.add).then_inc(pre_wm, 1)
            dve.wait_ge(pre_wm, 1)
            V.tensor_scalar_mul(wmean[:, :], wmean[:, :], 1.0 / HD1).then_inc(pre_wc, 1)
            dve.wait_ge(pre_wc, 1)
            for j in range(2):
                V.tensor_tensor(wqk[:, H1 * j:H1 * j + H1, :], wqk[:, H1 * j:H1 * j + H1, :],
                                wmean[:, H1 * j:H1 * j + H1].unsqueeze(2).to_broadcast([128, H1, HD1]),
                                ALU.subtract).then_inc(pre_wcs, 1)
            dve.wait_ge(S["a_x1"], B)

            def front_ff(n):
                for j in range(4):
                    ins = V.bn_stats(st[:, j, :], X[:, 4 * n + j, :])
                ins.then_inc(S["b_st"], 1)
                dve.wait_ge(S["b_st"], n + 1)
                if n:
                    dve.wait_ge(S["b_ve"], n)
                for j in range(4):
                    ins = V.bn_aggr(mv[:, j, :], st[:, j, :])
                ins.then_inc(S["b_mv"], 1)
                dve.wait_ge(S["b_mv"], n + 1)
                dve.wait_ge(S["b_rs"], n + 1)
                if n:
                    dve.wait_ge(S["b_xT"], n)
                for j in range(4):
                    ins = V.tensor_scalar(xnB[:, j, :], X[:, 4 * n + j, :], mv[:, j, 0:1], rstd[:, j:j + 1],
                                          ALU.subtract, ALU.mult)
                ins.then_inc(S["b_xn"], 1)
                dve.wait_ge(S["b_xT"], n + 1)
                if n:
                    dve.wait_ge(S["b_f1"], FC0 * n)
                for j in range(4):
                    t = 4 * n + j
                    ins = V.tensor_scalar(hB[:, 128 * j:128 * j + 128], PS[:, 0, 128 * j:128 * j + 128],
                                          adaT[:, 4, t:t + 1], adaT[:, 3, t:t + 1], ALU.mult, ALU.add)
                ins.then_inc(S["b_hT"], 1)

            def tail_ff(n):
                dve.wait_ge(S["b_f2"], n + 1)
                if n:
                    dve.wait_ge(S["b_fT"], n)
                for j in range(4):
                    t = 4 * n + j
                    ins = V.tensor_scalar(fB[:, 128 * j:128 * j + 128], PS[:, 5, 128 * j:128 * j + 128], p("b2"),
                                          adaT[:, 5, t:t + 1], ALU.add, ALU.mult)
                ins.then_inc(S["b_f"], 1)

            def add_ff(n):
                dve.wait_ge(S["b_fT"], n + 1)
                xs = X[:, 4 * n:4 * n + 4, :].rearrange("p b d -> p (b d)")
                V.tensor_tensor(xs, bank(6), xs, ALU.add).then_inc(S["b_x2"], 1)

            front_ff(0)
            for n in range(NB):
                if n + 1 < NB:
                    front_ff(n + 1)
                if n:
                    add_ff(n - 1)
                tail_ff(n)
            add_ff(NB - 1)

            def step1(b, front, attn, tail, first):
                n, t = b + 1, b - 1

                def reduce_sq(j):
                    dve.wait_ge(S["c_sq"], n * 4 + j + 1)
                    if not first:
                        dve.wait_ge(S["c_sse"], n * 4 + j - 3)
                    V.tensor_reduce(ss[:, j, :], sq[:, j % 2, :].rearrange("p (h d) -> p h d", d=HD1), AX.X, ALU.add)\
                        .then_inc(S["c_ss"], 1)

                def scale_qk(j):
                    dve.wait_ge(S["c_rq"], n * 4 + j + 1)
                    if not first:
                        dve.wait_ge(S["c_T"], n * 4 + j - 3)
                    V.tensor_tensor(qn[:, j, :].rearrange("p (h d) -> p h d", d=HD1),
                                    bank(4 - j % 2).rearrange("p (h d) -> p h d", d=HD1),
                                    rq[:, j, :].unsqueeze(2).to_broadcast([128, 8, HD1]), ALU.mult)\
                        .then_inc(S["c_qn"], 1)

                def scale_o(g):
                    dve.wait_ge(S["c_pv"], b * NG + g + 1)
                    v = PS[:, 5 + g % 2, 0:GH * (HD1 + 1)].rearrange("p (h w) -> p h w", w=HD1 + 1)
                    V.reciprocal(rec1[:, GH * g:GH * g + GH], v[:, :, HD1]).then_inc(S["c_rec"], 1)
                    dve.wait_ge(S["c_rec"], b * NG + g + 1)
                    if tail and g == 0:
                        dve.wait_ge(S["c_oT"], b * 2)
                    heads = o1[:, 8 * (g // 2):8 * (g // 2) + 8, :].rearrange("p (i two) d -> p two i d", two=2)
                    V.tensor_tensor(heads[:, g % 2, :, :], v[:, :, 0:HD1],
                                    rec1[:, GH * g:GH * g + GH].unsqueeze(2).to_broadcast([128, GH, HD1]),
                                    ALU.mult).then_inc(S["c_o"], 1)

                if front:
                    xb = X[:, n, :]
                    V.bn_stats(st[:, 0, :], xb).then_inc(S["c_st"], 1)
                    dve.wait_ge(S["c_st"], n * 1 + 1)
                    if not first:
                        dve.wait_ge(S["c_ve"], n * 1)
                    V.memset(tick[:, :], 0.0)
                    V.bn_aggr(mv[:, 0, :], st[:, 0, :]).then_inc(S["c_mv"], 1)
                    dve.wait_ge(S["c_rs"], n * 1 + 1)
                    dve.wait_ge(S["c_mv"], n * 1 + 1)
                    if not first:
                        dve.wait_ge(S["c_xT"], n * 1)
                    V.tensor_scalar(xn[:, :], xb, mv[:, 0, 0:1], rstd[:, 0:1], ALU.subtract, ALU.mult)\
                        .then_inc(S["c_xn"], 1)
                    dve.wait_ge(S["c_xT"], n * 1 + 1)
                    if not first:
                        dve.wait_ge(S["c_vp"], n * 2)
                    V.tensor_scalar(hT[:, :], PS[:, 3, 0:128], p("ln1_g"), shT[:, bass.ds(n, 1)],
                                    ALU.mult, ALU.add).then_inc(S["c_hT"], 1)
                    reduce_sq(0)
                    reduce_sq(1)
                    scale_qk(0)
                    scale_qk(1)
                if attn:
                    scale_o(0)
                if front:
                    reduce_sq(2)
                if attn:
                    scale_o(1)
                if tail:
                    dve.wait_ge(S["c_wo"], t * 1 + 1)
                    if not isinstance(t, int) or t > 0:
                        dve.wait_ge(S["c_x3T"], t * 1)
                        dve.wait_ge(S["c_xg"], t * 1)
                    V.tensor_tensor(x3[:, :], PS[:, 7, 0:128], X[:, t, :], ALU.add).then_inc(S["c_x3"], 1)
                if front:
                    scale_qk(2)
                    reduce_sq(3)
                    scale_qk(3)
                if tail:
                    dve.wait_ge(S["c_x3"], t * 1 + 1)
                    V.bn_stats(st3[:, :], x3[:, :]).then_inc(S["c_st3"], 1)
                    V.tensor_copy(X[:, t, :], x3[:, :]).then_inc(S["c_xs"], 1)
                if attn:
                    scale_o(2)
                if tail:
                    dve.wait_ge(S["c_st3"], t * 1 + 1)
                    if not isinstance(t, int) or t > 0:
                        dve.wait_ge(S["c_ve3"], t * 1)
                    V.memset(tick[:, :], 0.0)
                    V.bn_aggr(mv3[:, :], st3[:, :]).then_inc(S["c_mv3"], 1)
                    dve.wait_ge(S["c_mv3"], t * 1 + 1)
                    dve.wait_ge(S["c_rs3"], t * 1 + 1)
                    V.tensor_scalar(R[:, t, 0:D], x3[:, :], mv3[:, 0:1], rs3[:, :], ALU.subtract, ALU.mult)\
                        .then_inc(S["c_xg"], 1)
                if attn:
                    scale_o(3)
                if tail:
                    dve.wait_ge(S["c_g"], t * 1 + 1)
                    V.tensor_copy(G[:, t, :], PS[:, 7, 256:256 + E]).then_inc(S["c_gs"], 1)
                if front:
                    for g in range(NG):
                        dve.wait_ge(S["c_s"], n * NG + g + 1)
                        if g == 0 and not first:
                            dve.wait_ge(S["c_mT"], n * 1)
                        V.tensor_reduce(mneg[:, GH * g:GH * g + GH],
                                        bank(2).rearrange("p (h k) -> p h k", h=GH), AX.X, ALU.max,
                                        negate=True).then_inc(S["c_m"], 1)

            dve.wait_ge(S["b_x2"], NB)
            step1(-1, True, False, False, True)
            step1(0, True, True, False, False)
            with dve.Fori(1, B - 1) as b:
                step1(b, True, True, True, False)
            step1(B - 1, False, True, True, False)
            step1(B, False, False, True, False)

            dve.wait_ge(S["c_gs"], B)
            V.tensor_reduce(gm[:, :], G[:, :, :], AX.X, ALU.max).then_inc(S["d_gm"], 1)
            dve.wait_ge(S["d_gm"], 1)
            V.tensor_tensor(G[:, :, :], G[:, :, :], gm[:, :].unsqueeze(2).to_broadcast([128, B, E]), ALU.subtract)\
                .then_inc(S["d_gsub"], 1)
            dve.wait_ge(S["d_ge"], 1)
            V.tensor_reduce(gs[:, :], GP[:, :, :], AX.X, ALU.add).then_inc(S["d_gs"], 1)
            dve.wait_ge(S["d_gs"], 1)
            V.reciprocal(gr[:, :], gs[:, :]).then_inc(S["d_gr"], 1)
            dve.wait_ge(S["d_gr"], 1)
            V.tensor_tensor(GP[:, :, :], GP[:, :, :], gr[:, :].unsqueeze(2).to_broadcast([128, B, E]), ALU.mult)\
                .then_inc(S["d_gp"], 1)
            dve.wait_ge(S["d_gp"], 1)
            dve.wait_ge(S["c_xg"], B)
            V.tensor_copy(R[:, :, D:ROW], GP[:, :, :]).then_inc(S["d_gpr"], 1)
            dve.wait_ge(S["d_T"], 1)
            V.tensor_copy(GT[:, :], PS[:, 0, 0:128]).then_inc(S["d_GT"], 1)

            V.tensor_copy(cand[:, :], BITS[:, TOPBIT:TOPBIT + 1]).then_inc(S["d_cand"], 1)
            dve.wait_ge(S["d_GT"], 1)

            def count():
                V.tensor_scalar(ge[:, :], GT[:, :], cand[:, :].bitcast(f32), 0.0, ALU.is_ge, ALU.add,
                                accum_out=cnt[:, :]).then_inc(S["d_cnt"], 1)

            dve.wait_ge(S["d_cand"], 1)
            count()
            with dve.Fori(1, TOPBIT + 1) as i:
                dve.wait_ge(S["d_sum"], i * 1)
                V.tensor_scalar(flip[:, :], PS[:, 1, 0:1], float(CAP), k("pow2")[:, bass.ds(i - 1, 1)], ALU.is_lt,
                                ALU.mult).then_inc(S["d_flip"], 1)
                dve.wait_ge(S["d_flip"], i * 1)
                V.tensor_scalar(cand[:, :], flip[:, :], BITS[:, bass.ds(i - 1, 1)], cand[:, :], ALU.bitwise_xor,
                                ALU.bitwise_xor).then_inc(S["d_cand"], 1)
                dve.wait_ge(S["d_cand"], i + 1)
                count()
            dve.wait_ge(S["d_sum"], TOPBIT + 1)
            V.tensor_scalar(flip[:, :], PS[:, 1, 0:1], float(CAP), 1.0, ALU.is_lt, ALU.mult)\
                .then_inc(S["d_flip"], 1)
            dve.wait_ge(S["d_flip"], TOPBIT + 1)
            V.tensor_tensor(cand[:, :], flip[:, :], cand[:, :], ALU.bitwise_xor).then_inc(S["d_cand"], 1)
            dve.wait_ge(S["d_cand"], TOPBIT + 2)
            thr = cand[:, :].bitcast(f32)
            V.tensor_scalar(gtm[:, :], GT[:, :], thr, 0.0, ALU.is_gt, ALU.add, accum_out=ngt[:, :])\
                .then_inc(S["d_masks"], 1)
            V.tensor_scalar(eqm[:, :], GT[:, :], thr, 0.0, ALU.is_equal, ALU.add, accum_out=neq[:, :])\
                .then_inc(S["d_masks"], 1)
            dve.wait_ge(S["d_masks"], 2)
            V.tensor_tensor_scan(eqs[:, :], eqm[:, :], zero[:, :], 0.0, ALU.add, ALU.add).then_inc(S["d_scan"], 1)
            dve.wait_ge(S["d_sums"], 1)
            V.tensor_scalar(lim[:, 0:1], PS[:, 0, 0:1], -1.0, float(CAP), ALU.mult, ALU.add)\
                .then_inc(S["d_lim"], 1)
            dve.wait_ge(S["d_lim"], 1)
            V.tensor_tensor(lim[:, 1:2], lim[:, 0:1], PS[:, 0, 1:2], ALU.subtract).then_inc(S["d_lim"], 1)
            dve.wait_ge(S["d_lim"], 2)
            dve.wait_ge(S["d_scan"], 1)
            V.scalar_tensor_tensor(eqt[:, :], eqs[:, :], lim[:, 1:2], eqm[:, :], ALU.is_le, ALU.mult)\
                .then_inc(S["d_eqt"], 1)
            dve.wait_ge(S["d_eqt"], 1)
            V.tensor_tensor_scan(CC[:, 0:128], eqt[:, :], gtm[:, :], 0.0, ALU.add, ALU.add).then_inc(S["d_C"], 1)
            V.tensor_copy(CC[:, 129:130], k("base"))
            dve.wait_ge(S["d_off"], 1)
            V.tensor_copy(CC[:, 128:129], PS[:, 2, 0:1]).then_inc(S["d_offs"], 1)
            dve.wait_ge(S["d_offs"], 1)
            V.tensor_tensor(hiS[:, :], CC[:, 128:129], CC[:, 127:128], ALU.add).then_inc(S["d_hi"], 1)
            V.tensor_tensor(CE[:, :, :], CC[:, :].unsqueeze(1).to_broadcast([128, E, 130]),
                            k("emask").unsqueeze(2).to_broadcast([128, E, 130]), ALU.mult).then_inc(S["d_CE"], 1)
            dve.wait_ge(S["d_hi"], 1)
            V.tensor_scalar(inA[:, :], k("slots"), hiS[:, :], None, ALU.is_lt).then_inc(S["d_inA"], 1)
            dve.wait_ge(S["d_inA"], 1)
            V.scalar_tensor_tensor(inC[:, :], k("slots"), CC[:, 128:129], inA[:, :], ALU.is_ge, ALU.mult)\
                .then_inc(S["d_inC"], 1)
            done = 0
            for h in range(HALVES):
                dve.wait_ge(S["d_row"], h + 1)
                for j, (a, z) in enumerate(((0, 3), (3, 6), (6, 8))):
                    v = PS[:, 2 + 3 * h + j, 0:130 * (z - a)].rearrange("p (e w) -> p e w", w=130)
                    V.tensor_scalar(rr[:, h, a:z], v[:, :, 128], -1.0, k("slotid")[:, h:h + 1], ALU.mult, ALU.add)\
                        .then_inc(S["d_rr"], 1)
                    done += 1
                    dve.wait_ge(S["d_rr"], done)
                    ins = V.tensor_tensor(le[:, a:z, :], v[:, :, 0:128],
                                          rr[:, h, a:z].unsqueeze(2).to_broadcast([128, z - a, 128]), ALU.is_le)
                    ins.then_inc(S["d_scan"], 1)
                dve.wait_ge(S["d_scan"], 1 + 3 * (h + 1))
                V.tensor_reduce(nle[:, h, :], le[:, :, :], AX.X, ALU.add).then_inc(S["d_nle"], 1)
                dve.wait_ge(S["d_nle"], h + 1)
                for j, (a, z) in enumerate(((0, 3), (3, 6), (6, 8))):
                    v = PS[:, 2 + 3 * h + j, 0:130 * (z - a)].rearrange("p (e w) -> p e w", w=130)
                    ins = V.tensor_tensor(idx[:, h, a:z], v[:, :, 129], nle[:, h, a:z], ALU.add)
                ins.then_inc(S["d_le"], 1)

            def gained(e):
                dve.wait_ge(S["e_T"], e + 1)
                if e >= 2:
                    dve.wait_ge(S["e_f1"], DC // 2 * (e - 1))
                V.tensor_scalar(gT[:, e % 2, :], PS[:, 0, 0:CAP], p("mlp_g"), p("mlp_b"), ALU.mult, ALU.add)\
                    .then_inc(S["e_gT"], 1)

            def weigh(e):
                dve.wait_ge(S["e_f2"], e + 1)
                for h in range(HALVES):
                    V.tensor_scalar_mul(Y[:, e, h, :], PS[:, 5 + e % 2, 128 * h:128 * h + 128],
                                        GX[:, e, h, D + e:D + e + 1]).then_inc(S["e_y"], 1)

            gained(0)
            for e in range(E):
                if e + 1 < E:
                    gained(e + 1)
                if e:
                    weigh(e - 1)
            weigh(E - 1)

        @block.gpsimd
        def _(pool):
            Q = nc.gpsimd

            def rsqrt(o, ve, src, w, s_in, s_add, s_out, at, used=None):
                pool.wait_ge(s_in, at + 1)
                Q.tensor_tensor(ve, src, epsT[:, 0:w], ALU.add).then_inc(s_add, 1)
                pool.wait_ge(s_add, at + 1)
                if used is not None:
                    pool.wait_ge(*used)
                Q.tensor_tensor(o, ve, mhalf[:, 0:w], ALU.pow).then_inc(s_out, 1)

            pool.wait_ge(pre_const, 2)
            pool.wait_ge(ld_c, 96)

            def step0(b, front, attn, tail, first):
                n = b + 1
                if front:
                    rsqrt(rstd[:, 0:1], veps[:, 0:1], mv[:, 0, 1:2], 1, S["a_mv"], S["a_ve"], S["a_rs"], n * 1,
                          used=None if first else (S["a_xn"], n * 1))
                    pool.wait_ge(S["a_qT"], n * 1 + 1)
                    for g in range(NG):
                        if not first:
                            pool.wait_ge(S["a_sT"], b * NG + g + 1)
                        Q.tensor_tensor(Qm[:, GH * g:GH * g + GH, :], qT[:, :].unsqueeze(1).to_broadcast([128, GH, 128]),
                                        k("headmask")[:, GH * g:GH * g + GH].unsqueeze(2).to_broadcast([128, GH, 128]),
                                        ALU.mult).then_inc(S["a_qm"], 1)

            step0(-1, True, False, False, True)
            step0(0, True, True, False, False)
            with pool.Fori(1, B - 1) as b:
                step0(b, True, True, True, False)

            for n in range(B // 4):
                rsqrt(rstd[:, :], veps[:, :], mv[:, :, 1], 4, S["b_mv"], S["b_ve"], S["b_rs"], n,
                      used=(S["b_xn"], n) if n else (S["a_xn"], B))

            def step1(b, front, attn, tail, first):
                n, t = b + 1, b - 1
                if front:
                    rsqrt(rstd[:, 0:1], veps[:, 0:1], mv[:, 0, 1:2], 1, S["c_mv"], S["c_ve"], S["c_rs"], n * 1,
                          used=(S["b_xn"], B // 4) if first else (S["c_xn"], n * 1))
                    for j in range(4):
                        rsqrt(rq[:, j, :], sse[:, j, :], ss[:, j, :], 8, S["c_ss"], S["c_sse"], S["c_rq"],
                              n * 4 + j, used=None if first else (S["c_qn"], n * 4 + j - 3))
                if tail:
                    rsqrt(rs3[:, :], ve3[:, :], mv3[:, 1:2], 1, S["c_mv3"], S["c_ve3"], S["c_rs3"], t * 1,
                          used=None if isinstance(t, int) and t == 0 else (S["c_xg"], t * 1))

            step1(-1, True, False, False, True)
            step1(0, True, True, False, False)
            with pool.Fori(1, B - 1) as b:
                step1(b, True, True, True, False)
            step1(B - 1, False, True, True, False)
            step1(B, False, False, True, False)

            pool.wait_ge(S["d_rows"], 16)
            pool.wait_ge(S["d_le"], HALVES)
            for e in range(E):
                for h in range(HALVES):
                    Q.indirect_dma_start(out=GX[:, e, h, :], out_offset=None, in_=rows,
                                         in_offset=bass.IndirectOffsetOnAxis(ap=idx[:, h, e:e + 1], axis=0))\
                        .then_inc(S["e_gx"][e], 16)
            pool.wait_ge(S["d_xout"], 16)
            flat = out.rearrange("b p d -> (b p) d")
            for e in range(E):
                pool.wait_ge(S["e_y"], HALVES * (e + 1))
                if e:
                    pool.wait_ge(S["e_out"], 16 * HALVES * e)
                for h in range(HALVES):
                    Q.indirect_dma_start(out=flat,
                                         out_offset=bass.IndirectOffsetOnAxis(ap=idx[:, h, e:e + 1], axis=0),
                                         in_=Y[:, e, h, :], in_offset=None, compute_op=ALU.add)\
                        .then_inc(S["e_out"], 16)
            pool.wait_ge(S["e_out"], 16 * HALVES * E)


def kernel(**inputs):
    import concourse.bacc as bacc
    from concourse.bass_utils import run_bass_kernel_spmd

    def a(name):
        return np.ascontiguousarray(np.asarray(inputs[name]))

    def col(v):
        return v.reshape(-1, 128).T

    rows128 = np.arange(128)
    const = np.zeros((128, CONST_W), np.float32)
    def put(name, v):
        const[:, COLS[name][0]:COLS[name][1]] = v
    put("ident", np.eye(128))
    put("headmask", rows128[:, None] // HD0 == np.arange(H0)[None, :])
    same = (rows128[:, None] % E) == (rows128[None, :] % E)
    put("same", same)
    put("before", same & (rows128[:, None] // E < rows128[None, :] // E))
    put("emask", rows128[:, None] % E == np.arange(E)[None, :])
    put("slots", np.arange(CAP)[None, :])
    put("base", (rows128[:, None] // E) * 128)
    put("slotid", rows128[:, None] + 128 * np.arange(HALVES)[None, :])
    put("pow2", 2.0 ** (TOPBIT - np.arange(TOPBIT + 1))[None, :])
    order = [TOPBIT - 1 - i for i in range(TOPBIT)] + [TOPBIT]
    bits = np.tile(np.array([1 << j for j in order], np.int32)[None, :], (128, 1))
    sel = np.zeros((H0, H0, 128), np.float32)
    sel[np.arange(H0), np.arange(H0)] = 1.0

    param = np.zeros((128, PARAM_W), np.float32)
    vectors = {
        "b_ada": col(a("L0_cond_b_ada")), "bq": col(a("L0_cond_bq")), "bk": col(a("L0_cond_bk")),
        "bv": col(a("L0_cond_bv")), "bo": col(a("L0_cond_bo")), "b1": col(a("L0_cond_b1")),
        "b2": col(a("L0_cond_b2")), "b_ada1": col(a("L1_cond_b_ada")), "ln1_g": col(a("L1_cond_ln1_g")),
        "ln1_b": col(a("L1_cond_ln1_b")), "mlp_g": col(a("L1_cond_mlp_g")), "mlp_b": col(a("L1_cond_mlp_b")),
        "b1s": col(a("L1_cond_b1s").reshape(-1)), "cT": a("cond_1024").T, "wgate": a("L1_cond_Wgate").T,
    }
    for n in ("qn_g", "qn_b", "kn_g", "kn_b"):
        vectors[n] = np.concatenate([a("L1_cond_" + n)] * 2)[:, None]
    for n, v in vectors.items():
        param[:, PCOLS[n][0]:PCOLS[n][1]] = v

    arrays = {
        "x": a("x"), "const": const, "bits": bits, "sel": sel.reshape(H0, H0 * 128), "param": param,
        "w_ada": a("L0_cond_W_ada"),
        "wqkv0": np.concatenate([a("L0_cond_Wq"), a("L0_cond_Wk"), a("L0_cond_Wv")], axis=1),
        "wo": a("L0_cond_Wo"), "w1": a("L0_cond_W1"),
        "w2": a("L0_cond_W2").reshape(FC0, 128, D).transpose(1, 0, 2),
        "w_ada1": a("L1_cond_W_ada").T, "wqkv1": a("L1_cond_Wqkv").T,
        "wout": a("L1_cond_Wout").T.reshape(HP, 128, D).transpose(1, 0, 2),
        "fc1": a("L1_cond_fc1s").transpose(2, 0, 1),
        "fc2": a("L1_cond_fc2s").reshape(E, D, DC, 128).transpose(3, 0, 2, 1),
        "b2s": a("L1_cond_b2s").reshape(1, E * D),
    }
    arrays = {n: np.ascontiguousarray(v) for n, v in arrays.items()}

    nc = bacc.Bacc("TRN2", target_bir_lowering=False, num_devices=1)
    args = [nc.dram_tensor("in_" + n, v.shape, mybir.dt.from_np(v.dtype), kind="ExternalInput").ap()
            for n, v in arrays.items()]
    out = nc.dram_tensor("out", (B, N, D), mybir.dt.float32, kind="ExternalOutput").ap()
    rows = nc.dram_tensor("rows", (B * N, ROW), mybir.dt.float32).ap()
    cond_seq_kernel(nc, *args, out, rows)
    r = run_bass_kernel_spmd(nc, [{"in_" + n: v for n, v in arrays.items()}], core_ids=[0])
    return r.results[0]["out"]
```

```python
from contextlib import ExitStack

import numpy as np

import concourse.bass as bass
from concourse import mybir

B, N, D = 16, 128, 128
H0, HD0 = 16, 8
F0, FC0 = 512, 4
H1, HD1 = 16, 64
HP = H1 // 2
E, DD, DC = 8, 512, 4
CAP = B * N // E
HALVES = CAP // 128
GH = 4
NG = H0 // GH
ROW = D + E
EPS = 1e-5
GATE_BITS = 30
DIGIT = 3
ROUNDS = GATE_BITS // DIGIT
NCAND = 2 ** DIGIT - 1

_WIDTHS = [("ident", 128), ("headmask", H0), ("same", 128), ("before", 128), ("emask", E),
           ("slots", CAP), ("base", 1), ("slotid", HALVES), ("unit", ROUNDS)]
COLS, _at = {}, 0
for _n, _w in _WIDTHS:
    COLS[_n] = (_at, _at + _w)
    _at += _w
CONST_W = _at

_PW = [("b_ada", 6), ("bq", 1), ("bk", 1), ("bv", 1), ("bo", 1), ("b1", FC0), ("b2", 1), ("b_ada1", 1),
       ("ln1_g", 1), ("ln1_b", 1), ("qn_g", 1), ("qn_b", 1), ("kn_g", 1), ("kn_b", 1), ("mlp_g", 1),
       ("mlp_b", 1), ("b1s", E * DC), ("cT", B), ("wgate", E)]
PCOLS, _at = {}, 0
for _n, _w in _PW:
    PCOLS[_n] = (_at, _at + _w)
    _at += _w
PARAM_W = _at


def cond_seq_kernel(nc, x, const, bits, param, w_ada, wqkv0, wo, w1, w2, w_ada1, wqkv1, wout,
                    fc1, fc2, b2s, out, rows):
    f32, bf16, i32 = mybir.dt.float32, mybir.dt.bfloat16, mybir.dt.int32
    ALU, ACT, AX = mybir.AluOpType, mybir.ActivationFunctionType, mybir.AxisListType

    ctx = ExitStack()
    with ctx:
        def sb(name, shape, dt=f32):
            return ctx.enter_context(nc.sbuf_tensor(name, shape, dt))

        def sem(name):
            return ctx.enter_context(nc.semaphore(name))

        K = sb("K", [128, CONST_W])
        P = sb("P", [128, PARAM_W])
        BITS = sb("BITS", [128, ROUNDS * NCAND], i32)
        sameb = sb("sameb", [128, 128], bf16)
        identb = sb("identb", [128, 128], bf16)
        Wada = sb("Wada", [128, 6 * D])
        Wqkv0 = sb("Wqkv0", [128, 3 * D])
        Wo = sb("Wo", [128, D])
        W1 = sb("W1", [128, F0])
        W2 = sb("W2", [128, FC0, D])
        Wada1 = sb("Wada1", [128, D])
        Wqkv1 = sb("Wqkv1", [128, 3 * H1 * HD1])
        Wout = sb("Wout", [128, HP, D])
        FC1 = sb("FC1", [128, E, DD])
        FC2 = sb("FC2", [128, E, DC, D])
        B2S = sb("B2S", [1, E * D])
        ones = sb("ones", [1, 128])
        mhalf = sb("mhalf", [128, 16])
        epsT = sb("epsT", [128, 16])
        tick = sb("tick", [1, 1])
        zero = sb("zero", [128, 128])

        def k(name):
            return K[:, COLS[name][0]:COLS[name][1]]

        def p(name, j=None):
            a, z = PCOLS[name]
            return P[:, a:z] if j is None else P[:, a + j:a + j + 1]

        ident = k("ident")

        def hi(ap):
            return ap.bitcast(bf16).rearrange("p (n two) -> p n two", two=2)[:, :, 1]

        X = sb("X", [128, B, D])
        adaT = sb("adaT", [128, 6, B])
        sT = sb("sT", [128, B])
        sT2 = sb("sT2", [128, B])
        shT = sb("shT", [128, B])
        st = sb("st", [128, 4, 6])
        mv = sb("mv", [128, 4, 2])
        veps = sb("veps", [128, 4])
        rstd = sb("rstd", [128, 4])
        xn = sb("xn", [128, D])
        hT = sb("hT", [128, 128])
        mneg = sb("mneg", [128, H0], bf16)
        EX = sb("EX", [128, H0, 128])

        qT = sb("qT", [128, 128])
        kT = sb("kT", [128, 128])
        Qm = sb("Qm", [128, H0, 128])
        Vp = sb("Vp", [128, H0, 32])
        oTs = sb("oTs", [128, 4 * 128])
        rec0 = sb("rec0", [128, H0])
        o0 = sb("o0", [128, H0, HD0])
        o0T = sb("o0T", [128, 128])
        aT = sb("aT", [128, 128])

        xnB = sb("xnB", [128, 4, D])
        hB = sb("hB", [128, 512])
        gB = sb("gB", [128, FC0, 512])
        fB = sb("fB", [128, 512])

        sq = sb("sq", [128, 2, 512])
        ss = sb("ss", [128, 4, 8])
        sse = sb("sse", [128, 4, 8])
        rq = sb("rq", [128, 4, 8])
        qr = sb("qr", [128, 4, 512])
        hv = sb("hv", [128, 128])
        qn = sb("qn", [128, 4, 512])
        QT = sb("QT", [128, HP, 128])
        KT = sb("KT", [128, HP, 128])
        Va = sb("Va", [128, H1, HD1 + 1])
        rec1 = sb("rec1", [128, H1])
        o1 = sb("o1", [128, H1, HD1])
        o1T = sb("o1T", [128, HP, 128])
        x3 = sb("x3", [128, D])
        x3T = sb("x3T", [128, 128])
        G = sb("G", [128, B, E])
        R = sb("R", [128, B, ROW])
        st3 = sb("st3", [128, 6])
        mv3 = sb("mv3", [128, 2])
        ve3 = sb("ve3", [128, 1])
        rs3 = sb("rs3", [128, 1])
        wmean = sb("wmean", [128, 2 * H1])

        gm = sb("gm", [128, B])
        gs = sb("gs", [128, B])
        gr = sb("gr", [128, B])
        GP = sb("GP", [128, B, E])
        GT = sb("GT", [128, 128])
        cnt = sb("cnt", [128, NCAND], bf16)
        cand = sb("cand", [128, NCAND], i32)
        sat = sb("sat", [128, NCAND])
        nsat = sb("nsat", [128, 1])
        digit = sb("digit", [128, 1], i32)
        found = sb("found", [128, 1], i32)
        gtm = sb("gtm", [128, 128])
        ngt = sb("ngt", [128, 1])
        eqm = sb("eqm", [128, 128])
        neq = sb("neq", [128, 1])
        eqs = sb("eqs", [128, 128])
        lim = sb("lim", [128, 2])
        eqt = sb("eqt", [128, 128])
        CC = sb("CC", [128, 130])
        hiS = sb("hiS", [128, 1])
        inA = sb("inA", [128, CAP])
        inC = sb("inC", [128, CAP], bf16)
        CE = sb("CE", [128, E, 130], bf16)
        rr = sb("rr", [128, HALVES, E])
        le = sb("le", [128, E, 128])
        nle = sb("nle", [128, HALVES, E])
        idx = sb("idx", [128, HALVES, E], i32)
        GX = sb("GX", [128, E, HALVES, ROW])
        gT = sb("gT", [128, 2, CAP])
        yh = sb("yh", [128, 2, DC, CAP])
        Y = sb("Y", [128, E, HALVES, D])

        PS = ctx.enter_context(nc.psum_tensor("PS", [128, 8, 512], f32))

        def bank(i):
            return PS[:, i, :]

        ld_c, ld_x, ld_w0, ld_w1, ld_wB, ld_w2 = (sem(f"ld_{n}") for n in ("const", "x", "w0", "w1", "wB", "w2"))
        names = """pre_const pre_sel pre_ada pre_adab pre_e pre_e1 pre_r pre_s pre_sh pre_shb pre_wm pre_wc pre_wcs
        pre_vpad
        a_st a_mv a_ve a_rs a_xn a_xT a_hT a_qk a_vp a_qT a_kT a_v a_qm a_s a_m a_sT a_e a_pv a_oT
        a_ot a_rec a_o a_oo a_o2 a_wo a_aT a_xo a_x1
        b_st b_mv b_ve b_rs b_xn b_xT b_hT b_f1 b_g b_f2 b_f b_fT b_x2
        c_st c_mv c_ve c_rs c_xn c_xT c_hT c_qk c_qr c_sq c_hv c_ss c_sse c_rq c_qn c_T c_qkT c_vp c_v c_s c_m
        c_sT c_e c_pv c_rec c_o c_oT c_oTs c_wo c_x3 c_xs c_st3 c_mv3 c_ve3 c_rs3 c_xg c_x3T c_x3Ts c_g c_gs
        d_gm d_gsub d_ge d_gs d_gr d_gp d_gpr d_T d_GT d_same d_cand d_cnt d_sum d_nsat d_digit d_found d_masks d_sums d_scan d_lim d_eqt
        d_C d_off d_offs d_hi d_inA d_inC d_CE d_row d_rr d_le d_nle d_idx d_xout d_rows
        e_gx e_T e_gT e_f1 e_g e_f2 e_y e_out""".split()
        S = {n: sem(n) for n in names if n != "e_gx"}
        S["e_gx"] = [sem(f"e_gx{e}") for e in range(E)]
        (pre_const, pre_sel, pre_ada, pre_adab, pre_e, pre_e1, pre_r, pre_s, pre_sh, pre_shb, pre_wm, pre_wc,
         pre_wcs, pre_vpad) = (S[n] for n in names[:14])

        def later(i):
            return not isinstance(i, int) or i > 0

        def n_later(i, n):
            return not isinstance(i, int) or i > n

        SB = (2, 0)

        block = ctx.enter_context(nc.Block())

        @block.sync
        def _(sp):
            sp.dma_start(P[:, :], param).then_inc(ld_c, 16)
            sp.dma_start(K[:, :], const).then_inc(ld_c, 16)
            sp.dma_start(Wada[:, :], w_ada).then_inc(ld_c, 16)
            sp.dma_start(Wada1[:, :], w_ada1).then_inc(ld_c, 16)
            sp.dma_start(BITS[:, :], bits).then_inc(ld_c, 16)
            sp.dma_start(X[:, :, :], x.rearrange("b p d -> p b d")).then_inc(ld_x, 16)
            sp.dma_start(Wqkv0[:, :], wqkv0).then_inc(ld_w0, 16)
            sp.dma_start(Wo[:, :], wo).then_inc(ld_w0, 16)
            sp.dma_start(Wqkv1[:, :], wqkv1).then_inc(ld_w1, 16)
            sp.dma_start(W1[:, :], w1).then_inc(ld_wB, 16)
            sp.dma_start(W2[:, :, :], w2).then_inc(ld_wB, 16)
            sp.dma_start(Wout[:, :, :], wout).then_inc(ld_w2, 16)
            sp.dma_start(B2S[:, :], b2s).then_inc(ld_w2, 16)
            sp.dma_start(FC1[:, :, :], fc1).then_inc(ld_w2, 16)
            sp.dma_start(FC2[:, :, :, :], fc2).then_inc(ld_w2, 16)
            sp.wait_ge(S["c_xs"], B)
            sp.dma_start(out.rearrange("b p d -> p b d"), X[:, :, :]).then_inc(S["d_xout"], 16)
            sp.wait_ge(S["d_gpr"], 1)
            sp.dma_start(rows.rearrange("(b p) w -> p b w", p=128), R[:, :, :]).then_inc(S["d_rows"], 16)
            sp.wait_ge(S["d_xout"], 16)
            sp.wait_ge(S["d_rows"], 16)

        @block.tensor
        def _(pe):
            pe.wait_ge(ld_c, 80)
            for j in range(6):
                mm = nc.tensor.matmul(PS[:, 0, j * B:(j + 1) * B], Wada[:, j * D:(j + 1) * D], p("cT"),
                                      start=True, stop=True)
            mm.then_inc(pre_ada, 1)
            pe.wait_ge(pre_s, 1)
            nc.tensor.matmul(PS[:, 1, 0:B], Wada1[:, :], sT[:, :], start=True, stop=True).then_inc(pre_sh, 1)
            pe.wait_ge(ld_w0, 32)
            pe.wait_ge(pre_sel, 1)
            pe.wait_ge(pre_adab, 2)
            pe.wait_ge(pre_shb, 1)

            def transposed(o, i):
                return nc.tensor.transpose(o, i, ident)

            def max_rows(h):
                return mneg[:, h:h + 1].to_broadcast([128, 128])

            def scoresT0(b, g):
                if g == 0:
                    pe.wait_ge(S["a_m"], b * NG + NG)
                    pe.wait_ge(S["a_qm"], b * NG + NG)
                if later(b) or g >= 2:
                    pe.wait_ge(S["a_e"], b * NG + g - 1)
                for h in range(GH):
                    nc.tensor.matmul(PS[:, g % 2, 128 * h:128 * h + 128], max_rows(GH * g + h), identb[:, :],
                                     start=(h == 0), stop=False, skip_group_check=True)
                mm = nc.tensor.matmul(bank(g % 2), kT[:, :], Qm[:, GH * g:GH * g + GH, :], start=False, stop=True,
                                      skip_group_check=True)
                mm.then_inc(S["a_sT"], 1)

            def values0(b, g):
                pe.wait_ge(S["a_e"], b * NG + g + 1)
                if g == 0:
                    pe.wait_ge(S["a_v"], b * 1 + 1)
                    if later(b):
                        pe.wait_ge(S["a_oT"], b * 1)
                for h in range(GH):
                    mm = nc.tensor.matmul(PS[32 * h:32 * h + 32, 4, 128 * g:128 * g + 128],
                                          Vp[:, GH * g + h, :], EX[:, GH * g + h, :], start=True, stop=True,
                                          tile_position=(0, 32 * h))
                mm.then_inc(S["a_pv"], 1)

            def scores0(n, g):
                if g == 0:
                    pe.wait_ge(S["a_kT"], n * 1 + 1)
                pe.wait_ge(S["a_qm"], n * NG + g + 1)
                if later(n) or g >= 2:
                    pe.wait_ge(S["a_m"], n * NG + g - 1)
                for h in range(GH):
                    mm = nc.tensor.matmul(PS[:, 2 + g % 2, 128 * h:128 * h + 128], hi(Qm[:, GH * g + h, :]),
                                          hi(kT[:, :]), start=True, stop=True)
                mm.then_inc(S["a_s"], 1)

            def step0(b, ln, front, attn, tail):
                n, t = b + 1, b - 1
                if front:
                    pe.wait_ge(S["a_xn"], n * 1 + 1)
                    if later(n):
                        pe.wait_ge(S["a_v"], n * 1)
                    transposed(PS[:, 6, 0:128], xn[:, :]).then_inc(S["a_xT"], 1)
                if attn:
                    scoresT0(b, 0)
                if attn:
                    scoresT0(b, 1)
                if front:
                    pe.wait_ge(S["a_hT"], n * 1 + 1)
                    if later(n):
                        pe.wait_ge(S["a_kT"], n * 1)
                    nc.tensor.matmul(PS[:, 5, 0:128], Wqkv0[:, 0:128], hT[:, :], start=True, stop=True)
                    nc.tensor.matmul(PS[:, 5, 128:256], Wqkv0[:, 128:256], hT[:, :], start=True, stop=True)\
                        .then_inc(S["a_qk"], 1)
                if tail:
                    pe.wait_ge(S["a_oT"], t * 1 + 1)
                    if later(t):
                        pe.wait_ge(S["a_x1"], t * 1)
                    for g in range(NG):
                        mm = transposed(PS[:, 7, 128 * g:128 * g + 128], oTs[:, 128 * g:128 * g + 128])
                    mm.then_inc(S["a_ot"], 1)
                if attn:
                    values0(b, 0)
                if attn:
                    scoresT0(b, 2)
                if tail:
                    pe.wait_ge(S["a_o"], t * 1 + 1)
                    transposed(PS[:, 7, 0:128], o0[:, :, :].rearrange("p h d -> p (h d)")).then_inc(S["a_oo"], 1)
                if attn:
                    values0(b, 1)
                    scoresT0(b, 3)
                if tail:
                    pe.wait_ge(S["a_o2"], t * 1 + 1)
                    nc.tensor.matmul(PS[:, 7, 128:256], Wo[:, :], o0T[:, :], start=True, stop=True)\
                        .then_inc(S["a_wo"], 1)
                if attn:
                    values0(b, 2)
                if front:
                    scores0(n, 0)
                if tail:
                    pe.wait_ge(S["a_aT"], t * 1 + 1)
                    transposed(PS[:, 7, 0:128], aT[:, :]).then_inc(S["a_xo"], 1)
                if front:
                    for g in range(1, NG):
                        scores0(n, g)
                if attn:
                    values0(b, 3)
                if front:
                    nc.tensor.matmul(PS[:, 6, 128:256], hT[:, :], Wqkv0[:, 256:384], start=True, stop=True)\
                        .then_inc(S["a_vp"], 1)

            pe.wait_ge(ld_x, 16)
            step0(-2, True, False, False, False)
            step0(-1, True, True, False, False)
            step0(0, True, True, True, False)
            step0(1, True, True, True, True)
            with pe.Fori(2, B - 2) as b:
                step0(b, True, True, True, True)
            step0(B - 2, False, True, True, True)
            step0(B - 1, False, False, True, True)
            step0(B, False, False, False, True)
            pe.wait_ge(S["a_x1"], B)
            pe.wait_ge(S["a_e"], B * NG)
            pe.wait_ge(ld_wB, 32)
            NB = B // 4

            def front_ff(n):
                pe.wait_ge(S["b_xn"], n + 1)
                if n:
                    pe.wait_ge(S["b_hT"], n)
                for j in range(4):
                    mm = transposed(PS[:, 0, 128 * j:128 * j + 128], xnB[:, j, :])
                mm.then_inc(S["b_xT"], 1)

            def tail_ff(n):
                pe.wait_ge(S["b_f"], n + 1)
                if n:
                    pe.wait_ge(S["b_x2"], n)
                for j in range(4):
                    mm = transposed(PS[:, 6, 128 * j:128 * j + 128], fB[:, 128 * j:128 * j + 128])
                mm.then_inc(S["b_fT"], 1)

            front_ff(0)
            for n in range(NB):
                pe.wait_ge(S["b_hT"], n + 1)
                for c in range(FC0):
                    if n:
                        pe.wait_ge(S["b_g"], FC0 * (n - 1) + c + 1)
                    nc.tensor.matmul(bank(1 + c), W1[:, 128 * c:128 * c + 128], hB[:, :], start=True, stop=True)\
                        .then_inc(S["b_f1"], 1)
                if n + 1 < NB:
                    front_ff(n + 1)
                if n:
                    tail_ff(n - 1)
                for c in range(FC0):
                    pe.wait_ge(S["b_g"], FC0 * n + c + 1)
                    mm = nc.tensor.matmul(bank(5), W2[:, c, :], gB[:, c, :], start=(c == 0), stop=(c == FC0 - 1))
                mm.then_inc(S["b_f2"], 1)
            tail_ff(NB - 1)

            pe.wait_ge(S["b_x2"], NB)
            pe.wait_ge(S["b_hT"], NB)
            pe.wait_ge(S["b_g"], FC0 * NB)
            pe.wait_ge(pre_wcs, 2)
            pe.wait_ge(ld_w2, 64)

            def head1(g, i):
                return 8 * (g // 2) + 2 * i + g % 2

            def rows64(h):
                return slice(64 * (h % 2), 64 * (h % 2) + 64)

            def scoresT1(b, g):
                if g == 0:
                    pe.wait_ge(S["c_m"], b * NG + NG)
                if later(b) or g >= 2:
                    pe.wait_ge(S["c_e"], b * NG + g - 1)
                for i in range(GH):
                    h = head1(g, i)
                    o = PS[:, g % 2, 128 * i:128 * i + 128]
                    nc.tensor.matmul(o, KT[rows64(h), h // 2, :], QT[rows64(h), h // 2, :], start=True, stop=False)
                    mm = nc.tensor.matmul(o, max_rows(GH * g + i), identb[:, :], start=False, stop=True)
                mm.then_inc(S["c_sT"], 1)

            def values1(b, g):
                pe.wait_ge(S["c_e"], b * NG + g + 1)
                if g == 0:
                    pe.wait_ge(S["c_v"], b * 2 + 2)
                if later(b) or g >= 2:
                    pe.wait_ge(S["c_o"], b * NG + g - 1)
                w = HD1 + 1
                for i in range(GH):
                    mm = nc.tensor.matmul(PS[:, 5 + g % 2, w * i:w * i + w], EX[:, GH * g + i, :],
                                          Va[:, head1(g, i), :], start=True, stop=True)
                mm.then_inc(S["c_pv"], 1)

            def project1(n, j):
                if j == 0:
                    pe.wait_ge(S["c_hT"], n * 1 + 1)
                    if n_later(n, 1):
                        pe.wait_ge(S["c_v"], n * 2 - 3)
                elif j > 1:
                    pe.wait_ge(S["c_sq"], n * 4 + j - 1)
                nc.tensor.matmul(bank(4 - j % 2), hT[:, :], Wqkv1[:, 512 * j:512 * j + 512], start=True, stop=True)\
                    .then_inc(S["c_qk"], 1)

            def turn1(n, j, front1):
                pe.wait_ge(S["c_qn"], n * 4 + j + 1)
                if j < 2:
                    if front1:
                        pe.wait_ge(S["c_sq"], n * 4 + 7 + j)
                else:
                    pe.wait_ge(S["c_qkT"], n * 4 + j - 1)
                for i in range(4):
                    mm = transposed(PS[:, 4 - j % 2, 128 * i:128 * i + 128], qn[:, j, 128 * i:128 * i + 128])
                mm.then_inc(S["c_T"], 1)

            def value_proj1(n, j):
                pe.wait_ge(S["c_qkT"], n * 4 + j + 3)
                if j == 0:
                    pe.wait_ge(S["c_hv"], n * 1 + 1)
                nc.tensor.matmul(bank(4 - j), hv[:, :], Wqkv1[:, 2048 + 512 * j:2560 + 512 * j], start=True,
                                 stop=True).then_inc(S["c_vp"], 1)

            def scores1(n, g):
                if g >= 2:
                    pe.wait_ge(S["c_m"], n * NG + g - 1)
                elif later(n):
                    if g == 0:
                        pe.wait_ge(S["c_m"], n * NG - 1)
                    else:
                        pe.wait_ge(S["c_e"], n * NG - 1)
                pe.wait_ge(S["c_qkT"], n * 4 + 3 + g // 2)
                for i in range(GH):
                    h = head1(g, i)
                    mm = nc.tensor.matmul(PS[:, SB[g % 2], 128 * i:128 * i + 128], hi(QT[rows64(h), h // 2, :]),
                                          hi(KT[rows64(h), h // 2, :]), start=True, stop=True)
                mm.then_inc(S["c_s"], 1)

            def step1(b, front1, front2, attn, tail):
                m, n, t = b + 2, b + 1, b - 1
                if tail:
                    pe.wait_ge(S["c_o"], t * NG + NG)
                    if later(t):
                        pe.wait_ge(S["c_gs"], t * 1)
                    for i in range(4):
                        mm = transposed(PS[:, 7, 128 * i:128 * i + 128],
                                        o1[:, 2 * i:2 * i + 2, :].rearrange("p h d -> p (h d)"))
                    mm.then_inc(S["c_oT"], 1)
                if attn:
                    scoresT1(b, 0)
                    scoresT1(b, 1)
                if tail:
                    pe.wait_ge(S["c_oTs"], t * 2 + 1)
                    for i in range(4):
                        mm = transposed(PS[:, 7, 128 * i:128 * i + 128],
                                        o1[:, 8 + 2 * i:10 + 2 * i, :].rearrange("p h d -> p (h d)"))
                    mm.then_inc(S["c_oT"], 1)
                if front1:
                    pe.wait_ge(S["c_xn"], m * 1 + 1)
                    if n_later(m, 1):
                        pe.wait_ge(S["c_v"], m * 2 - 2)
                    transposed(PS[:, 3, 0:128], xn[:, :]).then_inc(S["c_xT"], 1)
                if attn:
                    values1(b, 0)
                if front1:
                    project1(m, 0)
                if attn:
                    scoresT1(b, 2)
                if front1:
                    project1(m, 1)
                if attn:
                    values1(b, 1)
                if tail:
                    pe.wait_ge(S["c_oTs"], t * 2 + 2)
                    for i in range(HP):
                        mm = nc.tensor.matmul(PS[:, 7, 0:128], o1T[:, i, :], Wout[:, i, :], start=(i == 0),
                                              stop=(i == HP - 1))
                    mm.then_inc(S["c_wo"], 1)
                if front1:
                    project1(m, 2)
                if attn:
                    scoresT1(b, 3)
                if front1:
                    project1(m, 3)
                if front2:
                    turn1(n, 0, front1)
                    turn1(n, 1, front1)
                if attn:
                    values1(b, 2)
                if front2:
                    turn1(n, 2, front1)
                    turn1(n, 3, front1)
                if tail:
                    pe.wait_ge(S["c_x3"], t * 1 + 1)
                    transposed(PS[:, 7, 128:256], x3[:, :]).then_inc(S["c_x3T"], 1)
                if attn:
                    values1(b, 3)
                if front2:
                    scores1(n, 0)
                    scores1(n, 1)
                if tail:
                    pe.wait_ge(S["c_x3Ts"], t * 1 + 1)
                    nc.tensor.matmul(PS[:, 7, 256:256 + E], x3T[:, :], p("wgate"), start=True, stop=True)\
                        .then_inc(S["c_g"], 1)
                if front2:
                    value_proj1(n, 0)
                    scores1(n, 2)
                    scores1(n, 3)
                    value_proj1(n, 1)

            step1(-2, True, False, False, False)
            step1(-1, True, True, False, False)
            step1(0, True, True, True, False)
            step1(1, True, True, True, True)
            with pe.Fori(2, B - 2) as b:
                step1(b, True, True, True, True)
            step1(B - 2, False, True, True, True)
            step1(B - 1, False, False, True, True)
            step1(B, False, False, False, True)

            pe.wait_ge(S["d_gp"], 1)
            transposed(PS[:, 0, 0:128], GP[:, :, :].rearrange("p b e -> p (b e)")).then_inc(S["d_T"], 1)
            pe.wait_ge(S["d_same"], 1)
            pe.wait_ge(S["d_cnt"], 1)
            nc.tensor.matmul(PS[:, 1, 0:NCAND], sameb[:, :], cnt[:, :], start=True, stop=True).then_inc(S["d_sum"], 1)
            with pe.Fori(1, ROUNDS) as i:
                pe.wait_ge(S["d_cnt"], i + 1)
                nc.tensor.matmul(PS[:, 1, 0:NCAND], sameb[:, :], cnt[:, :], start=True, stop=True)\
                    .then_inc(S["d_sum"], 1)
            pe.wait_ge(S["d_masks"], 2)
            nc.tensor.matmul(PS[:, 0, 0:1], k("same"), ngt[:, :], start=True, stop=True)
            nc.tensor.matmul(PS[:, 0, 1:2], k("before"), neq[:, :], start=True, stop=True).then_inc(S["d_sums"], 1)
            pe.wait_ge(S["d_C"], 1)
            nc.tensor.matmul(PS[:, 2, 0:1], k("before"), CC[:, 127:128], start=True, stop=True)\
                .then_inc(S["d_off"], 1)
            pe.wait_ge(S["d_CE"], 1)
            pe.wait_ge(S["d_inC"], 1)
            for h in range(HALVES):
                for j, (a, z) in enumerate(((0, 3), (3, 6), (6, 8))):
                    mm = nc.tensor.matmul(PS[:, 2 + 3 * h + j, 0:130 * (z - a)], inC[:, 128 * h:128 * h + 128],
                                          CE[:, a:z, :].rearrange("p e w -> p (e w)"), start=True, stop=True)
                mm.then_inc(S["d_row"], 1)

            pe.wait_ge(S["d_le"], HALVES)

            def turn_e(e):
                pe.wait_ge(S["e_gx"][e], 32)
                if e:
                    pe.wait_ge(S["e_gT"], e)
                for h in range(HALVES):
                    mm = transposed(PS[:, 0, 128 * h:128 * h + 128], GX[:, e, h, 0:D])
                mm.then_inc(S["e_T"], 1)

            def hidden_e(e):
                pe.wait_ge(S["e_gT"], e + 1)
                if e >= 2:
                    pe.wait_ge(S["e_g"], DC * (e - 1))
                for c in range(DC):
                    mm = nc.tensor.matmul(PS[:, 1 + 2 * (e % 2) + c // 2, CAP * (c % 2):CAP * (c % 2) + CAP],
                                          FC1[:, e, 128 * c:128 * c + 128], gT[:, e % 2, :], start=True, stop=True)
                    if c % 2:
                        mm.then_inc(S["e_f1"], 1)

            def out_e(e):
                pe.wait_ge(S["e_g"], DC * (e + 1))
                if e >= 2:
                    pe.wait_ge(S["e_y"], HALVES * (e - 1))
                for h in range(HALVES):
                    o = PS[:, 5 + e % 2, 128 * h:128 * h + 128]
                    nc.tensor.matmul(o, ones[:, :], B2S[:, D * e:D * e + D], start=True, stop=False)
                    for c in range(DC):
                        mm = nc.tensor.matmul(o, yh[:, e % 2, c, 128 * h:128 * h + 128], FC2[:, e, c, :],
                                              start=False, stop=(c == DC - 1))
                mm.then_inc(S["e_f2"], 1)

            turn_e(0)
            for e in range(E):
                hidden_e(e)
                if e + 1 < E:
                    turn_e(e + 1)
                if e:
                    out_e(e - 1)
            out_e(E - 1)

        @block.scalar
        def _(act):
            act.wait_ge(ld_c, 80)
            nc.scalar.activation(sT[:, :], p("cT"), ACT.Exp, scale=-1.0).then_inc(pre_e, 1)

            def step0(b, ln, front, attn, tail):
                n = b + 1

                def exps(g):
                    act.wait_ge(S["a_sT"], b * NG + g + 1)
                    if later(b):
                        act.wait_ge(S["a_pv"], b * NG + g - NG + 1)
                    nc.scalar.activation(EX[:, GH * g:GH * g + GH, :].rearrange("p h n -> p (h n)"),
                                         bank(g % 2), ACT.Exp, scale=float(1.0 / np.sqrt(np.float32(HD0))))\
                        .then_inc(S["a_e"], 1)

                if attn:
                    for g in range(NG):
                        exps(g)
                    act.wait_ge(S["a_pv"], b * NG + NG)
                    if later(b):
                        act.wait_ge(S["a_ot"], b * 1)
                    nc.scalar.activation(oTs[:, :], bank(4), ACT.Copy).then_inc(S["a_oT"], 1)
                if front:
                    act.wait_ge(S["a_vp"], n * 1 + 1)
                    if not later(n):
                        act.wait_ge(pre_vpad, 1)
                    nc.scalar.activation(Vp[:, :, 0:HD0], PS[:, 6, 128:256].rearrange("p (h d) -> p h d", d=HD0),
                                         ACT.Copy).then_inc(S["a_v"], 1)

            step0(-1, True, True, False, False)
            step0(0, True, True, True, False)
            step0(1, True, True, True, True)
            with act.Fori(2, B - 2) as b:
                step0(b, True, True, True, True)
            step0(B - 2, False, True, True, True)
            step0(B - 1, False, False, True, True)

            for n in range(B // 4):
                for c in range(FC0):
                    act.wait_ge(S["b_f1"], FC0 * n + c + 1)
                    if n:
                        act.wait_ge(S["b_f2"], n)
                    nc.scalar.activation(gB[:, c, :], bank(1 + c), ACT.Gelu, bias=p("b1", c)).then_inc(S["b_g"], 1)

            def step1(b, front1, front2, attn, tail):
                m, n, t = b + 2, b + 1, b - 1

                def exps(g):
                    act.wait_ge(S["c_sT"], b * NG + g + 1)
                    if later(b):
                        act.wait_ge(S["c_pv"], b * NG + g - NG + 1)
                    nc.scalar.activation(EX[:, GH * g:GH * g + GH, :].rearrange("p h n -> p (h n)"),
                                         bank(g % 2), ACT.Exp, scale=float(1.0 / np.sqrt(np.float32(HD1))))\
                        .then_inc(S["c_e"], 1)

                def squares(j):
                    act.wait_ge(S["c_qk"], m * 4 + j + 1)
                    if later(m):
                        act.wait_ge(S["c_qn"], m * 4 + j - 3)
                    nc.scalar.activation(qr[:, j, :], bank(4 - j % 2), ACT.Copy).then_inc(S["c_qr"], 1)
                    if later(m) or j >= 2:
                        act.wait_ge(S["c_ss"], m * 4 + j - 1)
                    nc.scalar.activation(sq[:, j % 2, :], bank(4 - j % 2), ACT.Square,
                                         scale=1.0 / float(np.sqrt(np.float32(HD1)))).then_inc(S["c_sq"], 1)

                def copy_oT(j):
                    act.wait_ge(S["c_oT"], t * 2 + j + 1)
                    if later(t) and j == 0:
                        act.wait_ge(S["c_wo"], t * 1)
                    nc.scalar.activation(o1T[:, 4 * j:4 * j + 4, :].rearrange("p i n -> p (i n)"), bank(7), ACT.Copy)\
                        .then_inc(S["c_oTs"], 1)

                def turned(j):
                    act.wait_ge(S["c_T"], n * 4 + j + 1)
                    if later(n):
                        act.wait_ge(S["c_sT"], n * NG)
                    dst = (QT, KT)[j // 2]
                    gn = ("qn", "kn")[j // 2]
                    nc.scalar.activation(dst[:, 4 * (j % 2):4 * (j % 2) + 4, :].rearrange("p i n -> p (i n)"),
                                         bank(4 - j % 2), ACT.Identity, scale=p(gn + "_g"), bias=p(gn + "_b"))\
                        .then_inc(S["c_qkT"], 1)

                def copy_v(j):
                    act.wait_ge(S["c_vp"], n * 2 + j + 1)
                    if later(n):
                        act.wait_ge(S["c_pv"], n * NG)
                    nc.scalar.activation(Va[:, 8 * j:8 * j + 8, 0:HD1],
                                         bank(4 - j).rearrange("p (h d) -> p h d", d=HD1), ACT.Copy)\
                        .then_inc(S["c_v"], 1)

                if tail:
                    copy_oT(0)
                if attn:
                    exps(0)
                    exps(1)
                if tail:
                    copy_oT(1)
                if front1:
                    squares(0)
                if attn:
                    exps(2)
                if front1:
                    squares(1)
                    squares(2)
                if attn:
                    exps(3)
                if front1:
                    squares(3)
                if front2:
                    turned(0)
                    turned(1)
                    turned(2)
                    turned(3)
                if tail:
                    act.wait_ge(S["c_x3T"], t * 1 + 1)
                    nc.scalar.activation(x3T[:, :], PS[:, 7, 128:256], ACT.Copy).then_inc(S["c_x3Ts"], 1)
                if front2:
                    copy_v(0)
                    copy_v(1)

            act.wait_ge(S["c_xn"], 1)
            step1(-2, True, False, False, False)
            step1(-1, True, True, False, False)
            step1(0, True, True, True, False)
            step1(1, True, True, True, True)
            with act.Fori(2, B - 2) as b:
                step1(b, True, True, True, True)
            step1(B - 2, False, True, True, True)
            step1(B - 1, False, False, True, True)
            step1(B, False, False, False, True)

            act.wait_ge(S["d_gsub"], 1)
            nc.scalar.activation(GP[:, :, :], G[:, :, :], ACT.Exp).then_inc(S["d_ge"], 1)
            for e in range(E):
                for c in range(DC):
                    act.wait_ge(S["e_f1"], DC // 2 * e + c // 2 + 1)
                    if e >= 2:
                        act.wait_ge(S["e_f2"], e - 1)
                    nc.scalar.activation(yh[:, e % 2, c, :],
                                         PS[:, 1 + 2 * (e % 2) + c // 2, CAP * (c % 2):CAP * (c % 2) + CAP],
                                         ACT.Gelu_apprx_tanh, bias=p("b1s", DC * e + c)).then_inc(S["e_g"], 1)

        @block.vector
        def _(dve):
            V = nc.vector
            V.memset(Vp[:, :, :], 0.0).then_inc(pre_const, 1)
            V.memset(Va[:, :, HD1:HD1 + 1], 1.0)
            V.memset(mhalf[:, :], -0.5)
            V.memset(epsT[:, :], EPS)
            V.memset(zero[:, :], 0.0)
            V.memset(ones[:, :], 1.0).then_inc(pre_const, 1)
            dve.wait_ge(pre_const, 1)
            V.memset(Vp[:, :, HD0:HD0 + 1], 1.0).then_inc(pre_vpad, 1)
            dve.wait_ge(pre_ada, 1)
            V.tensor_tensor(adaT[:, :, :], PS[:, 0, 0:6 * B].rearrange("p (j b) -> p j b", b=B),
                            p("b_ada").unsqueeze(2).to_broadcast([128, 6, B]), ALU.add).then_inc(pre_adab, 1)
            dve.wait_ge(pre_adab, 1)
            sc = adaT[:, :, :].rearrange("p (t j) b -> p t j b", t=2)[:, :, 1, :]
            V.tensor_scalar_add(sc, sc, 1.0).then_inc(pre_adab, 1)
            dve.wait_ge(pre_e, 1)
            V.tensor_scalar_add(sT2[:, :], sT[:, :], 1.0).then_inc(pre_e1, 1)
            dve.wait_ge(pre_e1, 1)
            V.reciprocal(sT2[:, :], sT2[:, :]).then_inc(pre_r, 1)
            dve.wait_ge(pre_r, 1)
            V.tensor_tensor(sT[:, :], p("cT"), sT2[:, :], ALU.mult).then_inc(pre_s, 1)
            dve.wait_ge(pre_sh, 1)
            V.tensor_scalar(shT[:, :], PS[:, 1, 0:B], p("b_ada1"), p("ln1_b"), ALU.add, ALU.add)\
                .then_inc(pre_shb, 1)
            dve.wait_ge(pre_shb, 1)
            dve.wait_ge(pre_adab, 2)
            V.tensor_copy(identb[:, :], ident).then_inc(pre_sel, 1)

            def step0(b, ln, front, attn, tail):
                m, n, t = b + 2, b + 1, b - 1
                if front:
                    dve.wait_ge(S["a_xT"], n * 1 + 1)
                    if later(n):
                        dve.wait_ge(S["a_vp"], n * 1)
                    V.tensor_scalar(hT[:, :], PS[:, 6, 0:128], adaT[:, 1, bass.ds(n, 1)],
                                    adaT[:, 0, bass.ds(n, 1)], ALU.mult, ALU.add).then_inc(S["a_hT"], 1)
                if tail:
                    dve.wait_ge(S["a_ot"], t * 1 + 1)
                    ot = bank(7).rearrange("p (h w) -> p h w", w=32)
                    V.reciprocal(rec0[:, :], ot[:, :, HD0]).then_inc(S["a_rec"], 1)
                    dve.wait_ge(S["a_rec"], t * 1 + 1)
                    V.tensor_tensor(o0[:, :, :], ot[:, :, 0:HD0],
                                    rec0[:, :].unsqueeze(2).to_broadcast([128, H0, HD0]), ALU.mult)\
                        .then_inc(S["a_o"], 1)
                if front:
                    dve.wait_ge(S["a_qk"], n * 1 + 1)
                    if later(n):
                        dve.wait_ge(S["a_qm"], n * NG)
                    V.tensor_scalar_add(qT[:, :], PS[:, 5, 0:128], p("bq")).then_inc(S["a_qT"], 1)
                if tail:
                    dve.wait_ge(S["a_oo"], t * 1 + 1)
                    V.tensor_scalar_add(o0T[:, :], PS[:, 7, 0:128], p("bv")).then_inc(S["a_o2"], 1)
                if front:
                    if later(n):
                        dve.wait_ge(S["a_sT"], n * NG)
                    V.tensor_scalar_add(kT[:, :], PS[:, 5, 128:256], p("bk")).then_inc(S["a_kT"], 1)
                if tail:
                    dve.wait_ge(S["a_wo"], t * 1 + 1)
                    V.tensor_scalar(aT[:, :], PS[:, 7, 128:256], p("bo"), adaT[:, 2, bass.ds(t, 1)],
                                    ALU.add, ALU.mult).then_inc(S["a_aT"], 1)
                if ln:
                    xb = X[:, m, :]
                    V.bn_stats(st[:, 0, :], xb).then_inc(S["a_st"], 1)
                    dve.wait_ge(S["a_st"], m * 1 + 1)
                    if later(m):
                        dve.wait_ge(S["a_ve"], m * 1)
                    V.memset(tick[:, :], 0.0)
                    V.bn_aggr(mv[:, 0, :], st[:, 0, :]).then_inc(S["a_mv"], 1)
                for g in range(NG):
                    if g == 2 and ln:
                        dve.wait_ge(S["a_rs"], m * 1 + 1)
                        dve.wait_ge(S["a_mv"], m * 1 + 1)
                        if later(m):
                            dve.wait_ge(S["a_xT"], m * 1)
                        V.tensor_scalar(xn[:, :], xb, mv[:, 0, 0:1], rstd[:, 0:1], ALU.subtract, ALU.mult)\
                            .then_inc(S["a_xn"], 1)
                    if front:
                        dve.wait_ge(S["a_s"], n * NG + g + 1)
                        if g == 0 and later(n):
                            dve.wait_ge(S["a_sT"], n * NG)
                        V.tensor_reduce(mneg[:, GH * g:GH * g + GH],
                                        bank(2 + g % 2).rearrange("p (h k) -> p h k", h=GH), AX.X, ALU.max,
                                        negate=True).then_inc(S["a_m"], 1)
                    if g == 1 and tail:
                        dve.wait_ge(S["a_xo"], t * 1 + 1)
                        xt = X[:, t, :]
                        V.tensor_tensor(xt, PS[:, 7, 0:128], xt, ALU.add).then_inc(S["a_x1"], 1)

            dve.wait_ge(ld_x, 16)
            step0(-2, True, False, False, False)
            step0(-1, True, True, False, False)
            step0(0, True, True, True, False)
            step0(1, True, True, True, True)
            dve.wait_ge(ld_w1, 16)
            wqk = Wqkv1[:, 0:2 * H1 * HD1].rearrange("p (h d) -> p h d", d=HD1)
            V.tensor_reduce(wmean[:, :], wqk, AX.X, ALU.add).then_inc(pre_wm, 1)
            dve.wait_ge(pre_wm, 1)
            V.tensor_scalar_mul(wmean[:, :], wmean[:, :], 1.0 / HD1).then_inc(pre_wc, 1)
            dve.wait_ge(pre_wc, 1)
            for j in range(2):
                V.tensor_tensor(wqk[:, H1 * j:H1 * j + H1, :], wqk[:, H1 * j:H1 * j + H1, :],
                                wmean[:, H1 * j:H1 * j + H1].unsqueeze(2).to_broadcast([128, H1, HD1]),
                                ALU.subtract).then_inc(pre_wcs, 1)
            with dve.Fori(2, B - 2) as b:
                step0(b, True, True, True, True)
            step0(B - 2, False, True, True, True)
            step0(B - 1, False, False, True, True)
            step0(B, False, False, False, True)

            NB = B // 4
            dve.wait_ge(S["a_x1"], B)

            def front_ff(n):
                for j in range(4):
                    ins = V.bn_stats(st[:, j, :], X[:, 4 * n + j, :])
                ins.then_inc(S["b_st"], 1)
                dve.wait_ge(S["b_st"], n + 1)
                if n:
                    dve.wait_ge(S["b_ve"], n)
                for j in range(4):
                    ins = V.bn_aggr(mv[:, j, :], st[:, j, :])
                ins.then_inc(S["b_mv"], 1)
                dve.wait_ge(S["b_mv"], n + 1)
                dve.wait_ge(S["b_rs"], n + 1)
                if n:
                    dve.wait_ge(S["b_xT"], n)
                for j in range(4):
                    ins = V.tensor_scalar(xnB[:, j, :], X[:, 4 * n + j, :], mv[:, j, 0:1], rstd[:, j:j + 1],
                                          ALU.subtract, ALU.mult)
                ins.then_inc(S["b_xn"], 1)
                dve.wait_ge(S["b_xT"], n + 1)
                if n:
                    dve.wait_ge(S["b_f1"], FC0 * n)
                for j in range(4):
                    t = 4 * n + j
                    ins = V.tensor_scalar(hB[:, 128 * j:128 * j + 128], PS[:, 0, 128 * j:128 * j + 128],
                                          adaT[:, 4, t:t + 1], adaT[:, 3, t:t + 1], ALU.mult, ALU.add)
                ins.then_inc(S["b_hT"], 1)

            def tail_ff(n):
                dve.wait_ge(S["b_f2"], n + 1)
                if n:
                    dve.wait_ge(S["b_fT"], n)
                for j in range(4):
                    t = 4 * n + j
                    ins = V.tensor_scalar(fB[:, 128 * j:128 * j + 128], PS[:, 5, 128 * j:128 * j + 128], p("b2"),
                                          adaT[:, 5, t:t + 1], ALU.add, ALU.mult)
                ins.then_inc(S["b_f"], 1)

            def add_ff(n):
                dve.wait_ge(S["b_fT"], n + 1)
                xs = X[:, 4 * n:4 * n + 4, :].rearrange("p b d -> p (b d)")
                V.tensor_tensor(xs, bank(6), xs, ALU.add).then_inc(S["b_x2"], 1)

            front_ff(0)
            for n in range(NB):
                if n + 1 < NB:
                    front_ff(n + 1)
                if n:
                    add_ff(n - 1)
                tail_ff(n)
            add_ff(NB - 1)

            def step1(b, front1, front2, attn, tail):
                m, n, t = b + 2, b + 1, b - 1

                def reduce_sq(j):
                    dve.wait_ge(S["c_sq"], m * 4 + j + 1)
                    if later(m):
                        dve.wait_ge(S["c_sse"], m * 4 + j - 3)
                    V.tensor_reduce(ss[:, j, :], sq[:, j % 2, :].rearrange("p (h d) -> p h d", d=HD1), AX.X, ALU.add)\
                        .then_inc(S["c_ss"], 1)

                def scale_qk(j):
                    dve.wait_ge(S["c_rq"], m * 4 + j + 1)
                    dve.wait_ge(S["c_qr"], m * 4 + j + 1)
                    if later(m):
                        dve.wait_ge(S["c_T"], m * 4 + j - 3)
                    V.tensor_tensor(qn[:, j, :].rearrange("p (h d) -> p h d", d=HD1),
                                    qr[:, j, :].rearrange("p (h d) -> p h d", d=HD1),
                                    rq[:, j, :].unsqueeze(2).to_broadcast([128, 8, HD1]), ALU.mult)\
                        .then_inc(S["c_qn"], 1)

                def scale_o(g):
                    dve.wait_ge(S["c_pv"], b * NG + g + 1)
                    v = PS[:, 5 + g % 2, 0:GH * (HD1 + 1)].rearrange("p (h w) -> p h w", w=HD1 + 1)
                    V.reciprocal(rec1[:, GH * g:GH * g + GH], v[:, :, HD1]).then_inc(S["c_rec"], 1)
                    dve.wait_ge(S["c_rec"], b * NG + g + 1)
                    if later(b) and g == 0:
                        dve.wait_ge(S["c_oT"], b * 2)
                    heads = o1[:, 8 * (g // 2):8 * (g // 2) + 8, :].rearrange("p (i two) d -> p two i d", two=2)
                    V.tensor_tensor(heads[:, g % 2, :, :], v[:, :, 0:HD1],
                                    rec1[:, GH * g:GH * g + GH].unsqueeze(2).to_broadcast([128, GH, HD1]),
                                    ALU.mult).then_inc(S["c_o"], 1)

                def maxima(g):
                    dve.wait_ge(S["c_s"], n * NG + g + 1)
                    if g == 0 and later(n):
                        dve.wait_ge(S["c_sT"], n * NG)
                    V.tensor_reduce(mneg[:, GH * g:GH * g + GH],
                                    bank(SB[g % 2]).rearrange("p (h k) -> p h k", h=GH), AX.X, ALU.max,
                                    negate=True).then_inc(S["c_m"], 1)

                if front1:
                    xb = X[:, m, :]
                    V.bn_stats(st[:, 0, :], xb).then_inc(S["c_st"], 1)
                    dve.wait_ge(S["c_st"], m * 1 + 1)
                    if later(m):
                        dve.wait_ge(S["c_ve"], m * 1)
                    V.memset(tick[:, :], 0.0)
                    V.bn_aggr(mv[:, 0, :], st[:, 0, :]).then_inc(S["c_mv"], 1)
                    dve.wait_ge(S["c_rs"], m * 1 + 1)
                    dve.wait_ge(S["c_mv"], m * 1 + 1)
                    if later(m):
                        dve.wait_ge(S["c_xT"], m * 1)
                    V.tensor_scalar(xn[:, :], xb, mv[:, 0, 0:1], rstd[:, 0:1], ALU.subtract, ALU.mult)\
                        .then_inc(S["c_xn"], 1)
                    dve.wait_ge(S["c_xT"], m * 1 + 1)
                    if later(m):
                        dve.wait_ge(S["c_qk"], m * 4)
                        dve.wait_ge(S["c_hv"], m * 1)
                    V.tensor_scalar(hT[:, :], PS[:, 3, 0:128], p("ln1_g"), shT[:, bass.ds(m, 1)],
                                    ALU.mult, ALU.add).then_inc(S["c_hT"], 1)
                if attn:
                    scale_o(0)
                if front1:
                    reduce_sq(0)
                if attn:
                    scale_o(1)
                if tail:
                    dve.wait_ge(S["c_wo"], t * 1 + 1)
                    if later(t):
                        dve.wait_ge(S["c_x3T"], t * 1)
                        dve.wait_ge(S["c_xg"], t * 1)
                        dve.wait_ge(S["c_xs"], t * 1)
                    V.tensor_tensor(x3[:, :], PS[:, 7, 0:128], X[:, t, :], ALU.add).then_inc(S["c_x3"], 1)
                if front1:
                    reduce_sq(1)
                if tail:
                    dve.wait_ge(S["c_x3"], t * 1 + 1)
                    V.bn_stats(st3[:, :], x3[:, :]).then_inc(S["c_st3"], 1)
                    V.tensor_copy(X[:, t, :], x3[:, :]).then_inc(S["c_xs"], 1)
                    dve.wait_ge(S["c_st3"], t * 1 + 1)
                    if later(t):
                        dve.wait_ge(S["c_ve3"], t * 1)
                    V.memset(tick[:, :], 0.0)
                    V.bn_aggr(mv3[:, :], st3[:, :]).then_inc(S["c_mv3"], 1)
                if front1:
                    reduce_sq(2)
                    reduce_sq(3)
                if attn:
                    scale_o(2)
                if attn:
                    scale_o(3)
                if front2:
                    maxima(0)
                    maxima(1)
                if tail:
                    dve.wait_ge(S["c_mv3"], t * 1 + 1)
                    dve.wait_ge(S["c_rs3"], t * 1 + 1)
                    V.tensor_scalar(R[:, t, 0:D], x3[:, :], mv3[:, 0:1], rs3[:, :], ALU.subtract, ALU.mult)\
                        .then_inc(S["c_xg"], 1)
                if front2:
                    maxima(2)
                    maxima(3)
                if tail:
                    dve.wait_ge(S["c_g"], t * 1 + 1)
                    V.tensor_copy(G[:, t, :], PS[:, 7, 256:256 + E]).then_inc(S["c_gs"], 1)
                if front1:
                    for j in range(4):
                        scale_qk(j)
                    if later(m):
                        dve.wait_ge(S["c_vp"], m * 2)
                    V.tensor_copy(hv[:, :], hT[:, :]).then_inc(S["c_hv"], 1)

            dve.wait_ge(S["b_x2"], NB)
            step1(-2, True, False, False, False)
            step1(-1, True, True, False, False)
            step1(0, True, True, True, False)
            step1(1, True, True, True, True)
            with dve.Fori(2, B - 2) as b:
                step1(b, True, True, True, True)
            step1(B - 2, False, True, True, True)
            step1(B - 1, False, False, True, True)
            step1(B, False, False, False, True)

            dve.wait_ge(S["c_gs"], B)
            V.tensor_reduce(gm[:, :], G[:, :, :], AX.X, ALU.max).then_inc(S["d_gm"], 1)
            dve.wait_ge(S["d_gm"], 1)
            V.tensor_tensor(G[:, :, :], G[:, :, :], gm[:, :].unsqueeze(2).to_broadcast([128, B, E]), ALU.subtract)\
                .then_inc(S["d_gsub"], 1)
            dve.wait_ge(S["d_ge"], 1)
            V.tensor_reduce(gs[:, :], GP[:, :, :], AX.X, ALU.add).then_inc(S["d_gs"], 1)
            dve.wait_ge(S["d_gs"], 1)
            V.reciprocal(gr[:, :], gs[:, :]).then_inc(S["d_gr"], 1)
            dve.wait_ge(S["d_gr"], 1)
            V.tensor_tensor(GP[:, :, :], GP[:, :, :], gr[:, :].unsqueeze(2).to_broadcast([128, B, E]), ALU.mult)\
                .then_inc(S["d_gp"], 1)
            dve.wait_ge(S["d_gp"], 1)
            dve.wait_ge(S["c_xg"], B)
            V.tensor_copy(R[:, :, D:ROW], GP[:, :, :]).then_inc(S["d_gpr"], 1)
            dve.wait_ge(S["d_T"], 1)
            V.tensor_copy(GT[:, :], PS[:, 0, 0:128]).then_inc(S["d_GT"], 1)

            V.tensor_copy(sameb[:, :], k("same")).then_inc(S["d_same"], 1)
            V.memset(found[:, :], 0).then_inc(S["d_found"], 1)
            V.tensor_copy(cand[:, :], BITS[:, 0:NCAND]).then_inc(S["d_cand"], 1)
            dve.wait_ge(S["d_GT"], 1)

            def count():
                for j in range(NCAND):
                    ins = V.tensor_scalar(le[:, j, :], GT[:, :], cand[:, j:j + 1].bitcast(f32), 0.0, ALU.is_ge, ALU.add,
                                          accum_out=cnt[:, j:j + 1])
                ins.then_inc(S["d_cnt"], 1)

            def next_digit(i):
                dve.wait_ge(S["d_sum"], i + 1)
                V.tensor_scalar(sat[:, :], PS[:, 1, 0:NCAND], float(CAP), 0.0, ALU.is_ge, ALU.add,
                                accum_out=nsat[:, :]).then_inc(S["d_nsat"], 1)
                dve.wait_ge(S["d_nsat"], i + 1)
                V.tensor_scalar(digit[:, :], nsat[:, :], 1.0, k("unit")[:, bass.ds(i, 1)], ALU.mult, ALU.mult)\
                    .then_inc(S["d_digit"], 1)
                dve.wait_ge(S["d_digit"], i + 1)

            def add_digit(i):
                V.tensor_tensor(found[:, :], found[:, :], digit[:, :], ALU.bitwise_or).then_inc(S["d_found"], 1)

            dve.wait_ge(S["d_cand"], 1)
            count()
            with dve.Fori(1, ROUNDS) as i:
                next_digit(i - 1)
                dve.wait_ge(S["d_found"], i * 1)
                V.tensor_scalar(cand[:, :], BITS[:, bass.ds(i * NCAND, NCAND)], digit[:, :], found[:, :],
                                ALU.bitwise_or, ALU.bitwise_or).then_inc(S["d_cand"], 1)
                add_digit(i - 1)
                dve.wait_ge(S["d_cand"], i + 1)
                count()
            next_digit(ROUNDS - 1)
            dve.wait_ge(S["d_found"], ROUNDS)
            add_digit(ROUNDS - 1)
            dve.wait_ge(S["d_found"], ROUNDS + 1)
            thr = found[:, :].bitcast(f32)
            V.tensor_scalar(gtm[:, :], GT[:, :], thr, 0.0, ALU.is_gt, ALU.add, accum_out=ngt[:, :])\
                .then_inc(S["d_masks"], 1)
            V.tensor_scalar(eqm[:, :], GT[:, :], thr, 0.0, ALU.is_equal, ALU.add, accum_out=neq[:, :])\
                .then_inc(S["d_masks"], 1)
            dve.wait_ge(S["d_masks"], 2)
            V.tensor_tensor_scan(eqs[:, :], eqm[:, :], zero[:, :], 0.0, ALU.add, ALU.add).then_inc(S["d_scan"], 1)
            dve.wait_ge(S["d_sums"], 1)
            V.tensor_scalar(lim[:, 0:1], PS[:, 0, 0:1], -1.0, float(CAP), ALU.mult, ALU.add)\
                .then_inc(S["d_lim"], 1)
            dve.wait_ge(S["d_lim"], 1)
            V.tensor_tensor(lim[:, 1:2], lim[:, 0:1], PS[:, 0, 1:2], ALU.subtract).then_inc(S["d_lim"], 1)
            dve.wait_ge(S["d_lim"], 2)
            dve.wait_ge(S["d_scan"], 1)
            V.scalar_tensor_tensor(eqt[:, :], eqs[:, :], lim[:, 1:2], eqm[:, :], ALU.is_le, ALU.mult)\
                .then_inc(S["d_eqt"], 1)
            dve.wait_ge(S["d_eqt"], 1)
            V.tensor_tensor_scan(CC[:, 0:128], eqt[:, :], gtm[:, :], 0.0, ALU.add, ALU.add).then_inc(S["d_C"], 1)
            V.tensor_copy(CC[:, 129:130], k("base"))
            dve.wait_ge(S["d_off"], 1)
            V.tensor_copy(CC[:, 128:129], PS[:, 2, 0:1]).then_inc(S["d_offs"], 1)
            dve.wait_ge(S["d_offs"], 1)
            V.tensor_tensor(hiS[:, :], CC[:, 128:129], CC[:, 127:128], ALU.add).then_inc(S["d_hi"], 1)
            V.tensor_tensor(CE[:, :, :], CC[:, :].unsqueeze(1).to_broadcast([128, E, 130]),
                            k("emask").unsqueeze(2).to_broadcast([128, E, 130]), ALU.mult).then_inc(S["d_CE"], 1)
            dve.wait_ge(S["d_hi"], 1)
            V.tensor_scalar(inA[:, :], k("slots"), hiS[:, :], None, ALU.is_lt).then_inc(S["d_inA"], 1)
            dve.wait_ge(S["d_inA"], 1)
            V.scalar_tensor_tensor(inC[:, :], k("slots"), CC[:, 128:129], inA[:, :], ALU.is_ge, ALU.mult)\
                .then_inc(S["d_inC"], 1)
            done = 0
            for h in range(HALVES):
                dve.wait_ge(S["d_row"], h + 1)
                for j, (a, z) in enumerate(((0, 3), (3, 6), (6, 8))):
                    v = PS[:, 2 + 3 * h + j, 0:130 * (z - a)].rearrange("p (e w) -> p e w", w=130)
                    V.tensor_scalar(rr[:, h, a:z], v[:, :, 128], -1.0, k("slotid")[:, h:h + 1], ALU.mult, ALU.add)\
                        .then_inc(S["d_rr"], 1)
                    done += 1
                    dve.wait_ge(S["d_rr"], done)
                    ins = V.tensor_tensor(le[:, a:z, :], v[:, :, 0:128],
                                          rr[:, h, a:z].unsqueeze(2).to_broadcast([128, z - a, 128]), ALU.is_le)
                    ins.then_inc(S["d_scan"], 1)
                dve.wait_ge(S["d_scan"], 1 + 3 * (h + 1))
                V.tensor_reduce(nle[:, h, :], le[:, :, :], AX.X, ALU.add).then_inc(S["d_nle"], 1)
                dve.wait_ge(S["d_nle"], h + 1)
                for j, (a, z) in enumerate(((0, 3), (3, 6), (6, 8))):
                    v = PS[:, 2 + 3 * h + j, 0:130 * (z - a)].rearrange("p (e w) -> p e w", w=130)
                    ins = V.tensor_tensor(idx[:, h, a:z], v[:, :, 129], nle[:, h, a:z], ALU.add)
                ins.then_inc(S["d_le"], 1)

            def gained(e):
                dve.wait_ge(S["e_T"], e + 1)
                if e >= 2:
                    dve.wait_ge(S["e_f1"], DC // 2 * (e - 1))
                V.tensor_scalar(gT[:, e % 2, :], PS[:, 0, 0:CAP], p("mlp_g"), p("mlp_b"), ALU.mult, ALU.add)\
                    .then_inc(S["e_gT"], 1)

            def weigh(e):
                dve.wait_ge(S["e_f2"], e + 1)
                for h in range(HALVES):
                    V.tensor_scalar_mul(Y[:, e, h, :], PS[:, 5 + e % 2, 128 * h:128 * h + 128],
                                        GX[:, e, h, D + e:D + e + 1]).then_inc(S["e_y"], 1)

            gained(0)
            for e in range(E):
                if e + 1 < E:
                    gained(e + 1)
                if e:
                    weigh(e - 1)
            weigh(E - 1)

        @block.gpsimd
        def _(pool):
            Q = nc.gpsimd

            def rsqrt(o, ve, src, w, s_in, s_add, s_out, at, used=None):
                pool.wait_ge(s_in, at + 1)
                Q.tensor_tensor(ve, src, epsT[:, 0:w], ALU.add).then_inc(s_add, 1)
                pool.wait_ge(s_add, at + 1)
                if used is not None:
                    pool.wait_ge(*used)
                Q.tensor_tensor(o, ve, mhalf[:, 0:w], ALU.pow).then_inc(s_out, 1)

            pool.wait_ge(pre_const, 2)
            pool.wait_ge(ld_c, 80)

            def step0(b, ln, front, attn, tail):
                m, n = b + 2, b + 1

                def mask(g):
                    if later(n):
                        pool.wait_ge(S["a_sT"], b * NG + g + 1)
                    Q.tensor_tensor(Qm[:, GH * g:GH * g + GH, :], qT[:, :].unsqueeze(1).to_broadcast([128, GH, 128]),
                                    k("headmask")[:, GH * g:GH * g + GH].unsqueeze(2).to_broadcast([128, GH, 128]),
                                    ALU.mult).then_inc(S["a_qm"], 1)

                if front:
                    pool.wait_ge(S["a_qT"], n * 1 + 1)
                    for g in range(NG):
                        mask(g)
                if ln:
                    rsqrt(rstd[:, 0:1], veps[:, 0:1], mv[:, 0, 1:2], 1, S["a_mv"], S["a_ve"], S["a_rs"], m * 1,
                          used=(S["a_xn"], m * 1) if later(m) else None)

            step0(-2, True, False, False, False)
            step0(-1, True, True, False, False)
            step0(0, True, True, True, False)
            step0(1, True, True, True, True)
            with pool.Fori(2, B - 2) as b:
                step0(b, True, True, True, True)
            step0(B - 2, False, True, True, True)

            for n in range(B // 4):
                rsqrt(rstd[:, :], veps[:, :], mv[:, :, 1], 4, S["b_mv"], S["b_ve"], S["b_rs"], n,
                      used=(S["b_xn"], n) if n else (S["a_xn"], B))

            def step1(b, front1, front2, attn, tail):
                m, n, t = b + 2, b + 1, b - 1
                if front1:
                    rsqrt(rstd[:, 0:1], veps[:, 0:1], mv[:, 0, 1:2], 1, S["c_mv"], S["c_ve"], S["c_rs"], m * 1,
                          used=(S["c_xn"], m * 1) if later(m) else (S["b_xn"], B // 4))

                def norms(j):
                    rsqrt(rq[:, j, :], sse[:, j, :], ss[:, j, :], 8, S["c_ss"], S["c_sse"], S["c_rq"],
                          m * 4 + j, used=(S["c_qn"], m * 4 + j - 3) if later(m) else None)

                if front1:
                    norms(0)
                    norms(1)
                if tail:
                    rsqrt(rs3[:, :], ve3[:, :], mv3[:, 1:2], 1, S["c_mv3"], S["c_ve3"], S["c_rs3"], t * 1,
                          used=(S["c_xg"], t * 1) if later(t) else None)
                if front1:
                    norms(2)
                    norms(3)

            step1(-2, True, False, False, False)
            step1(-1, True, True, False, False)
            step1(0, True, True, True, False)
            step1(1, True, True, True, True)
            with pool.Fori(2, B - 2) as b:
                step1(b, True, True, True, True)
            step1(B - 2, False, True, True, True)
            step1(B - 1, False, False, True, True)
            step1(B, False, False, False, True)

            pool.wait_ge(S["d_rows"], 16)
            pool.wait_ge(S["d_le"], HALVES)
            for e in range(E):
                for h in range(HALVES):
                    Q.indirect_dma_start(out=GX[:, e, h, :], out_offset=None, in_=rows,
                                         in_offset=bass.IndirectOffsetOnAxis(ap=idx[:, h, e:e + 1], axis=0))\
                        .then_inc(S["e_gx"][e], 16)
            pool.wait_ge(S["d_xout"], 16)
            flat = out.rearrange("b p d -> (b p) d")
            for e in range(E):
                pool.wait_ge(S["e_y"], HALVES * (e + 1))
                if e:
                    pool.wait_ge(S["e_out"], 16 * HALVES * e)
                for h in range(HALVES):
                    Q.indirect_dma_start(out=flat,
                                         out_offset=bass.IndirectOffsetOnAxis(ap=idx[:, h, e:e + 1], axis=0),
                                         in_=Y[:, e, h, :], in_offset=None, compute_op=ALU.add)\
                        .then_inc(S["e_out"], 16)
            pool.wait_ge(S["e_out"], 16 * HALVES * E)


def kernel(**inputs):
    import concourse.bacc as bacc
    from concourse.bass_utils import run_bass_kernel_spmd

    def a(name):
        return np.ascontiguousarray(np.asarray(inputs[name]))

    def col(v):
        return v.reshape(-1, 128).T

    rows128 = np.arange(128)
    const = np.zeros((128, CONST_W), np.float32)
    def put(name, v):
        const[:, COLS[name][0]:COLS[name][1]] = v
    put("ident", np.eye(128))
    put("headmask", rows128[:, None] // HD0 == np.arange(H0)[None, :])
    same = (rows128[:, None] % E) == (rows128[None, :] % E)
    put("same", same)
    put("before", same & (rows128[:, None] // E < rows128[None, :] // E))
    put("emask", rows128[:, None] % E == np.arange(E)[None, :])
    put("slots", np.arange(CAP)[None, :])
    put("base", (rows128[:, None] // E) * 128)
    put("slotid", rows128[:, None] + 128 * np.arange(HALVES)[None, :])
    unit = 2 ** (GATE_BITS - DIGIT * (1 + np.arange(ROUNDS)))
    put("unit", unit[None, :])
    bits = np.tile((unit[:, None] * (1 + np.arange(NCAND))[None, :]).reshape(1, -1).astype(np.int32), (128, 1))

    param = np.zeros((128, PARAM_W), np.float32)
    vectors = {
        "b_ada": col(a("L0_cond_b_ada")), "bq": col(a("L0_cond_bq")), "bk": col(a("L0_cond_bk")),
        "bv": col(a("L0_cond_bv")), "bo": col(a("L0_cond_bo")), "b1": col(a("L0_cond_b1")),
        "b2": col(a("L0_cond_b2")), "b_ada1": col(a("L1_cond_b_ada")), "ln1_g": col(a("L1_cond_ln1_g")),
        "ln1_b": col(a("L1_cond_ln1_b")), "mlp_g": col(a("L1_cond_mlp_g")), "mlp_b": col(a("L1_cond_mlp_b")),
        "b1s": col(a("L1_cond_b1s").reshape(-1)), "cT": a("cond_1024").T, "wgate": a("L1_cond_Wgate").T,
    }
    for n in ("qn_g", "qn_b", "kn_g", "kn_b"):
        vectors[n] = np.concatenate([a("L1_cond_" + n)] * 2)[:, None]
    for n, v in vectors.items():
        param[:, PCOLS[n][0]:PCOLS[n][1]] = v

    arrays = {
        "x": a("x"), "const": const, "bits": bits, "param": param,
        "w_ada": a("L0_cond_W_ada"),
        "wqkv0": np.concatenate([a("L0_cond_Wq"), a("L0_cond_Wk"), a("L0_cond_Wv")], axis=1),
        "wo": a("L0_cond_Wo"), "w1": a("L0_cond_W1"),
        "w2": a("L0_cond_W2").reshape(FC0, 128, D).transpose(1, 0, 2),
        "w_ada1": a("L1_cond_W_ada").T, "wqkv1": a("L1_cond_Wqkv").T,
        "wout": a("L1_cond_Wout").T.reshape(HP, 128, D).transpose(1, 0, 2),
        "fc1": a("L1_cond_fc1s").transpose(2, 0, 1),
        "fc2": a("L1_cond_fc2s").reshape(E, D, DC, 128).transpose(3, 0, 2, 1),
        "b2s": a("L1_cond_b2s").reshape(1, E * D),
    }
    arrays = {n: np.ascontiguousarray(v) for n, v in arrays.items()}

    nc = bacc.Bacc("TRN2", target_bir_lowering=False, num_devices=1)
    args = [nc.dram_tensor("in_" + n, v.shape, mybir.dt.from_np(v.dtype), kind="ExternalInput").ap()
            for n, v in arrays.items()]
    out = nc.dram_tensor("out", (B, N, D), mybir.dt.float32, kind="ExternalOutput").ap()
    rows = nc.dram_tensor("rows", (B * N, ROW), mybir.dt.float32).ap()
    cond_seq_kernel(nc, *args, out, rows)
    r = run_bass_kernel_spmd(nc, [{"in_" + n: v for n, v in arrays.items()}], core_ids=[0])
    return r.results[0]["out"]
```

```python
from contextlib import ExitStack

import numpy as np

import concourse.bass as bass
from concourse import mybir

B, N, D = 16, 128, 128
H0, HD0 = 16, 8
F0, FC0 = 512, 4
H1, HD1 = 16, 64
HP = H1 // 2
E, DD, DC = 8, 512, 4
CAP = B * N // E
HALVES = CAP // 128
GH = 4
NG = H0 // GH
ROW = D + E
EPS = 1e-5
GATE_BITS = 30
DIGIT = 3
ROUNDS = GATE_BITS // DIGIT
UPPER_ROUNDS = (GATE_BITS - 16) // DIGIT
NCAND = 2 ** DIGIT - 1

_WIDTHS = [("ident", 128), ("headmask", H0), ("same", 128), ("before", 128), ("emask", E),
           ("slots", CAP), ("base", 1), ("slotid", HALVES), ("unit", ROUNDS)]
COLS, _at = {}, 0
for _n, _w in _WIDTHS:
    COLS[_n] = (_at, _at + _w)
    _at += _w
CONST_W = _at

_PW = [("b_ada", 6), ("bq", 1), ("bk", 1), ("bv", 1), ("bo", 1), ("b1", FC0), ("b2", 1), ("b_ada1", 1),
       ("ln1_g", 1), ("ln1_b", 1), ("qn_g", 1), ("qn_b", 1), ("kn_g", 1), ("kn_b", 1), ("mlp_g", 1),
       ("mlp_b", 1), ("b1s", E * DC), ("cT", B), ("wgate", E)]
PCOLS, _at = {}, 0
for _n, _w in _PW:
    PCOLS[_n] = (_at, _at + _w)
    _at += _w
PARAM_W = _at


def cond_seq_kernel(nc, x, const, bits, param, w_ada, wqkv0, wo, w1, w2, w_ada1, wqkv1, wout,
                    fc1, fc2, b2s, out, rows):
    f32, bf16, i32 = mybir.dt.float32, mybir.dt.bfloat16, mybir.dt.int32
    f32r = mybir.dt.float32r
    ALU, ACT, AX = mybir.AluOpType, mybir.ActivationFunctionType, mybir.AxisListType

    ctx = ExitStack()
    with ctx:
        def sb(name, shape, dt=f32):
            return ctx.enter_context(nc.sbuf_tensor(name, shape, dt))

        def sem(name):
            return ctx.enter_context(nc.semaphore(name))

        K = sb("K", [128, CONST_W])
        P = sb("P", [128, PARAM_W])
        BITS = sb("BITS", [128, (ROUNDS + 1) * NCAND], i32)
        sameb = sb("sameb", [128, 128], bf16)
        identb = sb("identb", [128, 128], bf16)
        onesb = sb("onesb", [128, 128], bf16)
        Wada = sb("Wada", [128, 6 * D])
        Wqkv0 = sb("Wqkv0", [128, 3 * D])
        Wo = sb("Wo", [128, D])
        W1 = sb("W1", [128, F0])
        W2 = sb("W2", [128, FC0, D])
        Wada1 = sb("Wada1", [128, D])
        WqkvR = sb("WqkvR", [128, 3 * H1 * HD1], f32r)
        WqkvL = sb("WqkvL", [128, 3 * H1 * HD1], f32r)
        Wout = sb("Wout", [128, HP, D])
        FC1 = sb("FC1", [128, E, DD])
        Wqkv1 = FC1[:, :, :].rearrange("p e h -> p (e h)")[:, 0:3 * H1 * HD1]
        FC2 = sb("FC2", [128, E, DC, D])
        B2S = sb("B2S", [128, E * D])
        mhalf = sb("mhalf", [128, 16])
        epsT = sb("epsT", [128, 16])
        tick = sb("tick", [1, 1])
        zero = sb("zero", [128, 128])

        def k(name):
            return K[:, COLS[name][0]:COLS[name][1]]

        def p(name, j=None):
            a, z = PCOLS[name]
            return P[:, a:z] if j is None else P[:, a + j:a + j + 1]

        ident = k("ident")

        def hi(ap):
            return ap.bitcast(bf16).rearrange("p (n two) -> p n two", two=2)[:, :, 1]

        X = sb("X", [128, B, D])
        adaT = sb("adaT", [128, 6, B])
        sT = sb("sT", [128, B])
        sT2 = sb("sT2", [128, B])
        shT = sb("shT", [128, B])
        st = sb("st", [128, 1, 6])
        mv = sb("mv", [128, 1, 2])
        veps = sb("veps", [128, 1])
        rstd = sb("rstd", [128, 1])
        xn = sb("xn", [128, D])
        hT = sb("hT", [128, 128])
        mneg = sb("mneg", [128, H0], bf16)
        EX = sb("EX", [128, H0, 128])

        qT = sb("qT", [128, 128])
        kT = sb("kT", [128, 128])
        kb = sb("kb", [128, 128], bf16)
        Qm = sb("Qm", [128, H0, 128])
        Vp = sb("Vp", [128, H0, 32])
        oTs = sb("oTs", [128, 4 * 128])
        rec0 = sb("rec0", [128, H0])
        o0 = sb("o0", [128, H0, HD0])
        o0T = sb("o0T", [128, 128])
        aT = sb("aT", [128, 128])

        diag = Qm[:, 0:H1 // 2, :].rearrange("p h n -> p (h n)").bitcast(bf16).rearrange("p (h n) -> p h n", n=128)

        stF = sb("stF", [128, 4, 6])
        mvF = sb("mvF", [128, 4, 2])
        vepsF = sb("vepsF", [128, 4])
        rstdF = sb("rstdF", [128, 4])
        xnB = sb("xnB", [128, 2, 4, D])
        hB = sb("hB", [128, 2, 512])
        gB = sb("gB", [128, FC0, 512])
        fB = sb("fB", [128, 512])

        sq = sb("sq", [128, 2, 512])
        ss = sb("ss", [128, 4, 8])
        sse = sb("sse", [128, 4, 8])
        rq = sb("rq", [128, 4, 8])
        qr = sb("qr", [128, 4, 512])
        h2 = sb("h2", [128, 2, 128], f32r)
        hv = sb("hv", [128, 2, 128], f32r)
        qn = sb("qn", [128, 4, 512])
        QT = sb("QT", [128, HP, 128])
        KT = sb("KT", [128, HP, 128])
        Va = sb("Va", [128, H1, HD1 + 1])
        rec1 = sb("rec1", [128, H1])
        o1 = sb("o1", [128, H1, HD1])
        o1T = sb("o1T", [128, HP, 128])
        x3 = sb("x3", [128, D])
        x3T = sb("x3T", [128, 128])
        G = sb("G", [128, B, E])
        R = sb("R", [128, B, ROW])
        st3 = sb("st3", [128, 6])
        mv3 = sb("mv3", [128, 2])
        ve3 = sb("ve3", [128, 1])
        rs3 = sb("rs3", [128, 1])
        wmean = sb("wmean", [128, 2 * H1])

        gm = sb("gm", [128, B])
        gs = sb("gs", [128, B])
        gr = sb("gr", [128, B])
        GP = sb("GP", [128, B, E])
        GT = sb("GT", [128, 128])
        cnt = sb("cnt", [128, NCAND], bf16)
        cand = sb("cand", [128, NCAND], i32)
        sat = sb("sat", [128, NCAND])
        nsat = sb("nsat", [128, 1])
        digit = sb("digit", [128, 1], i32)
        found = sb("found", [128, 1], i32)
        base = sb("base", [128, NCAND], i32)
        GTh = sb("GTh", [128, 128], bf16)
        ge = sb("ge", [128, NCAND, 128], bf16)
        gtm = sb("gtm", [128, 128])
        ngt = sb("ngt", [128, 1])
        eqm = sb("eqm", [128, 128])
        neq = sb("neq", [128, 1])
        eqs = sb("eqs", [128, 128])
        lim = sb("lim", [128, 2])
        eqt = sb("eqt", [128, 128])
        CC = sb("CC", [128, 130])
        hiS = sb("hiS", [128, 1])
        inA = sb("inA", [128, CAP])
        inC = sb("inC", [128, CAP], bf16)
        CE = sb("CE", [128, E, 130], bf16)
        rr = sb("rr", [128, HALVES, E])
        le = sb("le", [128, E, 128])
        nle = sb("nle", [128, HALVES, E])
        idx = sb("idx", [128, HALVES, E], i32)
        GX = sb("GX", [128, E, HALVES, ROW])
        gT = sb("gT", [128, 2, CAP])
        yh = gB[:, :, :].rearrange("p c n -> p (c n)").rearrange("p (e c n) -> p e c n", e=2, n=CAP)
        Y = EX[:, :, :].rearrange("p (e h) d -> p e h d", h=HALVES)

        PS = ctx.enter_context(nc.psum_tensor("PS", [128, 8, 512], f32))

        def bank(i):
            return PS[:, i, :]

        ld_c, ld_x0, ld_x, ld_w0, ld_w1, ld_w2, ld_wE = (sem(f"ld_{n}") for n in
                                                                ("const", "x0", "x", "w0", "w1", "w2", "wE"))
        names = """pre_const pre_sel pre_ada pre_adab pre_e pre_e1 pre_r pre_s pre_sh pre_shb pre_wc pre_wcs pre_wr pre_wl
        pre_vpad
        a_st a_mv a_ve a_rs a_xn a_xT a_hT a_qk a_vp a_qT a_kb a_kT a_v a_qm a_s a_m a_sT a_e a_pv a_oT
        a_ot a_rec a_o a_oo a_o2 a_wo a_aT a_xo a_x1
        b_st b_mv b_ve b_rs b_xn b_xT b_hT b_f1 b_g b_f2 b_f b_fT b_x2
        c_st c_mv c_ve c_rs c_xn c_xT c_hr c_hf c_hT c_qk c_qr c_sq c_hv c_ss c_sse c_rq c_qn c_T c_qkT c_vp c_v c_s c_m c_dg
        c_sT c_e c_pv c_rec c_o c_oT c_oTs c_wo c_x3 c_xs c_st3 c_mv3 c_ve3 c_rs3 c_xg c_x3T c_x3Ts c_g c_gs
        d_gm d_gsub d_ge d_gs d_gr d_gp d_gpr d_T d_GT d_same d_cand d_cnt d_sum d_nsat d_digit d_found d_masks d_sums d_scan d_lim d_eqt
        d_C d_off d_offs d_hi d_inA d_inC d_CE d_row d_rr d_le d_nle d_xout d_rows
        e_gx e_T e_gT e_f1 e_g e_f2 e_yb e_y e_out""".split()
        S = {n: sem(n) for n in names if n != "e_gx"}
        S["e_gx"] = [sem(f"e_gx{e}") for e in range(E)]
        (pre_const, pre_sel, pre_ada, pre_adab, pre_e, pre_e1, pre_r, pre_s, pre_sh, pre_shb, pre_wc,
         pre_wcs, pre_wr, pre_wl, pre_vpad) = (S[n] for n in names[:15])

        def later(i):
            return not isinstance(i, int) or i > 0

        def later_than(i, n):
            return not isinstance(i, int) or i > n

        PARTS = ((0, 3), (3, 6), (6, E))
        PIECES = (4, 5, 0, 1, 2, 3)
        SB = (0, 2)

        block = ctx.enter_context(nc.Block())

        @block.sync
        def _(sp):
            xt = x.rearrange("b p d -> p b d")
            sp.dma_start(X[:, 0:2, :], xt[:, 0:2, :]).then_inc(ld_x0, 16)
            sp.dma_start(P[:, :], param).then_inc(ld_c, 16)
            sp.dma_start(Wada[:, :], w_ada).then_inc(ld_c, 16)
            sp.dma_start(K[:, :], const).then_inc(ld_c, 16)
            sp.dma_start(Wada1[:, :], w_ada1).then_inc(ld_c, 16)
            sp.dma_start(BITS[:, :], bits).then_inc(ld_c, 16)
            sp.dma_start(X[:, 2:B, :], xt[:, 2:B, :]).then_inc(ld_x, 16)
            sp.dma_start(Wqkv0[:, :], wqkv0).then_inc(ld_w0, 16)
            sp.dma_start(Wo[:, :], wo).then_inc(ld_w0, 16)
            sp.dma_start(Wqkv1, wqkv1).then_inc(ld_w1, 16)
            sp.dma_start(W1[:, :], w1).then_inc(ld_w2, 16)
            sp.dma_start(W2[:, :, :], w2).then_inc(ld_w2, 16)
            sp.dma_start(Wout[:, :, :], wout).then_inc(ld_w2, 16)
            sp.dma_start(B2S[:, :], b2s).then_inc(ld_w2, 16)
            sp.dma_start(FC2[:, :, :, :], fc2).then_inc(ld_wE, 16)
            sp.wait_ge(pre_wl, 6)
            sp.dma_start(FC1[:, :, :], fc1).then_inc(ld_wE, 16)
            sp.wait_ge(S["c_xs"], B)
            sp.dma_start(out.rearrange("b p d -> p b d"), X[:, :, :]).then_inc(S["d_xout"], 16)
            sp.wait_ge(S["d_gpr"], 1)
            sp.dma_start(rows.rearrange("(b p) w -> p b w", p=128), R[:, :, :]).then_inc(S["d_rows"], 16)
            sp.wait_ge(S["d_xout"], 16)
            sp.wait_ge(S["d_rows"], 16)

        @block.tensor
        def _(pe):
            pe.wait_ge(ld_c, 80)
            for j in range(6):
                mm = nc.tensor.matmul(PS[:, 0, j * B:(j + 1) * B], Wada[:, j * D:(j + 1) * D], p("cT"),
                                      start=True, stop=True)
            mm.then_inc(pre_ada, 1)
            pe.wait_ge(pre_s, 1)
            nc.tensor.matmul(PS[:, 1, 0:B], Wada1[:, :], sT[:, :], start=True, stop=True).then_inc(pre_sh, 1)
            pe.wait_ge(ld_w0, 32)
            pe.wait_ge(pre_sel, 1)
            pe.wait_ge(pre_adab, 2)
            pe.wait_ge(pre_shb, 1)

            def transposed(o, i):
                return nc.tensor.transpose(o, i, ident)

            def max_rows(h):
                return mneg[:, h:h + 1].to_broadcast([128, 128])

            def scoresT0(b, g):
                pe.wait_ge(S["a_m"], b * NG + g + 1)
                if g == 0:
                    pe.wait_ge(S["a_kT"], b * 1 + 1)
                if later(b) or g >= 2:
                    pe.wait_ge(S["a_e"], b * NG + g - 1)
                for h in range(GH):
                    nc.tensor.matmul(PS[:, g % 2, 128 * h:128 * h + 128], max_rows(GH * g + h), identb[:, :],
                                     start=(h == 0), stop=False, skip_group_check=True)
                mm = nc.tensor.matmul(bank(g % 2), kT[:, :], Qm[:, GH * g:GH * g + GH, :], start=False, stop=True,
                                      skip_group_check=True)
                mm.then_inc(S["a_sT"], 1)

            def values0(b, g):
                pe.wait_ge(S["a_e"], b * NG + g + 1)
                if g == 0:
                    pe.wait_ge(S["a_v"], b * 1 + 1)
                    if later(b):
                        pe.wait_ge(S["a_oT"], b * 1)
                for h in range(GH):
                    mm = nc.tensor.matmul(PS[32 * h:32 * h + 32, 4, 128 * g:128 * g + 128],
                                          Vp[:, GH * g + h, :], EX[:, GH * g + h, :], start=True, stop=True,
                                          tile_position=(0, 32 * h))
                mm.then_inc(S["a_pv"], 1)

            def scores0(n, g):
                if g == 0:
                    pe.wait_ge(S["a_kb"], n * 1 + 1)
                pe.wait_ge(S["a_qm"], n * NG + g + 1)
                if later(n) or g >= 2:
                    pe.wait_ge(S["a_m"], n * NG + g - 1)
                for h in range(GH):
                    mm = nc.tensor.matmul(PS[:, 2 + g % 2, 128 * h:128 * h + 128], hi(Qm[:, GH * g + h, :]),
                                          kb[:, :], start=True, stop=True)
                mm.then_inc(S["a_s"], 1)

            def values_back(t):
                pe.wait_ge(S["a_oT"], t * 1 + 1)
                if later(t):
                    pe.wait_ge(S["a_x1"], t * 1)
                for g in range(NG):
                    mm = transposed(PS[:, 7, 128 * g:128 * g + 128], oTs[:, 128 * g:128 * g + 128])
                mm.then_inc(S["a_ot"], 1)

            def turn_o0(t):
                pe.wait_ge(S["a_o"], t * 1 + 1)
                transposed(PS[:, 7, 0:128], o0[:, :, :].rearrange("p h d -> p (h d)")).then_inc(S["a_oo"], 1)

            def project_o0(t):
                pe.wait_ge(S["a_o2"], t * 1 + 1)
                nc.tensor.matmul(PS[:, 7, 128:256], Wo[:, :], o0T[:, :], start=True, stop=True)\
                    .then_inc(S["a_wo"], 1)

            def turn_a0(t):
                pe.wait_ge(S["a_aT"], t * 1 + 1)
                transposed(PS[:, 7, 0:128], aT[:, :]).then_inc(S["a_xo"], 1)

            def turn_x0(n):
                pe.wait_ge(S["a_xn"], n * 1 + 1)
                if later(n):
                    pe.wait_ge(S["a_hT"], n * 1)
                transposed(PS[:, 6, 0:128], xn[:, :]).then_inc(S["a_xT"], 1)

            def project_qk0(n):
                pe.wait_ge(S["a_hT"], n * 1 + 1)
                if later(n):
                    pe.wait_ge(S["a_v"], n * 1)
                nc.tensor.matmul(PS[:, 5, 0:128], Wqkv0[:, 0:128], hT[:, :], start=True, stop=True)
                nc.tensor.matmul(PS[:, 5, 128:256], Wqkv0[:, 128:256], hT[:, :], start=True, stop=True)\
                    .then_inc(S["a_qk"], 1)

            def project_v0(n):
                pe.wait_ge(S["a_kT"], n * 1 + 1)
                nc.tensor.matmul(PS[:, 5, 256:384], hT[:, :], Wqkv0[:, 256:384], start=True, stop=True)\
                    .then_inc(S["a_vp"], 1)

            def step0(b, ln, front, attn, tail):
                n, t = b + 1, b - 1
                if attn:
                    scoresT0(b, 0)
                if front:
                    turn_x0(n)
                if attn:
                    scoresT0(b, 1)
                if front:
                    project_qk0(n)
                if tail:
                    values_back(t)
                if attn:
                    values0(b, 0)
                    scoresT0(b, 2)
                if tail:
                    turn_o0(t)
                if front:
                    scores0(n, 0)
                if attn:
                    values0(b, 1)
                if tail:
                    project_o0(t)
                if attn:
                    scoresT0(b, 3)
                if front:
                    scores0(n, 1)
                if tail:
                    turn_a0(t)
                if front:
                    scores0(n, 2)
                if attn:
                    values0(b, 2)
                    values0(b, 3)
                if front:
                    project_v0(n)
                    scores0(n, 3)

            step0(-2, True, False, False, False)
            step0(-1, True, True, False, False)
            step0(0, True, True, True, False)
            step0(1, True, True, True, True)
            with pe.Fori(2, B - 2) as b:
                step0(b, True, True, True, True)
            step0(B - 2, False, True, True, True)

            NB = B // 4

            def front_ff(n):
                pe.wait_ge(S["b_xn"], n + 1)
                if n:
                    pe.wait_ge(S["b_hT"], n)
                for j in range(4):
                    mm = transposed(PS[:, 6, 128 * j:128 * j + 128], xnB[:, n % 2, j, :])
                mm.then_inc(S["b_xT"], 1)

            def hidden_ff(n, c):
                pe.wait_ge(S["b_hT"], n + 1)
                if FC0 * n + c >= 2:
                    pe.wait_ge(S["b_g"], FC0 * n + c - 1)
                nc.tensor.matmul(bank((2, 5)[c % 2]), W1[:, 128 * c:128 * c + 128], hB[:, n % 2, :], start=True,
                                 stop=True).then_inc(S["b_f1"], 1)

            def out_ff(n, c):
                pe.wait_ge(S["b_g"], FC0 * n + c + 1)
                if n and c == 0:
                    pe.wait_ge(S["b_f"], n)
                nc.tensor.matmul(bank(0), W2[:, c, :], gB[:, c, :], start=(c == 0), stop=(c == FC0 - 1))\
                    .then_inc(S["b_f2"], 1)

            def tail_ff(n):
                pe.wait_ge(S["b_f"], n + 1)
                if n:
                    pe.wait_ge(S["b_x2"], n)
                for j in range(4):
                    mm = transposed(PS[:, 1, 128 * j:128 * j + 128], fB[:, 128 * j:128 * j + 128])
                mm.then_inc(S["b_fT"], 1)

            pe.wait_ge(S["a_v"], B)
            front_ff(0)
            step0(B - 1, False, False, True, True)
            pe.wait_ge(ld_w2, 64)
            hidden_ff(0, 0)
            values_back(B - 1)
            hidden_ff(0, 1)
            turn_o0(B - 1)
            front_ff(1)
            project_o0(B - 1)
            hidden_ff(0, 2)
            turn_a0(B - 1)
            hidden_ff(0, 3)
            for n in range(1, NB - 1):
                for c in range(FC0):
                    out_ff(n - 1, c)
                    hidden_ff(n, c)
                front_ff(n + 1)
                tail_ff(n - 1)

            def turn_x1(m):
                pe.wait_ge(S["c_xn"], m * 1 + 1)
                if later_than(m, 1):
                    pe.wait_ge(S["c_v"], m * 2 - 2)
                elif m:
                    pe.wait_ge(S["c_sq"], m * 4)
                transposed(PS[:, 3, 0:128], xn[:, :]).then_inc(S["c_xT"], 1)

            def head1(g, i):
                return 8 * (g // 2) + 2 * i + g % 2

            def rows64(h):
                return slice(64 * (h % 2), 64 * (h % 2) + 64)

            def scoresT1(b, g):
                pe.wait_ge(S["c_m"], b * NG + max(g + 1, 3))
                if later(b) or g >= 2:
                    pe.wait_ge(S["c_e"], b * NG + g - 1)
                for i in range(GH):
                    h = head1(g, i)
                    nc.tensor.matmul(PS[:, g % 2, 128 * i:128 * i + 128], KT[rows64(h), h // 2, :],
                                     QT[rows64(h), h // 2, :], start=(i == 0), stop=False, skip_group_check=True)
                pe.wait_ge(S["c_dg"], b * NG + g + 1)
                mm = nc.tensor.matmul(bank(g % 2), onesb[:, :], diag[:, GH * g:GH * g + GH, :], start=False, stop=True,
                                      skip_group_check=True)
                mm.then_inc(S["c_sT"], 1)

            def values1(b, g):
                pe.wait_ge(S["c_e"], b * NG + g + 1)
                if g == 0:
                    pe.wait_ge(S["c_v"], b * 2 + 2)
                if later(b) or g >= 2:
                    pe.wait_ge(S["c_o"], b * NG + g - 1)
                w = HD1 + 1
                for i in range(GH):
                    mm = nc.tensor.matmul(PS[:, 5 + g % 2, w * i:w * i + w], EX[:, GH * g + i, :],
                                          Va[:, head1(g, i), :], start=True, stop=True)
                mm.then_inc(S["c_pv"], 1)

            def split_product(o, h, at, lower=None):
                w = slice(at, at + 512)
                nc.tensor.matmul(o, h[:, 0, :], WqkvR[:, w], start=True, stop=False)
                nc.tensor.matmul(o, h[:, 0, :], WqkvL[:, w], start=False, stop=False)
                if lower is not None:
                    pe.wait_ge(*lower)
                return nc.tensor.matmul(o, h[:, 1, :], WqkvR[:, w], start=False, stop=True)

            def project1(n, j):
                if j == 0:
                    pe.wait_ge(S["c_hr"], n * 1 + 1)
                    if later_than(n, 1):
                        pe.wait_ge(S["c_v"], n * 2 - 3)
                    elif n:
                        pe.wait_ge(S["c_sq"], n * 4)
                elif j > 1:
                    pe.wait_ge(S["c_sq"], n * 4 + j - 1)
                split_product(bank(4 - j % 2), h2, 512 * j, (S["c_hT"], n * 1 + 1) if j == 0 else None)\
                    .then_inc(S["c_qk"], 1)

            def turn1(n, j, front1):
                pe.wait_ge(S["c_qn"], n * 4 + j + 1)
                if j < 2:
                    if front1:
                        pe.wait_ge(S["c_sq"], n * 4 + 7 + j)
                else:
                    pe.wait_ge(S["c_qkT"], n * 4 + j - 1)
                for i in range(4):
                    mm = transposed(PS[:, 4 - j % 2, 128 * i:128 * i + 128], qn[:, j, 128 * i:128 * i + 128])
                mm.then_inc(S["c_T"], 1)

            def value_proj1(n, j):
                pe.wait_ge(S["c_qkT"], n * 4 + j + 3)
                if j == 0:
                    pe.wait_ge(S["c_hv"], n * 1 + 1)
                split_product(bank(4 - j), hv, 2 * H1 * HD1 + 512 * j).then_inc(S["c_vp"], 1)

            def scores1(n, g):
                if g >= 2:
                    pe.wait_ge(S["c_m"], n * NG + g - 1)
                elif later(n):
                    if g == 0:
                        pe.wait_ge(S["c_e"], n * NG - 1)
                    else:
                        pe.wait_ge(S["c_m"], n * NG)
                pe.wait_ge(S["c_qkT"], n * 4 + 3 + g // 2)
                for i in range(GH):
                    h = head1(g, i)
                    mm = nc.tensor.matmul(PS[:, SB[g % 2], 128 * i:128 * i + 128], hi(QT[rows64(h), h // 2, :]),
                                          hi(KT[rows64(h), h // 2, :]), start=True, stop=True)
                mm.then_inc(S["c_s"], 1)

            def turn_o1(t, j, at):
                pe.wait_ge(S["c_o"], t * NG + 2 * (j + 1))
                if j:
                    pe.wait_ge(S["c_oTs"], t * 2 + 1)
                elif at == 3:
                    pe.wait_ge(S["c_v"], B * 2)
                elif later(t):
                    pe.wait_ge(S["c_gs"], t * 1)
                for i in range(4):
                    h = 8 * j + 2 * i
                    mm = transposed(PS[:, at, 128 * i:128 * i + 128],
                                    o1[:, h:h + 2, :].rearrange("p h d -> p (h d)"))
                mm.then_inc(S["c_oT"], 1)

            def project_o1(t, j, at):
                pe.wait_ge(S["c_oTs"], t * 2 + (j + 1 if at == 4 else 2))
                for i in range(4 * j, 4 * j + 4):
                    mm = nc.tensor.matmul(PS[:, at, 0:128], o1T[:, i, :], Wout[:, i, :], start=(i == 0),
                                          stop=(i == HP - 1))
                if j:
                    mm.then_inc(S["c_wo"], 1)

            def step1(b, front1, front2, attn, tail):
                m, n, t = b + 2, b + 1, b - 1
                if tail and attn:
                    turn_o1(t, 0, 7)
                if attn:
                    scoresT1(b, 0)
                    scoresT1(b, 1)
                if tail and attn:
                    turn_o1(t, 1, 7)
                elif tail:
                    project_o1(t, 0, 4)
                    turn_o1(t, 1, 3)
                if attn:
                    scoresT1(b, 2)
                if front1:
                    turn_x1(m)
                if attn:
                    values1(b, 0)
                    values1(b, 1)
                if front1:
                    project1(m, 0)
                    project1(m, 1)
                if tail and attn:
                    project_o1(t, 0, 7)
                    project_o1(t, 1, 7)
                elif tail:
                    project_o1(t, 1, 4)
                if front1:
                    project1(m, 2)
                if attn:
                    scoresT1(b, 3)
                if front1:
                    project1(m, 3)
                if front2:
                    turn1(n, 0, front1)
                if attn:
                    values1(b, 2)
                if tail:
                    pe.wait_ge(S["c_x3"], t * 1 + 1)
                    transposed(PS[:, 7, 128:256], x3[:, :]).then_inc(S["c_x3T"], 1)
                if front2:
                    turn1(n, 1, front1)
                    turn1(n, 2, front1)
                if not (front1 or front2) and attn:
                    turn_o1(b, 0, 3)
                if attn:
                    values1(b, 3)
                if front2:
                    turn1(n, 3, front1)
                    scores1(n, 0)
                    scores1(n, 1)
                    value_proj1(n, 0)
                    scores1(n, 2)
                if tail:
                    pe.wait_ge(S["c_x3Ts"], t * 1 + 1)
                    nc.tensor.matmul(PS[:, 7, 256:256 + E], x3T[:, :], p("wgate"), start=True, stop=True)\
                        .then_inc(S["c_g"], 1)
                if front2:
                    value_proj1(n, 1)
                    scores1(n, 3)

            turn_x1(0)
            for c in range(FC0):
                out_ff(NB - 2, c)
                hidden_ff(NB - 1, c)
                pe.wait_ge(pre_wl, c + 3)
                project1(0, c)
            tail_ff(NB - 2)
            turn_x1(1)
            for c in range(FC0):
                out_ff(NB - 1, c)
                project1(1, c)
            for j in range(4):
                turn1(0, j, True)
            tail_ff(NB - 1)
            scores1(0, 0)
            scores1(0, 1)
            value_proj1(0, 0)
            scores1(0, 2)
            scores1(0, 3)
            value_proj1(0, 1)
            pe.wait_ge(S["b_x2"], NB)
            step1(0, True, True, True, False)
            step1(1, True, True, True, True)
            with pe.Fori(2, B - 2) as b:
                step1(b, True, True, True, True)
            step1(B - 2, False, True, True, True)
            step1(B - 1, False, False, True, True)
            step1(B, False, False, False, True)

            pe.wait_ge(S["d_gp"], 1)
            transposed(PS[:, 0, 0:128], GP[:, :, :].rearrange("p b e -> p (b e)")).then_inc(S["d_T"], 1)
            pe.wait_ge(S["d_same"], 1)
            for i in range(ROUNDS):
                pe.wait_ge(S["d_cnt"], i + 1)
                nc.tensor.matmul(PS[:, 1, 0:NCAND], sameb[:, :], cnt[:, :], start=True, stop=True)\
                    .then_inc(S["d_sum"], 1)
            pe.wait_ge(S["d_masks"], 2)
            nc.tensor.matmul(PS[:, 0, 0:1], k("same"), ngt[:, :], start=True, stop=True)
            nc.tensor.matmul(PS[:, 0, 1:2], k("before"), neq[:, :], start=True, stop=True).then_inc(S["d_sums"], 1)
            pe.wait_ge(S["d_C"], 1)
            nc.tensor.matmul(PS[:, 2, 0:1], k("before"), CC[:, 127:128], start=True, stop=True)\
                .then_inc(S["d_off"], 1)
            pe.wait_ge(S["d_CE"], 1)
            pe.wait_ge(S["d_inC"], 1)
            for j, (a, z) in enumerate(PARTS):
                for h in range(HALVES):
                    nc.tensor.matmul(PS[:, 2 + 3 * h + j, 0:130 * (z - a)], inC[:, 128 * h:128 * h + 128],
                                     CE[:, a:z, :].rearrange("p e w -> p (e w)"), start=True, stop=True)\
                        .then_inc(S["d_row"], 1)

            pe.wait_ge(ld_wE, 32)

            def turn_e(e):
                pe.wait_ge(S["e_gx"][e], 32)
                if e:
                    pe.wait_ge(S["e_gT"], e)
                for h in range(HALVES):
                    mm = transposed(PS[:, 0, 128 * h:128 * h + 128], GX[:, e, h, 0:D])
                mm.then_inc(S["e_T"], 1)

            def hidden_e(e):
                if e == 0:
                    pe.wait_ge(S["d_le"], len(PARTS))
                pe.wait_ge(S["e_gT"], e + 1)
                if e >= 2:
                    pe.wait_ge(S["e_g"], DC * (e - 1))
                for c in range(DC):
                    mm = nc.tensor.matmul(PS[:, 1 + 2 * (e % 2) + c // 2, CAP * (c % 2):CAP * (c % 2) + CAP],
                                          FC1[:, e, 128 * c:128 * c + 128], gT[:, e % 2, :], start=True, stop=True)
                    if c % 2:
                        mm.then_inc(S["e_f1"], 1)

            def out_e(e):
                pe.wait_ge(S["e_g"], DC * (e + 1))
                if e >= 2:
                    pe.wait_ge(S["e_yb"], e - 1)
                for h in range(HALVES):
                    o = PS[:, 5 + e % 2, 128 * h:128 * h + 128]
                    for c in range(DC):
                        mm = nc.tensor.matmul(o, yh[:, e % 2, c, 128 * h:128 * h + 128], FC2[:, e, c, :],
                                              start=(c == 0), stop=(c == DC - 1))
                mm.then_inc(S["e_f2"], 1)

            turn_e(0)
            hidden_e(0)
            turn_e(1)
            out_e(0)
            for e in range(1, E):
                hidden_e(e)
                if e + 1 < E:
                    turn_e(e + 1)
                if e > 1:
                    out_e(e - 1)
            out_e(E - 1)

        @block.scalar
        def _(act):
            act.wait_ge(ld_c, 80)
            nc.scalar.activation(sT[:, :], p("cT"), ACT.Exp, scale=-1.0).then_inc(pre_e, 1)

            def step0(b, ln, front, attn, tail):
                n = b + 1

                def exps(g):
                    act.wait_ge(S["a_sT"], b * NG + g + 1)
                    if later(b):
                        act.wait_ge(S["a_pv"], b * NG + g - NG + 1)
                    nc.scalar.activation(EX[:, GH * g:GH * g + GH, :].rearrange("p h n -> p (h n)"),
                                         bank(g % 2), ACT.Exp, scale=float(1.0 / np.sqrt(np.float32(HD0))))\
                        .then_inc(S["a_e"], 1)

                def copy_kT():
                    act.wait_ge(S["a_kb"], n * 1 + 1)
                    if later(n):
                        act.wait_ge(S["a_sT"], n * NG)
                    nc.scalar.activation(kT[:, :], PS[:, 5, 128:256], ACT.Identity, bias=p("bk"))\
                        .then_inc(S["a_kT"], 1)

                def copy_values():
                    act.wait_ge(S["a_pv"], b * NG + NG)
                    if later(b):
                        act.wait_ge(S["a_ot"], b * 1)
                    nc.scalar.activation(oTs[:, :], bank(4), ACT.Copy).then_inc(S["a_oT"], 1)

                def copy_v0():
                    act.wait_ge(S["a_vp"], n * 1 + 1)
                    if not later(n):
                        act.wait_ge(pre_vpad, 1)
                    nc.scalar.activation(Vp[:, :, 0:HD0], PS[:, 5, 256:384].rearrange("p (h d) -> p h d", d=HD0),
                                         ACT.Copy).then_inc(S["a_v"], 1)

                if attn:
                    exps(0)
                    exps(1)
                    exps(2)
                    exps(3)
                if front:
                    copy_kT()
                if attn:
                    copy_values()
                if front:
                    copy_v0()

            step0(-1, True, True, False, False)
            step0(0, True, True, True, False)
            step0(1, True, True, True, True)
            with act.Fori(2, B - 2) as b:
                step0(b, True, True, True, True)
            step0(B - 2, False, True, True, True)
            step0(B - 1, False, False, True, True)

            def gelu(n, c):
                act.wait_ge(S["b_f1"], FC0 * n + c + 1)
                if n:
                    act.wait_ge(S["b_f2"], FC0 * (n - 1) + c + 1)
                nc.scalar.activation(gB[:, c, :], bank((2, 5)[c % 2]), ACT.Gelu, bias=p("b1", c)).then_inc(S["b_g"], 1)

            def squares(m, j):
                act.wait_ge(S["c_qk"], m * 4 + j + 1)
                if later(m):
                    act.wait_ge(S["c_qn"], m * 4 + j - 3)
                nc.scalar.activation(qr[:, j, :], bank(4 - j % 2), ACT.Copy).then_inc(S["c_qr"], 1)
                if later(m) or j >= 2:
                    act.wait_ge(S["c_ss"], m * 4 + j - 1)
                nc.scalar.activation(sq[:, j % 2, :], bank(4 - j % 2), ACT.Square,
                                     scale=1.0 / float(np.sqrt(np.float32(HD1)))).then_inc(S["c_sq"], 1)

            def turned(n, j):
                act.wait_ge(S["c_T"], n * 4 + j + 1)
                if later(n):
                    act.wait_ge(S["c_sT"], n * NG)
                dst = (QT, KT)[j // 2]
                gn = ("qn", "kn")[j // 2]
                nc.scalar.activation(dst[:, 4 * (j % 2):4 * (j % 2) + 4, :].rearrange("p i n -> p (i n)"),
                                     bank(4 - j % 2), ACT.Identity, scale=p(gn + "_g"), bias=p(gn + "_b"))\
                    .then_inc(S["c_qkT"], 1)

            def copy_v(n, j):
                act.wait_ge(S["c_vp"], n * 2 + j + 1)
                if later(n):
                    act.wait_ge(S["c_pv"], n * NG)
                nc.scalar.activation(Va[:, 8 * j:8 * j + 8, 0:HD1],
                                     bank(4 - j).rearrange("p (h d) -> p h d", d=HD1), ACT.Copy)\
                    .then_inc(S["c_v"], 1)

            def step1(b, front1, front2, attn, tail):
                m, n, t = b + 2, b + 1, b - 1

                def exps(g):
                    act.wait_ge(S["c_sT"], b * NG + g + 1)
                    if later(b):
                        act.wait_ge(S["c_pv"], b * NG + g - NG + 1)
                    nc.scalar.activation(EX[:, GH * g:GH * g + GH, :].rearrange("p h n -> p (h n)"),
                                         bank(g % 2), ACT.Exp, scale=float(1.0 / np.sqrt(np.float32(HD1))))\
                        .then_inc(S["c_e"], 1)

                def copy_oT(t, j, at):
                    act.wait_ge(S["c_oT"], t * 2 + j + 1)
                    if later(t) and j == 0:
                        act.wait_ge(S["c_wo"], t * 1)
                    nc.scalar.activation(o1T[:, 4 * j:4 * j + 4, :].rearrange("p i n -> p (i n)"), bank(at), ACT.Copy)\
                        .then_inc(S["c_oTs"], 1)

                if tail and attn:
                    copy_oT(t, 0, 7)
                if attn:
                    exps(0)
                    exps(1)
                if tail:
                    copy_oT(t, 1, 7 if attn else 3)
                if front1:
                    squares(m, 0)
                if attn:
                    exps(2)
                if front1:
                    squares(m, 1)
                    squares(m, 2)
                if attn:
                    exps(3)
                if front1:
                    squares(m, 3)
                if front2:
                    turned(n, 0)
                    turned(n, 1)
                    turned(n, 2)
                    turned(n, 3)
                if tail:
                    act.wait_ge(S["c_x3T"], t * 1 + 1)
                    nc.scalar.activation(x3T[:, :], PS[:, 7, 128:256], ACT.Copy).then_inc(S["c_x3Ts"], 1)
                if front2:
                    copy_v(n, 0)
                    copy_v(n, 1)
                if not (front1 or front2) and attn:
                    copy_oT(b, 0, 3)

            def upper_weights(i):
                j = PIECES[i]
                if j < 4:
                    act.wait_ge(pre_wcs, j + 1)
                nc.scalar.activation(WqkvR[:, 512 * j:512 * j + 512], Wqkv1[:, 512 * j:512 * j + 512], ACT.Copy)\
                    .then_inc(pre_wr, 1)

            gelu(0, 0)
            gelu(0, 1)
            act.wait_ge(ld_w1, 16)
            upper_weights(0)
            upper_weights(1)
            gelu(0, 2)
            upper_weights(2)
            gelu(0, 3)
            upper_weights(3)
            for c in range(FC0):
                gelu(1, c)
                if c < 2:
                    upper_weights(4 + c)
            for c in range(FC0):
                gelu(2, c)
            for c in range(FC0):
                gelu(B // 4 - 1, c)
                squares(0, c)
            for j in range(4):
                squares(1, j)
            for j in range(4):
                turned(0, j)
            copy_v(0, 0)
            copy_v(0, 1)
            step1(0, True, True, True, False)
            step1(1, True, True, True, True)
            with act.Fori(2, B - 2) as b:
                step1(b, True, True, True, True)
            step1(B - 2, False, True, True, True)
            step1(B - 1, False, False, True, True)
            step1(B, False, False, False, True)

            act.wait_ge(S["d_gsub"], 1)
            nc.scalar.activation(GP[:, :, :], G[:, :, :], ACT.Exp).then_inc(S["d_ge"], 1)
            for e in range(E):
                for c in range(DC):
                    act.wait_ge(S["e_f1"], DC // 2 * e + c // 2 + 1)
                    if e >= 2:
                        act.wait_ge(S["e_f2"], e - 1)
                    nc.scalar.activation(yh[:, e % 2, c, :],
                                         PS[:, 1 + 2 * (e % 2) + c // 2, CAP * (c % 2):CAP * (c % 2) + CAP],
                                         ACT.Gelu_apprx_tanh, bias=p("b1s", DC * e + c)).then_inc(S["e_g"], 1)

        @block.vector
        def _(dve):
            V = nc.vector
            V.memset(Vp[:, :, :], 0.0).then_inc(pre_const, 1)
            V.memset(Va[:, :, HD1:HD1 + 1], 1.0)
            V.memset(mhalf[:, :], -0.5)
            V.memset(epsT[:, :], EPS)
            V.memset(onesb[:, :], 1.0)
            V.memset(zero[:, :], 0.0).then_inc(pre_const, 1)
            dve.wait_ge(pre_const, 1)
            V.memset(Vp[:, :, HD0:HD0 + 1], 1.0).then_inc(pre_vpad, 1)
            def stats0(m):
                V.bn_stats(st[:, 0, :], X[:, m, :]).then_inc(S["a_st"], 1)
                dve.wait_ge(S["a_st"], m * 1 + 1)
                if later(m):
                    dve.wait_ge(S["a_ve"], m * 1)
                V.memset(tick[:, :], 0.0)
                V.bn_aggr(mv[:, 0, :], st[:, 0, :]).then_inc(S["a_mv"], 1)

            def norm0(m):
                dve.wait_ge(S["a_rs"], m * 1 + 1)
                dve.wait_ge(S["a_mv"], m * 1 + 1)
                if later(m):
                    dve.wait_ge(S["a_xT"], m * 1)
                V.tensor_scalar(xn[:, :], X[:, m, :], mv[:, 0, 0:1], rstd[:, 0:1], ALU.subtract, ALU.mult)\
                    .then_inc(S["a_xn"], 1)

            def hidden0(n):
                dve.wait_ge(S["a_xT"], n * 1 + 1)
                if later(n):
                    dve.wait_ge(S["a_vp"], n * 1)
                V.tensor_scalar(hT[:, :], PS[:, 6, 0:128], adaT[:, 1, bass.ds(n, 1)],
                                adaT[:, 0, bass.ds(n, 1)], ALU.mult, ALU.add).then_inc(S["a_hT"], 1)

            def copy_qk(n):
                dve.wait_ge(S["a_qk"], n * 1 + 1)
                if later(n):
                    dve.wait_ge(S["a_qm"], n * NG)
                V.tensor_scalar_add(qT[:, :], PS[:, 5, 0:128], p("bq")).then_inc(S["a_qT"], 1)
                if later(n):
                    dve.wait_ge(S["a_s"], n * NG)
                V.tensor_scalar_add(kb[:, :], PS[:, 5, 128:256], p("bk")).then_inc(S["a_kb"], 1)

            def maxima0(n, g):
                if later(n):
                    dve.wait_ge(S["a_sT"], (n - 1) * NG + g + 1)
                dve.wait_ge(S["a_s"], n * NG + g + 1)
                V.tensor_reduce(mneg[:, GH * g:GH * g + GH],
                                bank(2 + g % 2).rearrange("p (h k) -> p h k", h=GH), AX.X, ALU.max,
                                negate=True).then_inc(S["a_m"], 1)

            def scale_o0(t):
                dve.wait_ge(S["a_ot"], t * 1 + 1)
                ot = bank(7).rearrange("p (h w) -> p h w", w=32)
                V.reciprocal(rec0[:, :], ot[:, :, HD0]).then_inc(S["a_rec"], 1)
                dve.wait_ge(S["a_rec"], t * 1 + 1)
                V.tensor_tensor(o0[:, :, :], ot[:, :, 0:HD0],
                                rec0[:, :].unsqueeze(2).to_broadcast([128, H0, HD0]), ALU.mult)\
                    .then_inc(S["a_o"], 1)

            def bias_o0(t):
                dve.wait_ge(S["a_oo"], t * 1 + 1)
                V.tensor_scalar_add(o0T[:, :], PS[:, 7, 0:128], p("bv")).then_inc(S["a_o2"], 1)

            def gate_o0(t):
                dve.wait_ge(S["a_wo"], t * 1 + 1)
                V.tensor_scalar(aT[:, :], PS[:, 7, 128:256], p("bo"), adaT[:, 2, bass.ds(t, 1)],
                                ALU.add, ALU.mult).then_inc(S["a_aT"], 1)

            def add_o0(t):
                dve.wait_ge(S["a_xo"], t * 1 + 1)
                xt = X[:, t, :]
                V.tensor_tensor(xt, PS[:, 7, 0:128], xt, ALU.add).then_inc(S["a_x1"], 1)

            def step0(b, ln, front, attn, tail):
                m, n, t = b + 2, b + 1, b - 1
                if front:
                    hidden0(n)
                    copy_qk(n)
                if tail:
                    scale_o0(t)
                if ln:
                    stats0(m)
                if tail:
                    bias_o0(t)
                    gate_o0(t)
                if front:
                    maxima0(n, 0)
                    maxima0(n, 1)
                    maxima0(n, 2)
                if tail:
                    add_o0(t)
                if ln:
                    norm0(m)
                if front:
                    maxima0(n, 3)

            dve.wait_ge(ld_x0, 16)
            step0(-2, True, False, False, False)

            dve.wait_ge(pre_ada, 1)
            V.tensor_tensor(adaT[:, :, :], PS[:, 0, 0:6 * B].rearrange("p (j b) -> p j b", b=B),
                            p("b_ada").unsqueeze(2).to_broadcast([128, 6, B]), ALU.add).then_inc(pre_adab, 1)
            dve.wait_ge(pre_adab, 1)
            sc = adaT[:, :, :].rearrange("p (t j) b -> p t j b", t=2)[:, :, 1, :]
            V.tensor_scalar_add(sc, sc, 1.0).then_inc(pre_adab, 1)
            dve.wait_ge(pre_e, 1)
            V.tensor_scalar_add(sT2[:, :], sT[:, :], 1.0).then_inc(pre_e1, 1)
            dve.wait_ge(pre_e1, 1)
            V.reciprocal(sT2[:, :], sT2[:, :]).then_inc(pre_r, 1)
            dve.wait_ge(pre_r, 1)
            V.tensor_tensor(sT[:, :], p("cT"), sT2[:, :], ALU.mult).then_inc(pre_s, 1)
            dve.wait_ge(pre_sh, 1)
            V.tensor_scalar(shT[:, :], PS[:, 1, 0:B], p("b_ada1"), p("ln1_b"), ALU.add, ALU.add)\
                .then_inc(pre_shb, 1)
            dve.wait_ge(pre_shb, 1)
            dve.wait_ge(pre_adab, 2)
            V.tensor_copy(identb[:, :], ident).then_inc(pre_sel, 1)
            dve.wait_ge(pre_adab, 2)

            step0(-1, True, True, False, False)
            dve.wait_ge(ld_x, 16)
            step0(0, True, True, True, False)
            step0(1, True, True, True, True)

            def weight_sums(i):
                V.tensor_reduce(wmean[:, H1 * i:H1 * i + H1],
                                Wqkv1[:, H1 * HD1 * i:H1 * HD1 * (i + 1)].rearrange("p (h d) -> p h d", d=HD1),
                                AX.X, ALU.add).then_inc(pre_wc, 1)

            dve.wait_ge(ld_w1, 16)
            weight_sums(0)
            with dve.Fori(2, B - 3) as b:
                step0(b, True, True, True, True)

            NB = B // 4

            def stats_ff(n):
                dve.wait_ge(S["a_x1"], 4 * n + 4)
                for j in range(4):
                    ins = V.bn_stats(stF[:, j, :], X[:, 4 * n + j, :])
                ins.then_inc(S["b_st"], 1)
                dve.wait_ge(S["b_st"], n + 1)
                if n:
                    dve.wait_ge(S["b_ve"], n)
                for j in range(4):
                    ins = V.bn_aggr(mvF[:, j, :], stF[:, j, :])
                ins.then_inc(S["b_mv"], 1)

            def norm_ff(n):
                dve.wait_ge(S["b_mv"], n + 1)
                dve.wait_ge(S["b_rs"], n + 1)
                if n >= 2:
                    dve.wait_ge(S["b_xT"], n - 1)
                for j in range(4):
                    ins = V.tensor_scalar(xnB[:, n % 2, j, :], X[:, 4 * n + j, :], mvF[:, j, 0:1], rstdF[:, j:j + 1],
                                          ALU.subtract, ALU.mult)
                ins.then_inc(S["b_xn"], 1)

            def shift_ff(n):
                dve.wait_ge(S["b_xT"], n + 1)
                if n >= 2:
                    dve.wait_ge(S["b_f1"], FC0 * (n - 1))
                for j in range(4):
                    t = 4 * n + j
                    ins = V.tensor_scalar(hB[:, n % 2, 128 * j:128 * j + 128], PS[:, 6, 128 * j:128 * j + 128],
                                          adaT[:, 4, t:t + 1], adaT[:, 3, t:t + 1], ALU.mult, ALU.add)
                ins.then_inc(S["b_hT"], 1)

            def gate_ff(n):
                dve.wait_ge(S["b_f2"], FC0 * (n + 1))
                if n:
                    dve.wait_ge(S["b_fT"], n)
                for j in range(4):
                    t = 4 * n + j
                    ins = V.tensor_scalar(fB[:, 128 * j:128 * j + 128], PS[:, 0, 128 * j:128 * j + 128], p("b2"),
                                          adaT[:, 5, t:t + 1], ALU.add, ALU.mult)
                ins.then_inc(S["b_f"], 1)

            def add_ff(n):
                dve.wait_ge(S["b_fT"], n + 1)
                xs = X[:, 4 * n:4 * n + 4, :].rearrange("p b d -> p (b d)")
                V.tensor_tensor(xs, bank(1), xs, ALU.add).then_inc(S["b_x2"], 1)

            def stats1(m):
                xb = X[:, m, :]
                V.bn_stats(st[:, 0, :], xb).then_inc(S["c_st"], 1)
                dve.wait_ge(S["c_st"], m * 1 + 1)
                if later(m):
                    dve.wait_ge(S["c_ve"], m * 1)
                V.memset(tick[:, :], 0.0)
                V.bn_aggr(mv[:, 0, :], st[:, 0, :]).then_inc(S["c_mv"], 1)

            def norm1(m):
                xb = X[:, m, :]
                dve.wait_ge(S["c_rs"], m * 1 + 1)
                dve.wait_ge(S["c_mv"], m * 1 + 1)
                if later(m):
                    dve.wait_ge(S["c_xT"], m * 1)
                V.tensor_scalar(xn[:, :], xb, mv[:, 0, 0:1], rstd[:, 0:1], ALU.subtract, ALU.mult)\
                    .then_inc(S["c_xn"], 1)

            def hidden1(m):
                dve.wait_ge(S["c_xT"], m * 1 + 1)
                if later(m):
                    dve.wait_ge(S["c_qk"], m * 4)
                    dve.wait_ge(S["c_hv"], m * 1)
                V.tensor_scalar(h2[:, 0, :], PS[:, 3, 0:128], p("ln1_g"), shT[:, bass.ds(m, 1)],
                                ALU.mult, ALU.add).then_inc(S["c_hr"], 1)
                V.tensor_scalar(hT[:, :], PS[:, 3, 0:128], p("ln1_g"), shT[:, bass.ds(m, 1)],
                                ALU.mult, ALU.add).then_inc(S["c_hf"], 1)
                dve.wait_ge(S["c_hf"], m * 1 + 1)
                V.tensor_tensor(h2[:, 1, :], hT[:, :], h2[:, 0, :].bitcast(f32), ALU.subtract)\
                    .then_inc(S["c_hT"], 1)

            def reduce_sq(m, j):
                dve.wait_ge(S["c_sq"], m * 4 + j + 1)
                if later(m):
                    dve.wait_ge(S["c_sse"], m * 4 + j - 3)
                V.tensor_reduce(ss[:, j, :], sq[:, j % 2, :].rearrange("p (h d) -> p h d", d=HD1), AX.X, ALU.add)\
                    .then_inc(S["c_ss"], 1)

            def scale_qk(m, j):
                dve.wait_ge(S["c_rq"], m * 4 + j + 1)
                dve.wait_ge(S["c_qr"], m * 4 + j + 1)
                if later(m):
                    dve.wait_ge(S["c_T"], m * 4 + j - 3)
                V.tensor_tensor(qn[:, j, :].rearrange("p (h d) -> p h d", d=HD1),
                                qr[:, j, :].rearrange("p (h d) -> p h d", d=HD1),
                                rq[:, j, :].unsqueeze(2).to_broadcast([128, 8, HD1]), ALU.mult)\
                    .then_inc(S["c_qn"], 1)

            def maxima(n, g):
                dve.wait_ge(S["c_s"], n * NG + g + 1)
                if later(n):
                    dve.wait_ge(S["c_dg"], (n - 1) * NG + g + 1)
                V.tensor_reduce(mneg[:, GH * g:GH * g + GH],
                                bank(SB[g % 2]).rearrange("p (h k) -> p h k", h=GH), AX.X, ALU.max,
                                negate=True).then_inc(S["c_m"], 1)

            def keep_h(m):
                if later(m):
                    dve.wait_ge(S["c_vp"], m * 2)
                dve.wait_ge(S["c_hT"], m * 1 + 1)
                V.tensor_copy(hv[:, :, :], h2[:, :, :]).then_inc(S["c_hv"], 1)

            def lower_weights(i):
                w = slice(512 * PIECES[i], 512 * PIECES[i] + 512)
                dve.wait_ge(pre_wr, i + 1)
                V.tensor_tensor(WqkvL[:, w], Wqkv1[:, w], WqkvR[:, w].bitcast(f32), ALU.subtract).then_inc(pre_wl, 1)

            stats_ff(0)
            step0(B - 3, True, True, True, True)
            norm_ff(0)
            step0(B - 2, False, True, True, True)
            shift_ff(0)
            weight_sums(1)
            dve.wait_ge(pre_wc, 2)
            V.tensor_scalar_mul(wmean[:, :], wmean[:, :], 1.0 / HD1).then_inc(pre_wc, 1)
            stats_ff(1)
            step0(B - 1, False, False, True, True)
            norm_ff(1)
            stats_ff(2)
            step0(B, False, False, False, True)
            shift_ff(1)
            norm_ff(2)
            stats_ff(3)
            lower_weights(0)
            lower_weights(1)
            norm_ff(3)
            lower_weights(2)
            gate_ff(0)
            shift_ff(2)
            add_ff(0)
            dve.wait_ge(S["b_x2"], 1)
            stats1(0)
            norm1(0)
            lower_weights(3)
            lower_weights(4)
            lower_weights(5)
            gate_ff(1)
            shift_ff(3)
            hidden1(0)
            add_ff(1)
            stats1(1)
            norm1(1)
            reduce_sq(0, 0)
            reduce_sq(0, 1)
            gate_ff(2)
            reduce_sq(0, 2)
            reduce_sq(0, 3)
            add_ff(2)
            keep_h(0)
            hidden1(1)
            scale_qk(0, 0)
            scale_qk(0, 1)
            reduce_sq(1, 0)
            scale_qk(0, 2)
            reduce_sq(1, 1)
            scale_qk(0, 3)
            reduce_sq(1, 2)
            reduce_sq(1, 3)
            gate_ff(3)
            maxima(0, 0)
            maxima(0, 1)
            add_ff(3)
            maxima(0, 2)
            maxima(0, 3)

            def step1(b, front1, front2, attn, tail):
                m, n, t = b + 2, b + 1, b - 1

                def scale_o(g):
                    dve.wait_ge(S["c_pv"], b * NG + g + 1)
                    v = PS[:, 5 + g % 2, 0:GH * (HD1 + 1)].rearrange("p (h w) -> p h w", w=HD1 + 1)
                    V.reciprocal(rec1[:, GH * g:GH * g + GH], v[:, :, HD1]).then_inc(S["c_rec"], 1)
                    dve.wait_ge(S["c_rec"], b * NG + g + 1)
                    if later(b) and g == 0:
                        dve.wait_ge(S["c_oT"], b * 2)
                    heads = o1[:, 8 * (g // 2):8 * (g // 2) + 8, :].rearrange("p (i two) d -> p two i d", two=2)
                    V.tensor_tensor(heads[:, g % 2, :, :], v[:, :, 0:HD1],
                                    rec1[:, GH * g:GH * g + GH].unsqueeze(2).to_broadcast([128, GH, HD1]),
                                    ALU.mult).then_inc(S["c_o"], 1)

                if front2:
                    keep_h(n)
                if front1:
                    stats1(m)
                if front2:
                    scale_qk(n, 0)
                    scale_qk(n, 1)
                if front1:
                    norm1(m)
                if front2:
                    scale_qk(n, 2)
                if front1:
                    hidden1(m)
                if attn:
                    scale_o(0)
                if front2:
                    scale_qk(n, 3)
                if front1:
                    reduce_sq(m, 0)
                if tail:
                    dve.wait_ge(S["c_wo"], t * 1 + 1)
                    if later(t):
                        dve.wait_ge(S["c_x3T"], t * 1)
                        dve.wait_ge(S["c_xg"], t * 1)
                        dve.wait_ge(S["c_xs"], t * 1)
                    V.tensor_tensor(x3[:, :], PS[:, 7 if attn else 4, 0:128], X[:, t, :], ALU.add).then_inc(S["c_x3"], 1)
                if front1:
                    reduce_sq(m, 1)
                if attn:
                    scale_o(1)
                if tail:
                    dve.wait_ge(S["c_x3"], t * 1 + 1)
                    V.bn_stats(st3[:, :], x3[:, :]).then_inc(S["c_st3"], 1)
                    V.tensor_copy(X[:, t, :], x3[:, :]).then_inc(S["c_xs"], 1)
                    dve.wait_ge(S["c_st3"], t * 1 + 1)
                    if later(t):
                        dve.wait_ge(S["c_ve3"], t * 1)
                    V.memset(tick[:, :], 0.0)
                    V.bn_aggr(mv3[:, :], st3[:, :]).then_inc(S["c_mv3"], 1)
                if front1:
                    reduce_sq(m, 2)
                if attn:
                    scale_o(2)
                if front1:
                    reduce_sq(m, 3)
                if attn:
                    scale_o(3)
                if front2:
                    maxima(n, 0)
                    maxima(n, 1)
                if tail:
                    dve.wait_ge(S["c_g"], t * 1 + 1)
                    V.tensor_copy(G[:, t, :], PS[:, 7, 256:256 + E]).then_inc(S["c_gs"], 1)
                if front2:
                    maxima(n, 2)
                if tail:
                    dve.wait_ge(S["c_mv3"], t * 1 + 1)
                    dve.wait_ge(S["c_rs3"], t * 1 + 1)
                    V.tensor_scalar(R[:, t, 0:D], x3[:, :], mv3[:, 0:1], rs3[:, :], ALU.subtract, ALU.mult)\
                        .then_inc(S["c_xg"], 1)
                if front2:
                    maxima(n, 3)

            step1(0, True, True, True, False)
            step1(1, True, True, True, True)
            with dve.Fori(2, B - 2) as b:
                step1(b, True, True, True, True)
            step1(B - 2, False, True, True, True)
            step1(B - 1, False, False, True, True)
            step1(B, False, False, False, True)

            dve.wait_ge(S["c_gs"], B)
            V.tensor_reduce(gm[:, :], G[:, :, :], AX.X, ALU.max).then_inc(S["d_gm"], 1)
            dve.wait_ge(S["d_gm"], 1)
            V.tensor_tensor(G[:, :, :], G[:, :, :], gm[:, :].unsqueeze(2).to_broadcast([128, B, E]), ALU.subtract)\
                .then_inc(S["d_gsub"], 1)
            dve.wait_ge(S["d_ge"], 1)
            V.tensor_reduce(gs[:, :], GP[:, :, :], AX.X, ALU.add).then_inc(S["d_gs"], 1)
            dve.wait_ge(S["d_gs"], 1)
            V.reciprocal(gr[:, :], gs[:, :]).then_inc(S["d_gr"], 1)
            dve.wait_ge(S["d_gr"], 1)
            V.tensor_tensor(GP[:, :, :], GP[:, :, :], gr[:, :].unsqueeze(2).to_broadcast([128, B, E]), ALU.mult)\
                .then_inc(S["d_gp"], 1)
            dve.wait_ge(S["d_gp"], 1)
            dve.wait_ge(S["c_xg"], B)
            V.tensor_copy(R[:, :, D:ROW], GP[:, :, :]).then_inc(S["d_gpr"], 1)
            dve.wait_ge(S["d_T"], 1)
            V.tensor_copy(GT[:, :], PS[:, 0, 0:128]).then_inc(S["d_GT"], 1)
            dve.wait_ge(S["d_GT"], 1)
            V.tensor_copy(GTh[:, :], hi(GT[:, :])).then_inc(S["d_GT"], 1)

            V.tensor_copy(sameb[:, :], k("same")).then_inc(S["d_same"], 1)
            V.memset(found[:, :], 0).then_inc(S["d_found"], 1)
            V.tensor_copy(cand[:, :], BITS[:, 0:NCAND]).then_inc(S["d_cand"], 1)
            V.tensor_copy(base[:, :], BITS[:, NCAND:2 * NCAND]).then_inc(S["d_found"], 1)
            dve.wait_ge(S["d_GT"], 2)

            def count(gates):
                for j in range(NCAND):
                    ins = V.tensor_scalar(ge[:, j, :], gates[:, :], cand[:, j:j + 1].bitcast(f32), 0.0, ALU.is_ge,
                                          ALU.add, accum_out=cnt[:, j:j + 1])
                ins.then_inc(S["d_cnt"], 1)

            def next_digit(i):
                dve.wait_ge(S["d_sum"], i + 1)
                V.tensor_scalar(sat[:, :], PS[:, 1, 0:NCAND], float(CAP), 0.0, ALU.is_ge, ALU.add,
                                accum_out=nsat[:, :]).then_inc(S["d_nsat"], 1)
                dve.wait_ge(S["d_nsat"], i + 1)
                V.tensor_tensor(digit[:, :], nsat[:, :], k("unit")[:, i:i + 1], ALU.mult)\
                    .then_inc(S["d_digit"], 1)
                dve.wait_ge(S["d_digit"], i + 1)

            def add_digit():
                V.tensor_tensor(found[:, :], found[:, :], digit[:, :], ALU.bitwise_or).then_inc(S["d_found"], 1)

            def search_round(i, gates):
                next_digit(i - 1)
                dve.wait_ge(S["d_found"], i * 2)
                V.tensor_tensor(cand[:, :], base[:, :], digit[:, :].to_broadcast([128, NCAND]), ALU.bitwise_or)\
                    .then_inc(S["d_cand"], 1)
                dve.wait_ge(S["d_cand"], i + 1)
                count(gates)
                add_digit()
                dve.wait_ge(S["d_found"], i * 2 + 1)
                V.tensor_tensor(base[:, :], BITS[:, (i + 1) * NCAND:(i + 2) * NCAND],
                                found[:, :].to_broadcast([128, NCAND]), ALU.bitwise_or).then_inc(S["d_found"], 1)

            dve.wait_ge(S["d_cand"], 1)
            count(GTh)
            for i in range(1, ROUNDS):
                search_round(i, GTh if i < UPPER_ROUNDS else GT)
            next_digit(ROUNDS - 1)
            dve.wait_ge(S["d_found"], 2 * ROUNDS)
            add_digit()
            dve.wait_ge(S["d_found"], 2 * ROUNDS + 1)
            thr = found[:, :].bitcast(f32)
            V.tensor_scalar(gtm[:, :], GT[:, :], thr, 0.0, ALU.is_gt, ALU.add, accum_out=ngt[:, :])\
                .then_inc(S["d_masks"], 1)
            V.tensor_scalar(eqm[:, :], GT[:, :], thr, 0.0, ALU.is_equal, ALU.add, accum_out=neq[:, :])\
                .then_inc(S["d_masks"], 1)
            dve.wait_ge(S["d_masks"], 2)
            V.tensor_tensor_scan(eqs[:, :], eqm[:, :], zero[:, :], 0.0, ALU.add, ALU.add).then_inc(S["d_scan"], 1)
            dve.wait_ge(S["d_sums"], 1)
            V.tensor_scalar(lim[:, 0:1], PS[:, 0, 0:1], -1.0, float(CAP), ALU.mult, ALU.add)\
                .then_inc(S["d_lim"], 1)
            dve.wait_ge(S["d_lim"], 1)
            V.tensor_tensor(lim[:, 1:2], lim[:, 0:1], PS[:, 0, 1:2], ALU.subtract).then_inc(S["d_lim"], 1)
            dve.wait_ge(S["d_lim"], 2)
            dve.wait_ge(S["d_scan"], 1)
            V.scalar_tensor_tensor(eqt[:, :], eqs[:, :], lim[:, 1:2], eqm[:, :], ALU.is_le, ALU.mult)\
                .then_inc(S["d_eqt"], 1)
            dve.wait_ge(S["d_eqt"], 1)
            V.tensor_tensor_scan(CC[:, 0:128], eqt[:, :], gtm[:, :], 0.0, ALU.add, ALU.add).then_inc(S["d_C"], 1)
            V.tensor_copy(CC[:, 129:130], k("base"))
            dve.wait_ge(S["d_C"], 1)

            def by_expert(a, z):
                return V.tensor_tensor(CE[:, :, a:z], CC[:, a:z].unsqueeze(1).to_broadcast([128, E, z - a]),
                                       k("emask").unsqueeze(2).to_broadcast([128, E, z - a]), ALU.mult)

            by_expert(0, 128)
            dve.wait_ge(S["d_off"], 1)
            V.tensor_copy(CC[:, 128:129], PS[:, 2, 0:1]).then_inc(S["d_offs"], 1)
            dve.wait_ge(S["d_offs"], 1)
            V.tensor_tensor(hiS[:, :], CC[:, 128:129], CC[:, 127:128], ALU.add).then_inc(S["d_hi"], 1)
            by_expert(128, 130).then_inc(S["d_CE"], 1)
            dve.wait_ge(S["d_hi"], 1)
            V.tensor_scalar(inA[:, :], k("slots"), hiS[:, :], None, ALU.is_lt).then_inc(S["d_inA"], 1)
            dve.wait_ge(S["d_inA"], 1)
            V.scalar_tensor_tensor(inC[:, :], k("slots"), CC[:, 128:129], inA[:, :], ALU.is_ge, ALU.mult)\
                .then_inc(S["d_inC"], 1)
            def row(j, h):
                a, z = PARTS[j]
                return PS[:, 2 + 3 * h + j, 0:130 * (z - a)].rearrange("p (e w) -> p e w", w=130)

            for j, (a, z) in enumerate(PARTS):
                w = z - a
                for h in range(HALVES):
                    dve.wait_ge(S["d_row"], HALVES * j + h + 1)
                    V.tensor_scalar(rr[:, h, a:z], row(j, h)[:, :, 128], -1.0, k("slotid")[:, h:h + 1], ALU.mult,
                                    ALU.add).then_inc(S["d_rr"], 1)
                    dve.wait_ge(S["d_rr"], HALVES * j + h + 1)
                    V.tensor_tensor(le[:, 3 * h:3 * h + w, :], row(j, h)[:, :, 0:128],
                                    rr[:, h, a:z].unsqueeze(2).to_broadcast([128, w, 128]), ALU.is_le)\
                        .then_inc(S["d_scan"], 1)
                dve.wait_ge(S["d_scan"], 1 + HALVES * (j + 1))
                V.tensor_reduce(nle[:, :, a:z],
                                le[:, 0:3 * HALVES, :].rearrange("p (h e) k -> p h e k", h=HALVES)[:, :, 0:w, :],
                                AX.X, ALU.add).then_inc(S["d_nle"], 1)
                dve.wait_ge(S["d_nle"], j + 1)
                for h in range(HALVES):
                    ins = V.tensor_tensor(idx[:, h, a:z], row(j, h)[:, :, 129], nle[:, h, a:z], ALU.add)
                ins.then_inc(S["d_le"], 1)

            def gained(e):
                dve.wait_ge(S["e_T"], e + 1)
                if e >= 2:
                    dve.wait_ge(S["e_f1"], DC // 2 * (e - 1))
                V.tensor_scalar(gT[:, e % 2, :], PS[:, 0, 0:CAP], p("mlp_g"), p("mlp_b"), ALU.mult, ALU.add)\
                    .then_inc(S["e_gT"], 1)

            def weigh(e):
                dve.wait_ge(S["e_f2"], e + 1)
                V.tensor_tensor(Y[:, e, :, :], PS[:, 5 + e % 2, 0:CAP].rearrange("p (h d) -> p h d", h=HALVES),
                                B2S[:, D * e:D * e + D].unsqueeze(1).to_broadcast([128, HALVES, D]), ALU.add)\
                    .then_inc(S["e_yb"], 1)
                dve.wait_ge(S["e_yb"], e + 1)
                for h in range(HALVES):
                    V.tensor_scalar_mul(Y[:, e, h, :], Y[:, e, h, :], GX[:, e, h, D + e:D + e + 1])\
                        .then_inc(S["e_y"], 1)

            gained(0)
            for e in range(E):
                if e + 1 < E:
                    gained(e + 1)
                if e:
                    weigh(e - 1)
            weigh(E - 1)

        @block.gpsimd
        def _(pool):
            Q = nc.gpsimd

            def rsqrt(o, ve, src, w, s_in, s_add, s_out, at, used=None):
                pool.wait_ge(s_in, at + 1)
                Q.tensor_tensor(ve, src, epsT[:, 0:w], ALU.add).then_inc(s_add, 1)
                pool.wait_ge(s_add, at + 1)
                if used is not None:
                    pool.wait_ge(*used)
                Q.tensor_tensor(o, ve, mhalf[:, 0:w], ALU.pow).then_inc(s_out, 1)

            pool.wait_ge(pre_const, 2)

            def step0(b, ln, front, attn, tail):
                m, n = b + 2, b + 1

                def mask(g):
                    if g == 0:
                        pool.wait_ge(S["a_qT"], n * 1 + 1)
                    if later(n):
                        pool.wait_ge(S["a_sT"], b * NG + g + 1)
                    Q.tensor_tensor(Qm[:, GH * g:GH * g + GH, :], qT[:, :].unsqueeze(1).to_broadcast([128, GH, 128]),
                                    k("headmask")[:, GH * g:GH * g + GH].unsqueeze(2).to_broadcast([128, GH, 128]),
                                    ALU.mult).then_inc(S["a_qm"], 1)

                def norm_x0():
                    rsqrt(rstd[:, 0:1], veps[:, 0:1], mv[:, 0, 1:2], 1, S["a_mv"], S["a_ve"], S["a_rs"], m * 1,
                          used=(S["a_xn"], m * 1) if later(m) else None)

                if front:
                    mask(0)
                    mask(1)
                    mask(2)
                    mask(3)
                if ln:
                    norm_x0()

            step0(-2, True, False, False, False)
            pool.wait_ge(ld_c, 80)
            step0(-1, True, True, False, False)
            step0(0, True, True, True, False)
            step0(1, True, True, True, True)
            with pool.Fori(2, B - 3) as b:
                step0(b, True, True, True, True)

            def rsqrt_ff(n):
                rsqrt(rstdF[:, :], vepsF[:, :], mvF[:, :, 1], 4, S["b_mv"], S["b_ve"], S["b_rs"], n,
                      used=(S["b_xn"], n) if n else None)

            rsqrt_ff(0)
            step0(B - 3, True, True, True, True)
            step0(B - 2, False, True, True, True)

            rsqrt_ff(1)
            pool.wait_ge(pre_wc, 3)
            for j in range(4):
                heads = Wqkv1[:, 512 * j:512 * j + 512].rearrange("p (h d) -> p h d", d=HD1)
                Q.tensor_tensor(heads, heads, wmean[:, 8 * j:8 * j + 8].unsqueeze(2).to_broadcast([128, 8, HD1]),
                                ALU.subtract).then_inc(pre_wcs, 1)
            rsqrt_ff(2)
            rsqrt_ff(3)

            def norm_x1(m):
                rsqrt(rstd[:, 0:1], veps[:, 0:1], mv[:, 0, 1:2], 1, S["c_mv"], S["c_ve"], S["c_rs"], m * 1,
                      used=(S["c_xn"], m * 1) if later(m) else (S["a_xn"], B))

            def norms(m, j):
                rsqrt(rq[:, j, :], sse[:, j, :], ss[:, j, :], 8, S["c_ss"], S["c_sse"], S["c_rq"],
                      m * 4 + j, used=(S["c_qn"], m * 4 + j - 3) if later(m) else None)

            def spread_max(n, g):
                pool.wait_ge(S["c_m"], n * NG + g + 1)
                if later(n):
                    pool.wait_ge(S["c_sT"], (n - 1) * NG + g + 1)
                Q.tensor_tensor(diag[:, GH * g:GH * g + GH, :], identb[:, :].unsqueeze(1).to_broadcast([128, GH, 128]),
                                mneg[:, GH * g:GH * g + GH].unsqueeze(2).to_broadcast([128, GH, 128]), ALU.mult)\
                    .then_inc(S["c_dg"], 1)

            def step1(b, front1, front2, attn, tail):
                m, n, t = b + 2, b + 1, b - 1
                if front1:
                    norm_x1(m)
                if attn:
                    spread_max(b, 2)
                    spread_max(b, 3)
                if front1:
                    norms(m, 0)
                    norms(m, 1)
                    norms(m, 2)
                if tail:
                    rsqrt(rs3[:, :], ve3[:, :], mv3[:, 1:2], 1, S["c_mv3"], S["c_ve3"], S["c_rs3"], t * 1,
                          used=(S["c_xg"], t * 1) if later(t) else None)
                if front1:
                    norms(m, 3)
                if front2:
                    spread_max(n, 0)
                    spread_max(n, 1)

            norm_x1(0)
            norm_x1(1)
            for m in range(2):
                for j in range(4):
                    norms(m, j)
            pool.wait_ge(S["a_sT"], B * NG)
            spread_max(0, 0)
            spread_max(0, 1)
            step1(0, True, True, True, False)
            step1(1, True, True, True, True)
            with pool.Fori(2, B - 2) as b:
                step1(b, True, True, True, True)
            step1(B - 2, False, True, True, True)
            step1(B - 1, False, False, True, True)
            step1(B, False, False, False, True)

            pool.wait_ge(S["d_rows"], 16)
            flat = out.rearrange("b p d -> (b p) d")
            ahead = 5

            def gather(e):
                pool.wait_ge(S["d_le"], 1 + sum(e >= z for a, z in PARTS))
                for h in range(HALVES):
                    Q.indirect_dma_start(out=GX[:, e, h, :], out_offset=None, in_=rows,
                                         in_offset=bass.IndirectOffsetOnAxis(ap=idx[:, h, e:e + 1], axis=0))\
                        .then_inc(S["e_gx"][e], 16)

            for e in range(ahead):
                gather(e)
            pool.wait_ge(S["d_xout"], 16)
            for e in range(E):
                if e + ahead < E:
                    gather(e + ahead)
                pool.wait_ge(S["e_y"], HALVES * (e + 1))
                if e:
                    pool.wait_ge(S["e_out"], 16 * HALVES * e)
                for h in range(HALVES):
                    Q.indirect_dma_start(out=flat,
                                         out_offset=bass.IndirectOffsetOnAxis(ap=idx[:, h, e:e + 1], axis=0),
                                         in_=Y[:, e, h, :], in_offset=None, compute_op=ALU.add)\
                        .then_inc(S["e_out"], 16)
            pool.wait_ge(S["e_out"], 16 * HALVES * E)


def kernel(**inputs):
    import concourse.bacc as bacc
    from concourse.bass_utils import run_bass_kernel_spmd

    def a(name):
        return np.ascontiguousarray(np.asarray(inputs[name]))

    def col(v):
        return v.reshape(-1, 128).T

    rows128 = np.arange(128)
    const = np.zeros((128, CONST_W), np.float32)
    def put(name, v):
        const[:, COLS[name][0]:COLS[name][1]] = v
    put("ident", np.eye(128))
    put("headmask", rows128[:, None] // HD0 == np.arange(H0)[None, :])
    same = (rows128[:, None] % E) == (rows128[None, :] % E)
    put("same", same)
    put("before", same & (rows128[:, None] // E < rows128[None, :] // E))
    put("emask", rows128[:, None] % E == np.arange(E)[None, :])
    put("slots", np.arange(CAP)[None, :])
    put("base", (rows128[:, None] // E) * 128)
    put("slotid", rows128[:, None] + 128 * np.arange(HALVES)[None, :])
    unit = 2 ** (GATE_BITS - DIGIT * (1 + np.arange(ROUNDS)))
    put("unit", unit[None, :])
    digits = np.append(unit, 0)[:, None] * (1 + np.arange(NCAND))[None, :]
    bits = np.tile(digits.reshape(1, -1).astype(np.int32), (128, 1))

    param = np.zeros((128, PARAM_W), np.float32)
    vectors = {
        "b_ada": col(a("L0_cond_b_ada")), "bq": col(a("L0_cond_bq")), "bk": col(a("L0_cond_bk")),
        "bv": col(a("L0_cond_bv")), "bo": col(a("L0_cond_bo")), "b1": col(a("L0_cond_b1")),
        "b2": col(a("L0_cond_b2")), "b_ada1": col(a("L1_cond_b_ada")), "ln1_g": col(a("L1_cond_ln1_g")),
        "ln1_b": col(a("L1_cond_ln1_b")), "mlp_g": col(a("L1_cond_mlp_g")), "mlp_b": col(a("L1_cond_mlp_b")),
        "b1s": col(a("L1_cond_b1s").reshape(-1)), "cT": a("cond_1024").T, "wgate": a("L1_cond_Wgate").T,
    }
    for n in ("qn_g", "qn_b", "kn_g", "kn_b"):
        vectors[n] = np.concatenate([a("L1_cond_" + n)] * 2)[:, None]
    for n, v in vectors.items():
        param[:, PCOLS[n][0]:PCOLS[n][1]] = v

    arrays = {
        "x": a("x"), "const": const, "bits": bits, "param": param,
        "w_ada": a("L0_cond_W_ada"),
        "wqkv0": np.concatenate([a("L0_cond_Wq"), a("L0_cond_Wk"), a("L0_cond_Wv")], axis=1),
        "wo": a("L0_cond_Wo"), "w1": a("L0_cond_W1"),
        "w2": a("L0_cond_W2").reshape(FC0, 128, D).transpose(1, 0, 2),
        "w_ada1": a("L1_cond_W_ada").T, "wqkv1": a("L1_cond_Wqkv").T,
        "wout": a("L1_cond_Wout").T.reshape(HP, 128, D).transpose(1, 0, 2),
        "fc1": a("L1_cond_fc1s").transpose(2, 0, 1),
        "fc2": a("L1_cond_fc2s").reshape(E, D, DC, 128).transpose(3, 0, 2, 1),
        "b2s": np.broadcast_to(a("L1_cond_b2s").reshape(1, E * D), (128, E * D)),
    }
    arrays = {n: np.ascontiguousarray(v) for n, v in arrays.items()}

    nc = bacc.Bacc("TRN2", target_bir_lowering=False, num_devices=1)
    args = [nc.dram_tensor("in_" + n, v.shape, mybir.dt.from_np(v.dtype), kind="ExternalInput").ap()
            for n, v in arrays.items()]
    out = nc.dram_tensor("out", (B, N, D), mybir.dt.float32, kind="ExternalOutput").ap()
    rows = nc.dram_tensor("rows", (B * N, ROW), mybir.dt.float32).ap()
    cond_seq_kernel(nc, *args, out, rows)
    r = run_bass_kernel_spmd(nc, [{"in_" + n: v for n, v in arrays.items()}], core_ids=[0])
    return r.results[0]["out"]
```
